# Optimizing a Trainium2 kernel written in Bass

```python
import numpy as np
import jax
import jax.numpy as jnp

def _softmax(x, axis=-1):
    return jax.nn.softmax(x, axis=axis)

def _gelu(x):
    return jax.nn.gelu(x, approximate=True)

def _silu(x):
    return jax.nn.silu(x)

def _sigmoid(x):
    return jax.nn.sigmoid(x)

def _layernorm(x, axis=-1, eps=1e-05):
    m = jnp.mean(x, axis=axis, keepdims=True)
    v = jnp.var(x, axis=axis, keepdims=True)
    return (x - m) / jnp.sqrt(v + eps)

def _scatter_add(tgt, idx, src, axis=0):
    return tgt.at[idx].add(src)

def _segment_sum(src, seg, n):
    return jax.ops.segment_sum(src, seg, n)
kernel_name = 'mk_adaln_ffn_d2_seqx_r4_7b3b1c'

def setup_inputs(seed: int=0):
    np.random.seed(seed)
    _w = jnp.asarray

    def _rec_inputs():
        import jax
        import jax.numpy as jnp
        _rk = jax.random.key(seed)
        x = 7.22e-05 + 1 * jax.random.normal(jax.random.fold_in(_rk, 1), (2, 1024, 256), jnp.float32)
        _lenS = 1024 - jax.random.randint(jax.random.fold_in(_rk, 7), (2,), 0, max(1, 1024 // 4) + 1, jnp.int32)
        _lenS2 = 1024 - jax.random.randint(jax.random.fold_in(_rk, 8), (2,), 0, max(1, 1024 // 4) + 1, jnp.int32)
        cond_64 = -0.104238 + 1.01173 * jax.random.normal(jax.random.fold_in(_rk, 11), (2, 64), jnp.float32)
        _validS = jnp.arange(1024)[None, :] < _lenS[:, None]
        _validS2 = jnp.arange(1024)[None, :] < _lenS2[:, None]
        _causal = jnp.tril(jnp.ones((1024, 1024), dtype=bool))
        mask_BxS_bf1 = jnp.ones((2, 1024), dtype=bool)
        return (x, cond_64, mask_BxS_bf1)
    x, cond_64, mask_BxS_bf1 = _rec_inputs()

    def _L0_cond_setup():
        import jax, jax.numpy as jnp
        import numpy as np
        B, S, H = (4, 512, 256)
        E = 8
        M = 128
        K = 2
        N_SHARED = 2
        SM = M * N_SHARED
        G = 64
        GE_TEMP = 1.0
        ALPHA = 0.001
        SEQ_AUX = True
        NORM_TOPK = True
        COS_TEMP = 0.78
        CONS_ALPHA = 0.01
        LEAKY_SLOPE = 0.01
        EPS_COS = 1e-08

        def _leaky(x):
            return jnp.where(x >= 0, x, LEAKY_SLOPE * x)

        def _moe_forward(hidden_states, g, wt, wg, w_gate, w_up, w_down, sw_gate, sw_up, sw_down):
            b, s, h = hidden_states.shape
            x = hidden_states.reshape(-1, h)
            T = x.shape[0]
            logits_h = x @ wt.T
            logits_g = g @ wg.T
            logits_g = jnp.repeat(logits_g, s, axis=0)
            logits = (logits_h + logits_g / GE_TEMP) / (1.0 + 1.0 / GE_TEMP)
            scores = jax.nn.softmax(logits, axis=-1)
            topk_w, topk_idx = jax.lax.top_k(scores, K)
            if K > 1 and NORM_TOPK:
                topk_w = topk_w / (topk_w.sum(-1, keepdims=True) + 1e-20)
            onehot = jax.nn.one_hot(topk_idx.reshape(b, s * K), E, dtype=jnp.float32)
            ce = onehot.sum(1) / (s * K / E)
            aux_loss = (ce * scores.reshape(b, s, E).mean(1)).sum(1).mean() * ALPHA
            gp = _leaky(jnp.einsum('th,ehm->etm', x, w_gate))
            up = jnp.einsum('th,ehm->etm', x, w_up)
            y_all = jnp.einsum('etm,emh->eth', gp * up, w_down)
            y_sel = y_all[topk_idx, jnp.arange(T)[:, None], :]
            y = (y_sel * topk_w[..., None]).sum(1).reshape(b, s, h)
            p = _leaky(hidden_states @ sw_gate) * (hidden_states @ sw_up) @ sw_down
            y = y + p
            num = jnp.sum(y * p, -1)
            den = jnp.maximum(jnp.linalg.norm(y, axis=-1), EPS_COS) * jnp.maximum(jnp.linalg.norm(p, axis=-1), EPS_COS)
            closs = CONS_ALPHA * jnp.mean(num / den / (1.0 + COS_TEMP))
            return (y, aux_loss + closs)
        key = jax.random.key(seed)
        ks = jax.random.split(key, 12)
        sh = 1.0 / np.sqrt(H)
        sm = 1.0 / np.sqrt(M)
        ssm = 1.0 / np.sqrt(SM)
        sg = 1.0 / np.sqrt(G)
        return {'hidden_states': jax.random.normal(ks[0], (B, S, H), jnp.float32), 'g': jax.random.normal(ks[1], (B, G), jnp.float32), 'wt': jax.random.uniform(ks[2], (E, H), jnp.float32, -sh, sh), 'wg': jax.random.uniform(ks[3], (E, G), jnp.float32, -sg, sg), 'w_gate': jax.random.uniform(ks[4], (E, H, M), jnp.float32, -sh, sh), 'w_up': jax.random.uniform(ks[5], (E, H, M), jnp.float32, -sh, sh), 'w_down': jax.random.uniform(ks[6], (E, M, H), jnp.float32, -sm, sm), 'sw_gate': jax.random.uniform(ks[7], (H, SM), jnp.float32, -sh, sh), 'sw_up': jax.random.uniform(ks[8], (H, SM), jnp.float32, -sh, sh), 'sw_down': jax.random.uniform(ks[9], (SM, H), jnp.float32, -ssm, ssm)}
    _L0_cond_all = _L0_cond_setup()
    _L0_cond_in = {k: v for k, v in _L0_cond_all.items() if k in ('wt', 'wg', 'w_gate', 'w_up', 'w_down', 'sw_gate', 'sw_up', 'sw_down')}
    del _L0_cond_all

    def _L0_ffn_setup():
        import jax, jax.numpy as jnp
        import numpy as np
        S, B, D, FF, E = (256, 2, 256, 512, 8)
        key = jax.random.key(seed)
        ks = jax.random.split(key, 8)
        s = 0.02
        return {'hidden_states': jax.random.normal(ks[0], (S, B, D), dtype=jnp.float32), 'router_w': jax.random.normal(ks[1], (E, D), dtype=jnp.float32) * s, 'expert_gate': jax.random.normal(ks[2], (E, D, FF), dtype=jnp.float32) * s, 'expert_up': jax.random.normal(ks[3], (E, D, FF), dtype=jnp.float32) * s, 'expert_down': jax.random.normal(ks[4], (E, FF, D), dtype=jnp.float32) * s, 'shared_gate': jax.random.normal(ks[5], (D, FF), dtype=jnp.float32) * s, 'shared_up': jax.random.normal(ks[6], (D, FF), dtype=jnp.float32) * s, 'shared_down': jax.random.normal(ks[7], (FF, D), dtype=jnp.float32) * s}
    _L0_ffn_all = _L0_ffn_setup()
    _L0_ffn_in = {k: v for k, v in _L0_ffn_all.items() if k in ('router_w', 'expert_gate', 'expert_up', 'expert_down', 'shared_gate', 'shared_up', 'shared_down')}
    del _L0_ffn_all

    def _L1_cond_setup():
        import jax, jax.numpy as jnp
        import numpy as np
        DIM = 256
        HEADS = 16
        DIM_HEAD = 64
        SCALE = 8.0

        def ln(x, g, eps=1e-05):
            mean = x.mean(axis=-1, keepdims=True)
            var = ((x - mean) ** 2).mean(axis=-1, keepdims=True)
            return (x - mean) * jax.lax.rsqrt(var + eps) * g

        def l2norm(t):
            n = jnp.maximum(jnp.linalg.norm(t, axis=-1, keepdims=True), 1e-12)
            return t / n

        def rel_pos_bias(n, w0, b0, g0, w1, b1, g1, w2, b2, dtype):
            pos = jnp.arange(-n + 1, n, dtype=dtype)[:, None]
            h = jax.nn.silu(ln(pos @ w0 + b0, g0))
            h = jax.nn.silu(ln(h @ w1 + b1, g1))
            h = h @ w2 + b2
            i = jnp.arange(n)
            idx = i[:, None] - i[None, :] + n - 1
            bias = h[idx]
            return jnp.transpose(bias, (2, 0, 1))
        key = jax.random.key(seed)
        ks = jax.random.split(key, 16)
        b, n = (2, 512)
        inner = HEADS * DIM_HEAD
        s = 0.02
        return {'x': jax.random.normal(ks[0], (b, n, DIM), jnp.float32), 'mask': jnp.ones((b, n), dtype=bool), 'g_norm': jnp.ones((DIM,), jnp.float32), 'Wq': jax.random.normal(ks[1], (DIM, inner), jnp.float32) * s, 'Wkv': jax.random.normal(ks[2], (DIM, 2 * DIM_HEAD), jnp.float32) * s, 'q_scale': jnp.ones((DIM_HEAD,), jnp.float32), 'k_scale': jnp.ones((DIM_HEAD,), jnp.float32), 'null_kv': jax.random.normal(ks[3], (2, DIM_HEAD), jnp.float32), 'null_attn_bias': jax.random.normal(ks[4], (HEADS,), jnp.float32), 'w0': jax.random.normal(ks[5], (1, DIM), jnp.float32) * s, 'b0': jnp.zeros((DIM,), jnp.float32), 'g0': jnp.ones((DIM,), jnp.float32), 'w1': jax.random.normal(ks[6], (DIM, DIM), jnp.float32) * s, 'b1': jnp.zeros((DIM,), jnp.float32), 'g1': jnp.ones((DIM,), jnp.float32), 'w2': jax.random.normal(ks[7], (DIM, HEADS), jnp.float32) * s, 'b2': jnp.zeros((HEADS,), jnp.float32), 'Wout': jax.random.normal(ks[8], (inner, DIM), jnp.float32) * s, 'g_out': jnp.ones((DIM,), jnp.float32)}
    _L1_cond_all = _L1_cond_setup()
    _L1_cond_in = {k: v for k, v in _L1_cond_all.items() if k in ('g_norm', 'Wq', 'Wkv', 'q_scale', 'k_scale', 'null_attn_bias', 'w0', 'b0', 'g0', 'w1', 'b1', 'g1', 'w2', 'b2', 'Wout', 'g_out')}
    del _L1_cond_all

    def _L1_ffn_setup():
        import jax, jax.numpy as jnp
        import numpy as np
        import math
        EMBED_DIM = 256
        FFN_DIM = 1024
        N_EXPERTS = 8
        TOP_K = 2
        CAP_FACTOR = 1.25
        key = jax.random.key(seed)
        k0, k1, k2, k3 = jax.random.split(key, 4)
        B, S = (4, 512)
        x = jax.random.normal(k0, (B, S, EMBED_DIM), dtype=jnp.float32)
        Wr = jax.random.normal(k1, (EMBED_DIM, N_EXPERTS), dtype=jnp.float32) * 0.02
        W1 = jax.random.normal(k2, (N_EXPERTS, EMBED_DIM, FFN_DIM), dtype=jnp.float32) * 0.02
        W2 = jax.random.normal(k3, (N_EXPERTS, FFN_DIM, EMBED_DIM), dtype=jnp.float32) * 0.02
        return {'x': x, 'Wr': Wr, 'W1': W1, 'W2': W2}
    _L1_ffn_all = _L1_ffn_setup()
    _L1_ffn_in = {k: v for k, v in _L1_ffn_all.items() if k in ('Wr', 'W1', 'W2')}
    del _L1_ffn_all
    return {'x': x, 'cond_64': cond_64, 'mask_BxS_bf1': mask_BxS_bf1, 'L0_cond_wt': _L0_cond_in['wt'], 'L0_cond_wg': _L0_cond_in['wg'], 'L0_cond_w_gate': _L0_cond_in['w_gate'], 'L0_cond_w_up': _L0_cond_in['w_up'], 'L0_cond_w_down': _L0_cond_in['w_down'], 'L0_cond_sw_gate': _L0_cond_in['sw_gate'], 'L0_cond_sw_up': _L0_cond_in['sw_up'], 'L0_cond_sw_down': _L0_cond_in['sw_down'], 'L0_ffn_router_w': _L0_ffn_in['router_w'], 'L0_ffn_expert_gate': _L0_ffn_in['expert_gate'], 'L0_ffn_expert_up': _L0_ffn_in['expert_up'], 'L0_ffn_expert_down': _L0_ffn_in['expert_down'], 'L0_ffn_shared_gate': _L0_ffn_in['shared_gate'], 'L0_ffn_shared_up': _L0_ffn_in['shared_up'], 'L0_ffn_shared_down': _L0_ffn_in['shared_down'], 'L1_cond_g_norm': _L1_cond_in['g_norm'], 'L1_cond_Wq': _L1_cond_in['Wq'], 'L1_cond_Wkv': _L1_cond_in['Wkv'], 'L1_cond_q_scale': _L1_cond_in['q_scale'], 'L1_cond_k_scale': _L1_cond_in['k_scale'], 'L1_cond_null_attn_bias': _L1_cond_in['null_attn_bias'], 'L1_cond_w0': _L1_cond_in['w0'], 'L1_cond_b0': _L1_cond_in['b0'], 'L1_cond_g0': _L1_cond_in['g0'], 'L1_cond_w1': _L1_cond_in['w1'], 'L1_cond_b1': _L1_cond_in['b1'], 'L1_cond_g1': _L1_cond_in['g1'], 'L1_cond_w2': _L1_cond_in['w2'], 'L1_cond_b2': _L1_cond_in['b2'], 'L1_cond_Wout': _L1_cond_in['Wout'], 'L1_cond_g_out': _L1_cond_in['g_out'], 'L1_ffn_Wr': _L1_ffn_in['Wr'], 'L1_ffn_W1': _L1_ffn_in['W1'], 'L1_ffn_W2': _L1_ffn_in['W2']}

def reference(x, cond_64, mask_BxS_bf1, L0_cond_wt, L0_cond_wg, L0_cond_w_gate, L0_cond_w_up, L0_cond_w_down, L0_cond_sw_gate, L0_cond_sw_up, L0_cond_sw_down, L0_ffn_router_w, L0_ffn_expert_gate, L0_ffn_expert_up, L0_ffn_expert_down, L0_ffn_shared_gate, L0_ffn_shared_up, L0_ffn_shared_down, L1_cond_g_norm, L1_cond_Wq, L1_cond_Wkv, L1_cond_q_scale, L1_cond_k_scale, L1_cond_null_attn_bias, L1_cond_w0, L1_cond_b0, L1_cond_g0, L1_cond_w1, L1_cond_b1, L1_cond_g1, L1_cond_w2, L1_cond_b2, L1_cond_Wout, L1_cond_g_out, L1_ffn_Wr, L1_ffn_W1, L1_ffn_W2):
    import jax
    import jax.numpy as jnp

    def _L0_cond_ref(hidden_states, g, wt, wg, w_gate, w_up, w_down, sw_gate, sw_up, sw_down):
        import jax, jax.numpy as jnp
        import numpy as np
        B, S, H = (4, 512, 256)
        E = 8
        M = 128
        K = 2
        N_SHARED = 2
        SM = M * N_SHARED
        G = 64
        GE_TEMP = 1.0
        ALPHA = 0.001
        SEQ_AUX = True
        NORM_TOPK = True
        COS_TEMP = 0.78
        CONS_ALPHA = 0.01
        LEAKY_SLOPE = 0.01
        EPS_COS = 1e-08

        def _leaky(x):
            return jnp.where(x >= 0, x, LEAKY_SLOPE * x)

        def _moe_forward(hidden_states, g, wt, wg, w_gate, w_up, w_down, sw_gate, sw_up, sw_down):
            b, s, h = hidden_states.shape
            x = hidden_states.reshape(-1, h)
            T = x.shape[0]
            logits_h = x @ wt.T
            logits_g = g @ wg.T
            logits_g = jnp.repeat(logits_g, s, axis=0)
            logits = (logits_h + logits_g / GE_TEMP) / (1.0 + 1.0 / GE_TEMP)
            scores = jax.nn.softmax(logits, axis=-1)
            topk_w, topk_idx = jax.lax.top_k(scores, K)
            if K > 1 and NORM_TOPK:
                topk_w = topk_w / (topk_w.sum(-1, keepdims=True) + 1e-20)
            onehot = jax.nn.one_hot(topk_idx.reshape(b, s * K), E, dtype=jnp.float32)
            ce = onehot.sum(1) / (s * K / E)
            aux_loss = (ce * scores.reshape(b, s, E).mean(1)).sum(1).mean() * ALPHA
            gp = _leaky(jnp.einsum('th,ehm->etm', x, w_gate))
            up = jnp.einsum('th,ehm->etm', x, w_up)
            y_all = jnp.einsum('etm,emh->eth', gp * up, w_down)
            y_sel = y_all[topk_idx, jnp.arange(T)[:, None], :]
            y = (y_sel * topk_w[..., None]).sum(1).reshape(b, s, h)
            p = _leaky(hidden_states @ sw_gate) * (hidden_states @ sw_up) @ sw_down
            y = y + p
            num = jnp.sum(y * p, -1)
            den = jnp.maximum(jnp.linalg.norm(y, axis=-1), EPS_COS) * jnp.maximum(jnp.linalg.norm(p, axis=-1), EPS_COS)
            closs = CONS_ALPHA * jnp.mean(num / den / (1.0 + COS_TEMP))
            return (y, aux_loss + closs)
        y, _ = _moe_forward(hidden_states, g, wt, wg, w_gate, w_up, w_down, sw_gate, sw_up, sw_down)
        return y

    def _L0_ffn_ref(hidden_states, router_w, expert_gate, expert_up, expert_down, shared_gate, shared_up, shared_down):
        import jax, jax.numpy as jnp
        import numpy as np
        S, B, D, FF, E = (256, 2, 256, 512, 8)
        seq, bs, d = hidden_states.shape
        n_experts = expert_gate.shape[0]
        x = hidden_states.reshape(-1, d)
        logits = jnp.einsum('td,ed->te', x, router_w)
        top_logit = jnp.max(logits, axis=-1)
        top_idx = jnp.argmax(logits, axis=-1)
        score = jax.nn.sigmoid(top_logit)
        onehot = jax.nn.one_hot(top_idx, n_experts, dtype=x.dtype)
        xs = x * score[:, None]
        g = jnp.einsum('td,edf->etf', xs, expert_gate)
        u = jnp.einsum('td,edf->etf', xs, expert_up)
        h = jax.nn.silu(g) * u
        eo = jnp.einsum('etf,efd->etd', h, expert_down)
        moe_out = jnp.einsum('te,etd->td', onehot, eo)
        sh = jax.nn.silu(x @ shared_gate) * (x @ shared_up) @ shared_down
        return (moe_out + sh).reshape(seq, bs, d)

    def _L1_cond_ref(x, mask, g_norm, Wq, Wkv, q_scale, k_scale, null_kv, null_attn_bias, w0, b0, g0, w1, b1, g1, w2, b2, Wout, g_out):
        import jax, jax.numpy as jnp
        import numpy as np
        DIM = 256
        HEADS = 16
        DIM_HEAD = 64
        SCALE = 8.0

        def ln(x, g, eps=1e-05):
            mean = x.mean(axis=-1, keepdims=True)
            var = ((x - mean) ** 2).mean(axis=-1, keepdims=True)
            return (x - mean) * jax.lax.rsqrt(var + eps) * g

        def l2norm(t):
            n = jnp.maximum(jnp.linalg.norm(t, axis=-1, keepdims=True), 1e-12)
            return t / n

        def rel_pos_bias(n, w0, b0, g0, w1, b1, g1, w2, b2, dtype):
            pos = jnp.arange(-n + 1, n, dtype=dtype)[:, None]
            h = jax.nn.silu(ln(pos @ w0 + b0, g0))
            h = jax.nn.silu(ln(h @ w1 + b1, g1))
            h = h @ w2 + b2
            i = jnp.arange(n)
            idx = i[:, None] - i[None, :] + n - 1
            bias = h[idx]
            return jnp.transpose(bias, (2, 0, 1))
        b, n, _ = x.shape
        xn = ln(x, g_norm)
        q = (xn @ Wq).reshape(b, n, HEADS, DIM_HEAD).transpose(0, 2, 1, 3)
        kv = xn @ Wkv
        k, v = (kv[..., :DIM_HEAD], kv[..., DIM_HEAD:])
        nk = jnp.broadcast_to(null_kv[0], (b, 1, DIM_HEAD))
        nv = jnp.broadcast_to(null_kv[1], (b, 1, DIM_HEAD))
        k = jnp.concatenate([nk, k], axis=1)
        v = jnp.concatenate([nv, v], axis=1)
        q = l2norm(q) * q_scale
        k = l2norm(k) * k_scale
        sim = jnp.einsum('bhid,bjd->bhij', q, k) * SCALE
        bias = rel_pos_bias(n, w0, b0, g0, w1, b1, g1, w2, b2, q.dtype)
        null_bias = jnp.broadcast_to(null_attn_bias[:, None, None], (HEADS, n, 1))
        attn_bias = jnp.concatenate([null_bias, bias], axis=-1)
        sim = sim + attn_bias
        neg = -jnp.finfo(sim.dtype).max
        causal = jnp.triu(jnp.ones((n, n + 1), dtype=bool), k=2)
        sim = jnp.where(causal, neg, sim)
        m = jnp.pad(mask, ((0, 0), (1, 0)), constant_values=True)[:, None, None, :]
        sim = jnp.where(m, sim, neg)
        attn = jax.nn.softmax(sim, axis=-1)
        out = jnp.einsum('bhij,bjd->bhid', attn, v)
        out = out.transpose(0, 2, 1, 3).reshape(b, n, HEADS * DIM_HEAD)
        return ln(out @ Wout, g_out)

    def _L1_ffn_ref(x, Wr, W1, W2):
        import jax, jax.numpy as jnp
        import numpy as np
        import math
        EMBED_DIM = 256
        FFN_DIM = 1024
        N_EXPERTS = 8
        TOP_K = 2
        CAP_FACTOR = 1.25
        B, S, D = x.shape
        t = B * S
        xf = x.reshape(t, D)
        probs = jax.nn.softmax(xf.astype(jnp.float32) @ Wr, axis=-1)
        topk_probs, topk_experts = jax.lax.top_k(probs, TOP_K)
        cap = max(math.ceil(t * TOP_K * CAP_FACTOR / N_EXPERTS), 1)
        y = jnp.zeros_like(xf)
        for e in range(N_EXPERTS):
            mask = topk_experts == e
            gate = jnp.sum(jnp.where(mask, topk_probs, 0.0), axis=-1)
            has = jnp.any(mask, axis=-1)
            g_masked = jnp.where(has, gate, -jnp.inf)
            vals, idx = jax.lax.top_k(g_masked, cap)
            g = jnp.where(jnp.isfinite(vals), vals, 0.0)
            xe = xf[idx]
            h = jax.nn.relu(xe @ W1[e]) @ W2[e]
            y = y.at[idx].add(g[:, None] * h)
        return y.reshape(B, S, D)
    x = x + _L0_ffn_ref(_L0_cond_ref(x, cond_64, L0_cond_wt, L0_cond_wg, L0_cond_w_gate, L0_cond_w_up, L0_cond_w_down, L0_cond_sw_gate, L0_cond_sw_up, L0_cond_sw_down), L0_ffn_router_w, L0_ffn_expert_gate, L0_ffn_expert_up, L0_ffn_expert_down, L0_ffn_shared_gate, L0_ffn_shared_up, L0_ffn_shared_down)
    x = x + _L1_ffn_ref(_L1_cond_ref(x, mask_BxS_bf1, L1_cond_g_norm, L1_cond_Wq, L1_cond_Wkv, L1_cond_q_scale, L1_cond_k_scale, cond_64, L1_cond_null_attn_bias, L1_cond_w0, L1_cond_b0, L1_cond_g0, L1_cond_w1, L1_cond_b1, L1_cond_g1, L1_cond_w2, L1_cond_b2, L1_cond_Wout, L1_cond_g_out), L1_ffn_Wr, L1_ffn_W1, L1_ffn_W2)
    return x

_drawn_inputs = setup_inputs


def setup_inputs(seed=0):
    import zlib

    import numpy as np

    out = dict(_drawn_inputs(seed))
    spreads = {'L1_cond_g_norm': (1.0, 0.2),
     'L1_cond_q_scale': (1.0, 0.2),
     'L1_cond_k_scale': (1.0, 0.2),
     'L1_cond_b0': (0.0, 0.1),
     'L1_cond_g0': (1.0, 0.2),
     'L1_cond_b1': (0.0, 0.1),
     'L1_cond_g1': (1.0, 0.2),
     'L1_cond_b2': (0.0, 0.1),
     'L1_cond_g_out': (1.0, 0.2)}
    factors = {}
    for name, (base, spread) in spreads.items():
        noise = np.random.default_rng([zlib.crc32(name.encode()), seed]).standard_normal(out[name].shape)
        drawn = base * np.exp(spread * noise) if base else spread * noise
        out[name] = jnp.asarray(drawn.astype(out[name].dtype))
    for name, factor in factors.items():
        out[name] = (out[name] * factor).astype(out[name].dtype)
    return out
```

```python
import numpy as np
import concourse.bass as bass
from concourse import mybir
from contextlib import ExitStack

F32 = mybir.dt.float32
BF16 = mybir.dt.bfloat16
I32 = mybir.dt.int32
U8 = mybir.dt.uint8
ALU = mybir.AluOpType
ACT = mybir.ActivationFunctionType
AX = mybir.AxisListType.X

P = 128
BATCH, SEQ, D = 2, 1024, 256
TOK = BATCH * SEQ
KT = D // P
NT = TOK // P
BLK = 512
NB = TOK // BLK
TPB = BLK // P
E = 8
HEADS, DH = 16, 64
NCH = HEADS * DH // P
NQ = SEQ // P
HG = 4
NHG = HEADS // HG
UNITS = NQ * NHG
CAP = 640
BITS = 30
NEG = -1.0e30
LROW = P - 1 + SEQ

C_ID, C_MEAN, C_B64, C_TRI, C_SEL, C_WD, C_EPS, C_END = 0, 128, 256, 384, 512, 514, 522, 523
ATT_LINKS = UNITS * (HG + 1)
PAR = {}
_at = 0
for _n, _w in (("w0", 2), ("b0", 2), ("g0", 2), ("b1", 2), ("g1", 2), ("gn", 2), ("go", 2), ("qs", 1),
               ("ks", 1), ("nk", 1), ("nab", 16), ("nv", 64), ("b2", 1)):
    PAR[_n] = (_at, _at + _w)
    _at += _w
PAR_END = _at

MOE = [dict(mt=1, sh=2, pair=True), dict(mt=4, sh=4, pair=True), dict(mt=8, sh=0, pair=False)]


def wcols(mt, pair):
    return (2 if pair else 1) * KT * mt * P + mt * D


def steps_of(l):
    return NB * (E * MOE[l]["mt"] + MOE[l]["sh"])


def build(nc, A):
    ctx = ExitStack()
    with ctx:
        def sb(name, shape, dt=F32):
            return ctx.enter_context(nc.sbuf_tensor(name, shape, dt))

        def sem(name):
            return ctx.enter_context(nc.semaphore(name))

        xT = sb("xT", [P, KT, TOK])
        cst = sb("cst", [P, C_END])
        par = sb("par", [P, PAR_END])
        wbuf = [sb(f"wbuf{i}", [P, 4096]) for i in range(2)]
        wsh = sb("wsh", [P, 3072])
        small = sb("small", [P, 2048])
        TA = sb("TA", [P, HEADS * SEQ])
        PB = sb("PB", [P, 8192])
        kall = sb("kall", [P, TOK])
        vall = sb("vall", [P, NT * (DH + 1)])
        kcur = sb("kcur", [P, SEQ])
        vcur = sb("vcur", [P, NQ * (DH + 1)])
        qtile = [sb(f"qtile{i}", [P, NCH, P]) for i in range(2)]
        obuf = [sb(f"obuf{i}", [P, 2, P]) for i in range(2)]
        dbuf = [sb(f"dbuf{i}", [DH + 1, HG * P]) for i in range(2)]
        ones_bf = sb("ones_bf", [P, P], BF16)
        tri_bf = sb("tri_bf", [P, P], BF16)
        mask8 = sb("mask8", [P, NT], U8)
        bits = sb("bits", [P, BITS], I32)
        ps = ctx.enter_context(nc.psum_tensor("ps", [P, 8 * BLK], F32))

        def bank(i, n=BLK):
            return ps[:, i * BLK:i * BLK + n]

        ident = cst[:, C_ID:C_ID + P]
        meanm = cst[:, C_MEAN:C_MEAN + P]
        b64 = cst[:, C_B64:C_B64 + P]
        sel2 = cst[:, C_SEL:C_SEL + 2]
        wdesc = cst[:, C_WD:C_WD + E]
        eps = cst[:, C_EPS:C_EPS + 1]

        def pr(name, k=None):
            a, b = PAR[name]
            return par[:, a:b] if k is None else par[:, a + k:a + k + 1]

        def sm(at, n):
            return small[:, at:at + n]
        L = sm(0, 128)
        R1, R2, R3, R4 = sm(128, 128), sm(256, 128), sm(384, 128), sm(512, 128)
        M1, M2, W1c, W2c, Zc = sm(640, 16), sm(656, 16), sm(672, 16), sm(688, 16), sm(704, 16)
        comb = sm(720, 144)
        cur = [sm(864, 16), sm(880, 16)]
        thr, cand = sm(896, 8), sm(904, 8)
        cnt, take = sm(912, 8), sm(920, 8)
        cmpb = sb("cmpb", [P, P], BF16)
        stdc, rstd = sm(928, 4), sm(932, 4)
        qs8, knull, kn1, kn2 = sm(936, 1), sm(937, 2), sm(939, 1), sm(940, 1)
        n2s, rns = sm(944, 72), sm(1016, 72)
        maskf = sm(1088, 16)
        mx, sn, negm, dn, pn = sm(1104, 8), sm(1112, 4), sm(1120, 8), sm(1128, 4), sm(1136, 8)
        wrt = sm(1152, 3 * KT * E)
        wg = sm(1200, 8)
        cond = sm(1208, 2)
        vnull = sm(1216, DH + 1)

        yT = TA[:, 0:KT * TOK].rearrange("p (k t) -> p k t", k=KT)
        aT = TA[:, KT * TOK:2 * KT * TOK].rearrange("p (k t) -> p k t", k=KT)
        mo = 2 * KT * TOK
        xg = [TA[:, mo + i * 1024:mo + (i + 1) * 1024].rearrange("p (k t) -> p k t", k=KT) for i in range(2)]
        gs = [TA[:, mo + 2048 + i * BLK:mo + 2048 + (i + 1) * BLK] for i in range(2)]
        hb = [TA[:, mo + 3072 + i * BLK:mo + 3072 + (i + 1) * BLK] for i in range(2)]
        ablk = [TA[:, mo + 4096:mo + 8192].rearrange("p (c t) -> p c t", c=NCH),
                PB[:, 4096:8192].rearrange("p (c t) -> p c t", c=NCH)]
        xc = PB[:, 0:1024].rearrange("p (k t) -> p k t", k=KT)
        sq = PB[:, 1024:2048].rearrange("p (k t) -> p k t", k=KT)
        lsrc = PB[:, 2048:3072].rearrange("p (k t) -> p k t", k=KT)
        lout = PB[:, 3072:4096].rearrange("p (k t) -> p k t", k=KT)
        lrev = lsrc
        posr = PB[:, 4096:5120]
        w1sb = PB[:, 5120:5632]
        w2sb = PB[:, 5632:5664]
        lrow = PB[0:HEADS, 5664:5664 + LROW]
        qraw = TA[:, 0:9 * BLK].rearrange("p (c t) -> p c t", c=9)
        qsq = [TA[:, 9 * BLK + i * BLK:9 * BLK + (i + 1) * BLK] for i in range(2)]
        qout = [TA[:, 11 * BLK + i * BLK:11 * BLK + (i + 1) * BLK] for i in range(2)]
        wqk = PB[:, 4096:4096 + KT * 9 * P].rearrange("p (k m) -> p k m", k=KT)
        wv = PB[:, 6400:6400 + KT * DH].rearrange("p (k m) -> p k m", k=KT)
        bsel = PB[0:18, 6528:6528 + 9 * P]
        rnT = PB[0:18, 7680:7680 + BLK]
        prob = [PB[:, h * SEQ:(h + 1) * SEQ] for h in range(HG)]
        probT = PB[:, 4096:8192].rearrange("p (k h q) -> p k h q", k=NQ, h=HG)
        diag = wsh[:, 0:HG * P]
        wout = wbuf[0][:, 0:NCH * D].rearrange("p (c m) -> p c m", c=NCH)
        rden = [wbuf[1][:, 0:2048].rearrange("p (c t) -> p c t", c=4), wbuf[1][:, 2048:4096].rearrange("p (c t) -> p c t", c=4)]
        dcmp = wsh[:, 1024:1024 + 256]
        rcmp = wsh[:, 1280:1280 + 256]

        l_d = nc.dram_tensor("bias_rows", (HEADS, LROW), F32, kind="Internal").ap()
        q_d = nc.dram_tensor("q_tiles", (P, NCH, TOK), F32, kind="Internal").ap()
        o_d = nc.dram_tensor("attn_num", (P, NCH, TOK), F32, kind="Internal").ap()
        d_d = nc.dram_tensor("attn_den", (HEADS, TOK), F32, kind="Internal").ap()
        r_d = nc.dram_tensor("attn_rden", (HEADS, TOK), F32, kind="Internal").ap()

        const_in = sem("const_in")
        relw_in = sem("relw_in")
        w_in = [sem("w_in0"), sem("w_in1")]
        wsh_in = sem("wsh_in")
        ln_src, ln_mean, ln_xc, ln_sq = sem("ln_src"), sem("ln_mean"), sem("ln_xc"), sem("ln_sq")
        ln_var, ln_std, ln_rstd, ln_bc, ln_out = (sem("ln_var"), sem("ln_std"), sem("ln_rstd"), sem("ln_bc"),
                                                  sem("ln_out"))
        silu_done, w1_done, w2_done, rows_done, rows_out = (sem("silu_done"), sem("w1_done"), sem("w2_done"),
                                                            sem("rows_done"), sem("rows_out"))
        logits_done, top_diff, top_exp, comb_done = (sem("logits_done"), sem("top_diff"), sem("top_exp"),
                                                     sem("comb_done"))
        ge_ready, ge_count = sem("ge_ready"), sem("ge_count")
        tie_ready, tie_count = sem("tie_ready"), sem("tie_count")
        M = []
        for l in range(3):
            M.append({n: sem(f"m{l}_{n}") for n in ("cur", "bc", "xg", "gu", "act", "h", "down", "yacc", "leaky")})
        dchain, cap_chain, att_chain = sem("dve_chain"), sem("cap_chain"), sem("att_chain")
        q_sqfree, q_tr, q_rnT = sem("q_sqfree"), sem("q_tr"), sem("q_rnT")
        pool_init = sem("pool_init")
        qkv_w_in, wout_in = sem("qkv_w_in"), sem("wout_in")
        q_mm, q_copied, q_sq, q_n2, q_std, q_rn, q_rb, q_norm = (
            sem("q_mm"), sem("q_copied"), sem("q_sq"), sem("q_n2"), sem("q_std"), sem("q_rn"), sem("q_rb"),
            sem("q_norm"))
        q_out = [sem("q_out0"), sem("q_out1")]
        v_mm, v_done, lrev_done = sem("v_mm"), sem("v_done"), sem("lrev_done")
        nk_sq, nk_mm, nk_std, nk_done = sem("nk_sq"), sem("nk_mm"), sem("nk_std"), sem("nk_done")
        toep_in = sem("toep_in")
        kv_cur = sem("kv_cur")
        q_in = [sem("q_in0"), sem("q_in1")]
        null_mm, sim_done, added, dn_done = (sem("null_mm"), sem("sim_done"),
                                                        sem("added"), sem("dn_done"))
        exp_done, pn_done, diag_done, tr_done = (sem("exp_done"), sem("pn_done"), sem("diag_done"),
                                                 sem("tr_done"))
        evac = [sem("evac_act"), sem("evac_dve")]
        av_done, o_copied = sem("av_done"), sem("o_copied")
        o_out, batch_stored = [sem("o_out0"), sem("o_out1")], sem("batch_stored")
        den_in, rden_done, rden_out = sem("den_in"), sem("rden_done"), sem("rden_out")
        ab_in = [sem("ab_in0"), sem("ab_in1")]
        ab_scaled, proj_mm, proj_cp = sem("ab_scaled"), sem("proj_mm"), sem("proj_cp")
        y_out = sem("y_out")

        LN_REL, LN_QKV, LN_PROJ = 0, 4, 8

        block = ctx.enter_context(nc.Block())

        def groups(qt):
            n = qt + 1
            return [(a, min(a + 4, n)) for a in range(0, n, 4)]
        EV, _e = [], 0
        for qt in range(NQ):
            EV.append(_e)
            _e += NHG * 2 * len(groups(qt))
        EV_B = _e
        TR_B = 2 * EV_B

        def tr_index(u, h, g):
            qt, hg = divmod(u, NHG)
            n = len(groups(qt))
            return 2 * EV[qt] + (hg * HG + h) * n + g

        def ev_index(u, h, g):
            qt, hg = divmod(u, NHG)
            n = len(groups(qt))
            return EV[qt] + (hg * 2 + h // 2) * n + g

        @block.sync
        def _(sp):
            for dst, src in ((cst[:, :], A["cst"]), (par[:, :], A["par"]), (xT[:, :, :], A["xT"]),
                             (wrt, A["wrt"]), (wg[0:64, :], A["wg"]), (cond[0:64, :], A["condT"]),
                             (mask8[:, :], A["mask"]), (bits[:, :], A["bits"])):
                sp.dma_start(dst, src).then_inc(const_in, 16)
            for dst, src in ((posr, A["posr"]), (w1sb, A["w1"]), (w2sb, A["w2"])):
                sp.dma_start(dst, src).then_inc(relw_in, 16)

            def experts(l):
                m, src = M[l], A[f"wexp{l}"]
                n = wcols(MOE[l]["mt"], MOE[l]["pair"])
                for i in range(2):
                    sp.dma_start(wbuf[i][:, 0:n], src[i]).then_inc(w_in[i], 16)
                if MOE[l]["sh"]:
                    sp.dma_start(wsh[:, 0:wcols(MOE[l]["sh"], True)], A[f"wsh{l}"]).then_inc(wsh_in, 16)
                with sp.Fori(1, E // 2) as it:
                    for i in range(2):
                        sp.wait_ge(m["down"], (it * 2 - 1 + i) * (NB * MOE[l]["mt"]))
                        sp.dma_start(wbuf[i][:, 0:n], src[bass.ds(it * 2 + i, 1)].rearrange("a p n -> (a p) n"))\
                          .then_inc(w_in[i], 16)

            experts(0)
            sp.wait_ge(rows_done, 3)
            sp.dma_start(l_d, lrow).then_inc(rows_out, 16)
            sp.wait_ge(M[0]["down"], steps_of(0))
            experts(1)
            sp.wait_ge(rows_out, 16)
            for dst, src in ((wqk[:, :, :], A["wqk"]), (wv[:, :, :], A["wv"]), (bsel, A["bsel"])):
                sp.dma_start(dst, src).then_inc(qkv_w_in, 16)
            sp.wait_ge(M[1]["down"], steps_of(1))
            sp.dma_start(wout, A["wout"]).then_inc(wout_in, 16)
            for b in range(NB):
                for c in range(NCH):
                    n = b * 9 + c
                    sp.wait_ge(q_norm, n + 1)
                    sp.dma_start(q_d[:, c, b * BLK:(b + 1) * BLK], qout[c % 2]).then_inc(q_out[c % 2], 16)
            for i in range(2):
                sp.wait_ge(q_out[i], 16 * NB * NCH // 2)
            sp.wait_ge(q_norm, NB * 9)
            for h in range(HEADS):
                sp.dma_start(TA[:, h * SEQ:(h + 1) * SEQ],
                             bass.AP(l_d.tensor, h * LROW, [[1, P], [1, SEQ]])).then_inc(toep_in, 16)
            sp.sem_inc(batch_stored, 1)
            with sp.Fori(0, BATCH) as b:
                def load_q(qt):
                    sp.dma_start(qtile[qt % 2][:, :, :], q_d[:, :, bass.ds(b * SEQ + qt * P, P)])\
                      .then_inc(q_in[qt % 2], 16)
                sp.wait_ge(kv_cur, b + 1)
                load_q(0)
                load_q(1)
                for u in range(UNITS):
                    qt, hg = divmod(u, NHG)
                    if hg == 0 and 1 <= qt < NQ - 1:
                        sp.wait_ge(sim_done, (b * UNITS + qt * NHG) * HG)
                        load_q(qt + 1)
                    sp.wait_ge(o_copied, b * UNITS + u + 1)
                    sp.dma_start(o_d[:, hg * 2:hg * 2 + 2, bass.ds(b * SEQ + qt * P, P)], obuf[u % 2][:, :, :])\
                      .then_inc(o_out[u % 2], 16)
                    sp.dma_start(d_d[hg * HG:(hg + 1) * HG, bass.ds(b * SEQ + qt * P, P)],
                                 dbuf[u % 2][DH:DH + 1, :].rearrange("a (h q) -> a h q", h=HG))\
                      .then_inc(o_out[u % 2], 16)
                for i in range(2):
                    sp.wait_ge(o_out[i], (b + 1) * (UNITS * 16))
                sp.sem_inc(batch_stored, 1)
            sp.dma_start(dcmp, d_d.rearrange("h (a t) -> (h a) t", a=8)).then_inc(den_in, 16)
            sp.wait_ge(rden_done, 1)
            sp.dma_start(r_d.rearrange("h (a t) -> (h a) t", a=8), rcmp).then_inc(rden_out, 16)
            sp.wait_ge(rden_out, 16)

            def load_ab(b):
                sp.dma_start(ablk[b % 2][:, :, :], o_d[:, :, b * BLK:(b + 1) * BLK]).then_inc(ab_in[b % 2], 16)
                for par_ in range(2):
                    for j in range(2):
                        sp.dma_start(rden[j][par_ * 64:par_ * 64 + 64, :, :],
                                     bass.AP(r_d.tensor, (par_ + 8 * j) * TOK + b * BLK,
                                             [[0, 64], [2 * TOK, 4], [1, BLK]])).then_inc(ab_in[b % 2], 16)
            load_ab(0)
            for b in range(1, NB):
                sp.wait_ge(proj_mm, b)
                load_ab(b)
            sp.wait_ge(proj_mm, NB)
            experts(2)
            sp.wait_ge(M[2]["yacc"], E * NB)
            sp.dma_start(A["out"], xT[:, :, :]).then_inc(y_out, 16)
            sp.wait_ge(y_out, 16)

        @block.tensor
        def _(pe):
            mm = nc.tensor.matmul

            def ln_pe(i, src):
                pe.wait_ge(ln_src, i + 1)
                for k in range(KT):
                    last = mm(bank(0), meanm, src[:, k, :], start=(k == 0), stop=(k == KT - 1))
                last.then_inc(ln_mean, 1)
                pe.wait_ge(ln_sq, i + 1)
                for t in range(TPB):
                    for k in range(KT):
                        last = mm(ps[:, BLK + t:BLK + t + 1], sq[:, k, t * P:(t + 1) * P], meanm[:, 0:1],
                                  start=(k == 0), stop=(k == KT - 1))
                last.then_inc(ln_var, 1)
                pe.wait_ge(ln_rstd, i + 1)
                for t in range(TPB):
                    last = mm(ps[:, 2 * BLK + t * P:2 * BLK + (t + 1) * P],
                              rstd[:, t:t + 1].broadcast_to((P, P)), ident, start=True, stop=True)
                last.then_inc(ln_bc, 1)

            def logits_pe(l, src):
                for t in range(NT):
                    o = bank(7)[:, t * E:(t + 1) * E]
                    for k in range(KT):
                        last = mm(o, src[:, k, t * P:(t + 1) * P], wrt[:, (l * KT + k) * E:(l * KT + k + 1) * E],
                                  start=(k == 0), stop=(k == KT - 1 and l > 0))
                    if l == 0:
                        b = t * P // SEQ
                        last = mm(o, cond[0:64, b:b + 1].broadcast_to((64, P)), wg[0:64, :], start=False, stop=True)
                last.then_inc(logits_done, 1)

            def moe_items(l, j0, s0, items, mt, raw):
                m, pair = M[l], MOE[l]["pair"]
                prev = None

                def bc(n):
                    c = items[n][3]
                    pe.wait_ge(m["cur"], items[n][4])
                    for t in range(TPB):
                        tt = (n % NB) * TPB + t
                        last = mm(bank(6)[:, t * P:(t + 1) * P], cur[c][:, tt:tt + 1].broadcast_to((P, P)), ident,
                                  start=True, stop=True)
                    last.then_inc(m["bc"], 1)

                def down(n, mi, s):
                    w = items[n][0]
                    off = (2 if pair else 1) * KT * mt * P
                    pe.wait_ge(m["h"], s0 + s + 1)
                    if mi == 0 and n > 0:
                        pe.wait_ge(m["yacc"], j0 + n)
                    for k in range(KT):
                        last = mm(bank(4 + k), w[:, off + mi * D + k * P:off + mi * D + (k + 1) * P], hb[s % 2],
                                  start=(mi == 0), stop=(mi == mt - 1))
                    last.then_inc(m["down"], 1)

                bc(0)
                s = 0
                for n, (w, wsem, wval, c, cval) in enumerate(items):
                    for mi in range(mt):
                        if mi == 0:
                            if n % NB == 0:
                                pe.wait_ge(wsem, wval)
                            pe.wait_ge(m["xg"], j0 + n + 1)
                        for half in range(2 if pair else 1):
                            for k in range(KT):
                                col = half * KT * mt * P + k * mt * P + mi * P
                                x = raw[:, k, (n % NB) * BLK:(n % NB + 1) * BLK] if (l == 0 and half) else xg[n % 2][:, k, :]
                                last = mm(bank((2 if half else 0) + s % 2), w[:, col:col + P], x,
                                          start=(k == 0), stop=(k == KT - 1))
                        last.then_inc(m["gu"], 1)
                        if mi == 0 and n + 1 < len(items):
                            bc(n + 1)
                        if prev is not None:
                            down(*prev)
                        prev = (n, mi, s)
                        s += 1
                down(*prev)

            def moe_pe(l, raw, wbase):
                mt, sh = MOE[l]["mt"], MOE[l]["sh"]
                with pe.Fori(0, E // 2) as it:
                    items = [(wbuf[i], w_in[i], (it + wbase + 1) * 16, i, it * 2 + i + 1) for i in range(2) for _ in range(NB)]
                    moe_items(l, it * (2 * NB), it * (2 * NB * mt), items, mt, raw)
                if sh:
                    items = [(wsh, wsh_in, 16 * (l + 1), 0, E + 1)] * NB
                    moe_items(l, E * NB, E * NB * mt, items, sh, raw)

            pe.wait_ge(const_in, 16 * 8)
            pe.wait_ge(relw_in, 16 * 3)
            for b in range(2):
                ln_pe(LN_REL + 2 * b, lsrc)
                pe.wait_ge(silu_done, 2 * b + 1)
                for mt_ in range(KT):
                    for k in range(KT):
                        last = mm(bank(3 + mt_), w1sb[:, k * D + mt_ * P:k * D + (mt_ + 1) * P], lout[:, k, :],
                                  start=(k == 0), stop=(k == KT - 1))
                last.then_inc(w1_done, 1)
                ln_pe(LN_REL + 2 * b + 1, lsrc)
                pe.wait_ge(silu_done, 2 * b + 2)
                for k in range(KT):
                    last = mm(bank(5)[0:HEADS, :], w2sb[:, k * HEADS:(k + 1) * HEADS], lout[:, k, :],
                              start=(k == 0), stop=(k == KT - 1))
                last.then_inc(w2_done, 1)
            pe.wait_ge(nk_sq, 1)
            mm(bank(6)[:, 0:1], b64, kn1, start=True, stop=True).then_inc(nk_mm, 1)
            pe.wait_ge(nk_std, 1)
            logits_pe(0, xT)
            moe_pe(0, xT, 0)
            pe.wait_ge(M[0]["yacc"], (E + 1) * NB)
            logits_pe(1, yT)
            moe_pe(1, yT, E // 2)
            pe.wait_ge(M[1]["yacc"], (E + 1) * NB)
            pe.wait_ge(qkv_w_in, 48)
            for b in range(NB):
                ln_pe(LN_QKV + b, xT[:, :, b * BLK:(b + 1) * BLK])
                pe.wait_ge(ln_out, LN_QKV + b + 1)

                def n2_mm(c):
                    pe.wait_ge(q_sq, b * 9 + c + 1)
                    for t in range(TPB):
                        o = bank(5)[:, (t * 9 + c) * 2:(t * 9 + c) * 2 + 2]
                        last = mm(o, qsq[c % 2][:, t * P:(t + 1) * P], sel2, start=True, stop=True)
                    last.then_inc(q_n2 if c == 8 else q_sqfree, 1)
                for c in range(9):
                    n = b * 9 + c
                    if n >= 2:
                        pe.wait_ge(q_copied, n - 1)
                        pe.wait_ge(q_sq, n - 1)
                    if c == 8:
                        pe.wait_ge(lrev_done, b + 1)
                    for k in range(KT):
                        last = mm(bank(3 + c % 2), wqk[:, k, c * P:(c + 1) * P], (lrev if c == 8 else lout)[:, k, :],
                                  start=(k == 0), stop=(k == KT - 1))
                    last.then_inc(q_mm, 1)
                    if c >= 1:
                        n2_mm(c - 1)
                n2_mm(8)
                if b >= 1:
                    pe.wait_ge(v_done, b)
                for t in range(TPB):
                    for k in range(KT):
                        last = mm(bank(1)[:, t * DH:(t + 1) * DH], lrev[:, k, t * P:(t + 1) * P], wv[:, k, :],
                                  start=(k == 0), stop=(k == KT - 1))
                last.then_inc(v_mm, 1)
                pe.wait_ge(q_rn, b + 1)
                for t in range(TPB):
                    last = nc.tensor.transpose(bank(5)[0:18, t * P:(t + 1) * P], rns[:, t * 18:(t + 1) * 18], ident)
                last.then_inc(q_tr, 1)
                pe.wait_ge(q_rnT, b + 1)
                for c in range(9):
                    n = b * 9 + c
                    if n >= 2:
                        pe.wait_ge(q_norm, n - 1)
                    mm(bank(6 + n % 2), bsel[:, c * P:(c + 1) * P], rnT, start=True, stop=True).then_inc(q_rb, 1)
                pe.wait_ge(v_done, b + 1)
            pe.wait_ge(nk_done, 1)
            pe.wait_ge(pool_init, 2)
            with pe.Fori(0, BATCH) as b:
                ub = b * UNITS

                def sims(u):
                    qt, hg = divmod(u, NHG)
                    nk = (qt + 1) * P
                    if hg == 0:
                        pe.wait_ge(q_in[qt % 2], (b * (NQ // 2) + qt // 2 + 1) * 16)
                    for c in range(2):
                        last = mm(bank(7)[:, 2 * c:2 * c + 2], qtile[qt % 2][:, hg * 2 + c, :], knull,
                                  start=True, stop=True)
                    last.then_inc(null_mm, 1)
                    for h in range(HG):
                        if u * HG + h >= 2:
                            pe.wait_ge(added, (ub + u) * HG + h - 1)
                        base = (h % 2) * 64
                        for f in range(0, nk, BLK):
                            w = min(BLK, nk - f)
                            last = mm(ps[:, (h % 2) * 2 * BLK + f:(h % 2) * 2 * BLK + f + w],
                                      qtile[qt % 2][base:base + 64, hg * 2 + h // 2, :], kcur[base:base + 64, SEQ - nk + f:SEQ - nk + f + w],
                                      start=True, stop=True)
                        last.then_inc(sim_done, 1)

                pe.wait_ge(kv_cur, b + 1)
                sims(0)
                for u in range(UNITS):
                    qt, hg = divmod(u, NHG)
                    n = 0
                    done = []
                    for h in range(HG):
                        pe.wait_ge(exp_done, (ub + u) * HG + h + 1)
                        for g, (k0, k1) in enumerate(groups(qt)):
                            if n >= 2:
                                ph, pg = done[n - 2]
                                pe.wait_ge(evac[ph % 2], b * EV_B + ev_index(u, ph, pg) + 1)
                            for kt in range(k0, k1):
                                o = bank(4 + n % 2)[:, (kt - k0) * P:(kt - k0 + 1) * P]
                                last = nc.tensor.transpose(o, prob[h][:, kt * P:(kt + 1) * P], ident)
                            last.then_inc(tr_done, 1)
                            done.append((h, g))
                            n += 1
                    if u + 1 < UNITS:
                        sims(u + 1)
                    g = len(groups(qt))
                    for e in range(2):
                        pe.wait_ge(evac[e], b * EV_B + ev_index(u, 2 + e, g - 1) + 1)
                    if u >= 1:
                        pe.wait_ge(o_copied, ub + u)
                    for kt in range(qt + 1):
                        mm(bank(6)[0:DH + 1, :], vcur[:, (NQ - 1 - qt + kt) * (DH + 1):(NQ - qt + kt) * (DH + 1)],
                           probT[:, kt, :, :].rearrange("p h q -> p (h q)"), start=(kt == 0), stop=False)
                    pe.wait_ge(diag_done, ub + u + 1)
                    mm(bank(6)[0:DH + 1, :], vnull, diag, start=False, stop=True).then_inc(av_done, 1)
            pe.wait_ge(wout_in, 16)
            for b in range(NB):
                pe.wait_ge(ab_scaled, b + 1)
                for k in range(KT):
                    for c in range(NCH):
                        last = mm(bank(3 + k), wout[:, c, k * P:(k + 1) * P], ablk[b % 2][:, c, :],
                                  start=(c == 0), stop=(c == NCH - 1))
                last.then_inc(proj_mm, 1)
                ln_pe(LN_PROJ + b, lsrc)
            pe.wait_ge(ln_out, LN_PROJ + NB)
            logits_pe(2, aT)
            with pe.Fori(0, BITS) as i:
                pe.wait_ge(ge_ready, i + 1)
                mm(bank(7)[:, 0:P], ones_bf[:, :], cmpb[:, :], start=True, stop=True).then_inc(ge_count, 1)
            for i in range(3):
                pe.wait_ge(tie_ready, i + 1)
                mm(bank(7)[:, 0:P], ones_bf[:, :] if i < 2 else tri_bf[:, :], cmpb[:, :], start=True, stop=True)\
                    .then_inc(tie_count, 1)
            moe_pe(2, aT, E)

        @block.scalar
        def _(act):
            fn = nc.scalar.activation

            def ln_act(i):
                act.wait_ge(ln_xc, i + 1)
                fn(sq, xc, ACT.Square).then_inc(ln_sq, 1)
                act.wait_ge(ln_var, i + 1)
                fn(stdc, bank(1)[:, 0:TPB], ACT.Sqrt, bias=eps).then_inc(ln_std, 1)

            def moe_act(l):
                m, mt, sh, pair = M[l], MOE[l]["mt"], MOE[l]["sh"], MOE[l]["pair"]
                f = (ACT.Copy, ACT.Silu, ACT.Relu)[l]

                def steps(s0, n):
                    for s in range(n):
                        act.wait_ge(m["gu"], s0 + s + 1)
                        if pair:
                            if s >= 2:
                                act.wait_ge(m["h"], s0 + s - 1)
                            fn(gs[s % 2], bank(s % 2), f).then_inc(m["act"], 1)
                        else:
                            if s >= 2:
                                act.wait_ge(m["down"], s0 + s - 1)
                            fn(hb[s % 2], bank(s % 2), f).then_inc(m["h"], 1)
                with act.Fori(0, E // 2) as it:
                    steps(it * (2 * NB * mt), 2 * NB * mt)
                if sh:
                    steps(E * NB * mt, NB * sh)

            act.wait_ge(const_in, 16 * 8)
            for b in range(2):
                for i in range(2):
                    ln_act(LN_REL + 2 * b + i)
                    act.wait_ge(ln_out, LN_REL + 2 * b + i + 1)
                    fn(lout, lout, ACT.Silu).then_inc(silu_done, 1)
            act.wait_ge(nk_mm, 1)
            fn(kn2, bank(6)[:, 0:1], ACT.Sqrt).then_inc(nk_std, 1)

            def top_act(l):
                act.wait_ge(top_diff, l + 1)
                if l == 0:
                    fn(W2c, Zc, ACT.Exp).then_inc(top_exp, 1)
                elif l == 1:
                    fn(W2c, Zc, ACT.Exp, scale=-1.0).then_inc(top_exp, 1)
                else:
                    fn(R4, R4, ACT.Exp).then_inc(top_exp, 1)
            top_act(0)
            moe_act(0)
            top_act(1)
            moe_act(1)
            for b in range(NB):
                ln_act(LN_QKV + b)
                for c in range(9):
                    n = b * 9 + c
                    act.wait_ge(q_mm, n + 1)
                    if b >= 1:
                        act.wait_ge(q_norm, n - 9 + 1)
                    fn(qraw[:, c, :], bank(3 + c % 2), ACT.Copy).then_inc(q_copied, 1)
                    if c >= 2:
                        act.wait_ge(q_sqfree, b * 8 + c - 1)
                    fn(qsq[c % 2], bank(3 + c % 2), ACT.Square).then_inc(q_sq, 1)
                act.wait_ge(q_n2, b + 1)
                fn(n2s, bank(5)[:, 0:72], ACT.Sqrt).then_inc(q_std, 1)
                act.wait_ge(q_tr, b + 1)
                fn(rnT, bank(5)[0:18, :], ACT.Copy).then_inc(q_rnT, 1)
            with act.Fori(0, BATCH) as b:
                ub = b * UNITS

                def exps(u):
                    qt, hg = divmod(u, NHG)
                    for h in range(HG):
                        act.wait_ge(added, (ub + u) * HG + h + 1)
                        fn(prob[h][:, 0:(qt + 1) * P], prob[h][:, 0:(qt + 1) * P], ACT.Exp,
                           bias=negm[:, (u % 2) * 4 + h:(u % 2) * 4 + h + 1]).then_inc(exp_done, 1)
                    act.wait_ge(dn_done, ub + u + 1)
                    if u >= 2:
                        act.wait_ge(diag_done, ub + u - 1)
                    fn(pn[:, (u % 2) * 4:(u % 2) * 4 + 4], dn, ACT.Exp).then_inc(pn_done, 1)
                exps(0)
                for u in range(UNITS):
                    qt, hg = divmod(u, NHG)
                    for h in range(0, HG, 2):
                        for g, (k0, k1) in enumerate(groups(qt)):
                            act.wait_ge(tr_done, b * TR_B + tr_index(u, h, g) + 1)
                            n = (h * len(groups(qt)) + g) % 2
                            fn(probT[:, k0:k1, h, :], bank(4 + n)[:, 0:(k1 - k0) * P]
                               .rearrange("p (k q) -> p k q", q=P), ACT.Copy).then_inc(evac[0], 1)
                    if u + 1 < UNITS:
                        exps(u + 1)
            for b in range(NB):
                act.wait_ge(proj_mm, b + 1)
                for k in range(KT):
                    last = fn(lsrc[:, k, :], bank(3 + k), ACT.Copy)
                last.then_inc(ln_src, 1)
                ln_act(LN_PROJ + b)
            top_act(2)
            moe_act(2)

        @block.gpsimd
        def _(pool):
            nc.gpsimd.memset(ones_bf[:, :], 1.0).then_inc(pool_init, 1)
            pool.wait_ge(const_in, 16 * 8)
            nc.gpsimd.tensor_copy(tri_bf[:, :], cst[:, C_TRI:C_TRI + P]).then_inc(pool_init, 1)
            for b in range(NB):
                pool.wait_ge(ln_out, LN_QKV + b + 1)
                if b:
                    pool.wait_ge(v_mm, b)
                nc.gpsimd.tensor_copy(lrev, lout[:, :, ::-1]).then_inc(lrev_done, 1)
            pool.wait_ge(M[1]["down"], steps_of(1))
            with pool.Fori(0, BATCH) as b:
                for u in range(UNITS):
                    pool.wait_ge(pn_done, b * UNITS + u + 1)
                    pool.wait_ge(av_done, b * UNITS + u) if u else None
                    nc.gpsimd.tensor_tensor(
                        diag.rearrange("p (h q) -> p h q", h=HG),
                        ident.unsqueeze(1).broadcast_to((P, HG, P)),
                        pn[:, (u % 2) * 4:(u % 2) * 4 + 4].unsqueeze(2).broadcast_to((P, HG, P)),
                        ALU.mult).then_inc(diag_done, 1)

        @block.vector
        def _(dve):
            v = nc.vector
            chain = [0]

            def link(ins):
                chain[0] += 1
                ins.then_inc(dchain, 1)
                dve.wait_ge(dchain, chain[0])

            def ln_dve(i, src, dst, g):
                dve.wait_ge(ln_mean, i + 1)
                v.tensor_tensor(xc, src, bank(0).unsqueeze(1).broadcast_to((P, KT, BLK)), ALU.subtract)\
                    .then_inc(ln_xc, 1)
                dve.wait_ge(ln_std, i + 1)
                v.reciprocal(rstd, stdc).then_inc(ln_rstd, 1)
                dve.wait_ge(ln_bc, i + 1)
                for k in range(KT):
                    last = v.scalar_tensor_tensor(out=dst[:, k, :], in0=xc[:, k, :], scalar=pr(g, k), in1=bank(2),
                                                  op0=ALU.mult, op1=ALU.mult)
                last.then_inc(ln_out, 1)

            dve.wait_ge(const_in, 16 * 8)
            dve.wait_ge(relw_in, 16 * 3)
            for b in range(2):
                if b:
                    dve.wait_ge(w2_done, b)
                for k in range(KT):
                    last = v.tensor_scalar(lsrc[:, k, :], posr[:, b * BLK:(b + 1) * BLK], pr("w0", k), pr("b0", k),
                                           ALU.mult, ALU.add)
                last.then_inc(ln_src, 1)
                ln_dve(LN_REL + 2 * b, lsrc, lout, "g0")
                dve.wait_ge(w1_done, b + 1)
                for k in range(KT):
                    last = v.tensor_scalar(lsrc[:, k, :], bank(3 + k), pr("b1", k), None, ALU.add)
                last.then_inc(ln_src, 1)
                ln_dve(LN_REL + 2 * b + 1, lsrc, lout, "g1")
                dve.wait_ge(w2_done, b + 1)
                v.tensor_scalar(lrow[:, P - 1 + b * BLK:P - 1 + (b + 1) * BLK], bank(5)[0:HEADS, :], par[0:HEADS, PAR["b2"][0]:PAR["b2"][1]],
                                None, ALU.add).then_inc(rows_done, 1)
            v.memset(lrow[:, 0:P - 1], NEG).then_inc(rows_done, 1)
            v.tensor_tensor(kn1, pr("nk"), pr("nk"), ALU.mult).then_inc(nk_sq, 1)
            link(v.tensor_scalar(qs8, pr("qs"), 8.0, None, ALU.mult))
            link(v.tensor_copy(maskf, mask8[:, :]))
            dve.wait_ge(nk_std, 1)
            link(v.tensor_scalar(kn2, kn2, 1e-12, None, ALU.max))
            link(v.reciprocal(kn2, kn2))
            link(v.tensor_tensor(kn2, kn2, pr("nk"), ALU.mult))
            link(v.tensor_tensor(kn2, kn2, pr("ks"), ALU.mult))
            v.tensor_scalar(knull, sel2, kn2, None, ALU.mult).then_inc(nk_done, 1)
            link(v.tensor_copy(vnull[:, 0:DH], pr("nv")))
            v.memset(vnull[:, DH:DH + 1], 1.0).then_inc(nk_done, 1)
            link(v.memset(yT, 0.0))

            L3 = L.rearrange("p (t e) -> p t e", e=E)
            c3 = comb.rearrange("p (e t) -> p t e", t=NT)

            def t3(x):
                return x.rearrange("p (t e) -> p t e", e=E)

            def bt(x):
                return x.unsqueeze(2).broadcast_to((P, NT, E))

            def be(x):
                return x.unsqueeze(1).broadcast_to((P, NT, E))

            def pick(src, mval, onehot, tmp):
                link(v.tensor_reduce(mval, t3(src), AX, ALU.max))
                link(v.tensor_tensor(t3(tmp), t3(src), bt(mval), ALU.is_equal))
                link(v.tensor_tensor(t3(tmp), t3(tmp), be(wdesc), ALU.mult))
                link(v.tensor_reduce(W1c, t3(tmp), AX, ALU.max))
                link(v.tensor_tensor(t3(onehot), t3(tmp), bt(W1c), ALU.is_equal))

            def second(first, tmp):
                link(v.scalar_tensor_tensor(out=tmp, in0=first, scalar=NEG, in1=L, op0=ALU.mult, op1=ALU.add))

            def route(l):
                dve.wait_ge(logits_done, l + 1)
                link(v.tensor_scalar(L, bank(7)[:, 0:P], 0.5 if l == 0 else 1.0, None, ALU.mult))
                pick(L, M1, R1, R4)
                if l != 1:
                    second(R1, R3)
                    pick(R3, M2, R2, R4)
                link(v.memset(comb, 1.0))
                if l == 0:
                    v.tensor_tensor(Zc, M2, M1, ALU.subtract).then_inc(top_diff, 1)
                    dve.wait_ge(top_exp, 1)
                    link(v.tensor_scalar(W1c, W2c, 1.0, None, ALU.add))
                    link(v.reciprocal(W1c, W1c))
                    link(v.tensor_tensor(W2c, W2c, W1c, ALU.mult))
                    link(v.tensor_tensor(t3(R1), t3(R1), bt(W1c), ALU.mult))
                    link(v.tensor_tensor(t3(R2), t3(R2), bt(W2c), ALU.mult))
                    v.tensor_tensor(c3[:, :, 0:E], t3(R1), t3(R2), ALU.add).then_inc(comb_done, 1)
                elif l == 1:
                    v.tensor_copy(Zc, M1).then_inc(top_diff, 1)
                    dve.wait_ge(top_exp, 2)
                    link(v.tensor_scalar(W1c, W2c, 1.0, None, ALU.add))
                    link(v.reciprocal(W1c, W1c))
                    v.tensor_tensor(c3[:, :, 0:E], t3(R1), bt(W1c), ALU.mult).then_inc(comb_done, 1)
                else:
                    v.tensor_tensor(t3(R4), L3, bt(M1), ALU.subtract).then_inc(top_diff, 1)
                    link(v.tensor_tensor(R2, R1, R2, ALU.add))
                    dve.wait_ge(top_exp, 3)
                    link(v.tensor_reduce(W1c, t3(R4), AX, ALU.add))
                    link(v.reciprocal(W1c, W1c))
                    link(v.tensor_tensor(t3(R4), t3(R4), bt(W1c), ALU.mult))
                    link(v.tensor_tensor(R1, R4, R2, ALU.mult))
                    link(v.memset(thr.bitcast(I32), 0))
                    with dve.Fori(0, BITS) as i:
                        def bl(n, ins):
                            ins.then_inc(cap_chain, 1)
                            dve.wait_ge(cap_chain, i * 5 + n)
                        bl(1, v.tensor_tensor(cand.bitcast(I32), thr.bitcast(I32),
                                              bits[:, bass.ds(i, 1)].broadcast_to((P, E)), ALU.bitwise_or))
                        v.tensor_tensor(t3(cmpb[:, :]), t3(R1), be(cand), ALU.is_ge).then_inc(ge_ready, 1)
                        dve.wait_ge(ge_count, i + 1)
                        bl(2, v.tensor_reduce(cnt, bank(7)[:, 0:P].rearrange("p (t e) -> p e t", e=E), AX, ALU.add))
                        bl(3, v.tensor_scalar(take, cnt, CAP - 0.5, None, ALU.is_ge))
                        bl(4, v.tensor_tensor(cand, cand, take, ALU.mult))
                        bl(5, v.tensor_tensor(thr, thr, cand, ALU.max))
                    link(v.tensor_tensor(t3(R3), t3(R1), be(thr), ALU.is_gt))
                    v.tensor_copy(cmpb[:, :], R3).then_inc(tie_ready, 1)
                    dve.wait_ge(tie_count, 1)
                    link(v.tensor_reduce(cnt, bank(7)[:, 0:P].rearrange("p (t e) -> p e t", e=E), AX, ALU.add))
                    link(v.tensor_scalar(cnt, cnt, -1.0, float(CAP), ALU.mult, ALU.add))
                    link(v.tensor_tensor(t3(R2), t3(R1), be(thr), ALU.is_equal))
                    v.tensor_copy(cmpb[:, :], R2).then_inc(tie_ready, 1)
                    dve.wait_ge(tie_count, 2)
                    link(v.tensor_copy(R4, bank(7)[:, 0:P]))
                    v.tensor_copy(cmpb[:, :], R2).then_inc(tie_ready, 1)
                    dve.wait_ge(tie_count, 3)
                    link(v.tensor_copy(L, bank(7)[:, 0:P]))
                    for t in range(1, NT):
                        if t > 1:
                            link(v.tensor_tensor(R4[:, (t - 1) * E:t * E], R4[:, (t - 1) * E:t * E],
                                                 R4[:, (t - 2) * E:(t - 1) * E], ALU.add))
                    link(v.tensor_tensor(L[:, E:], L[:, E:], R4[:, 0:(NT - 1) * E], ALU.add))
                    link(v.tensor_tensor(t3(L), t3(L), be(cnt), ALU.is_lt))
                    link(v.tensor_tensor(R2, R2, L, ALU.mult))
                    link(v.tensor_tensor(R2, R2, R3, ALU.add))
                    v.tensor_tensor(c3[:, :, 0:E], t3(R1), t3(R2), ALU.mult).then_inc(comb_done, 1)
                dve.wait_ge(comb_done, l + 1)

            def moe_dve(l, raw, acc):
                m, mt, sh, pair = M[l], MOE[l]["mt"], MOE[l]["sh"], MOE[l]["pair"]

                def items(j0, s0, nitems, mt):
                    def weigh(n):
                        dve.wait_ge(m["bc"], j0 + n + 1)
                        if n >= 2:
                            dve.wait_ge(m["gu"], s0 + (n - 1) * mt)
                        v.tensor_tensor(xg[n % 2], raw[:, :, (n % NB) * BLK:(n % NB + 1) * BLK],
                                        bank(6).unsqueeze(1).broadcast_to((P, KT, BLK)), ALU.mult)\
                            .then_inc(m["xg"], 1)

                    def add(n):
                        dve.wait_ge(m["down"], s0 + (n + 1) * mt)
                        if n >= NB:
                            dve.wait_ge(m["yacc"], j0 + n - NB + 1)
                        a = acc[:, :, (n % NB) * BLK:(n % NB + 1) * BLK]
                        v.tensor_tensor(a, a, ps[:, 4 * BLK:6 * BLK].rearrange("p (k t) -> p k t", k=KT), ALU.add)\
                            .then_inc(m["yacc"], 1)

                    weigh(0)
                    s = 0
                    for n in range(nitems):
                        for mi in range(mt):
                            if pair:
                                dve.wait_ge(m["act"], s0 + s + 1)
                                if s >= 2:
                                    dve.wait_ge(m["down"], s0 + s - 1)
                                if l == 0:
                                    v.scalar_tensor_tensor(out=gs[s % 2], in0=gs[s % 2], scalar=0.01, in1=gs[s % 2],
                                                           op0=ALU.mult, op1=ALU.max).then_inc(m["leaky"], 1)
                                    dve.wait_ge(m["leaky"], s0 + s + 1)
                                v.tensor_tensor(hb[s % 2], gs[s % 2], bank(2 + s % 2), ALU.mult).then_inc(m["h"], 1)
                            if mi == 0:
                                if n:
                                    add(n - 1)
                                if n + 1 < nitems:
                                    weigh(n + 1)
                            s += 1
                    add(nitems - 1)

                with dve.Fori(0, E // 2) as it:
                    for i in range(2):
                        v.tensor_copy(cur[i], comb[:, bass.ds((it * 2 + i) * NT, NT)]).then_inc(m["cur"], 1)
                    items(it * (2 * NB), it * (2 * NB * mt), 2 * NB, mt)
                if sh:
                    v.tensor_copy(cur[0], comb[:, E * NT:(E + 1) * NT]).then_inc(m["cur"], 1)
                    items(E * NB, E * NB * mt, NB, sh)
                dve.wait_ge(m["yacc"], (E + (1 if sh else 0)) * NB)

            route(0)
            moe_dve(0, xT, yT)
            route(1)
            moe_dve(1, yT, xT)
            for b in range(NB):
                if b:
                    dve.wait_ge(v_mm, b)
                dve.sem_inc(ln_src, 1)
                ln_dve(LN_QKV + b, xT[:, :, b * BLK:(b + 1) * BLK], lout, "gn")
                dve.wait_ge(q_std, b + 1)
                link(v.tensor_scalar(n2s, n2s, 1e-12, None, ALU.max))
                v.reciprocal(rns, n2s).then_inc(q_rn, 1)
                dve.wait_ge(v_mm, b + 1)
                for t in range(TPB):
                    tt = (b ^ 1) * TPB + t
                    o = vall[:, tt * (DH + 1):(tt + 1) * (DH + 1)]
                    v.tensor_scalar(o[:, 0:DH], bank(1)[:, t * DH:(t + 1) * DH], maskf[:, tt:tt + 1], None, ALU.mult)
                    last = v.tensor_copy(o[:, DH:DH + 1], maskf[:, tt:tt + 1])
                last.then_inc(v_done, 1)
                for c in range(9):
                    n = b * 9 + c
                    dve.wait_ge(q_rb, n + 1)
                    if c < NCH:
                        dst = qout[c % 2]
                        w = b * (NCH // 2) + c // 2
                        if w:
                            dve.wait_ge(q_out[c % 2], 16 * w)
                    else:
                        dst = kall[:, (b ^ 1) * BLK:((b ^ 1) + 1) * BLK]
                    v.scalar_tensor_tensor(out=dst, in0=qraw[:, c, :], scalar=(qs8 if c < NCH else pr("ks")),
                                           in1=bank(6 + n % 2), op0=ALU.mult, op1=ALU.mult).then_inc(q_norm, 1)
            dve.wait_ge(v_done, NB)
            dve.wait_ge(q_norm, NB * 9)
            with dve.Fori(0, BATCH) as b:
                ub = b * UNITS
                at_c = [0]

                def tick(ins):
                    at_c[0] += 1
                    ins.then_inc(att_chain, 1)

                def adds(u):
                    qt, hg = divmod(u, NHG)
                    nk = (qt + 1) * P
                    o4 = (u % 2) * 4
                    dve.wait_ge(null_mm, ub + u + 1)
                    dve.wait_ge(sim_done, (ub + u) * HG + 1)
                    tick(v.tensor_tensor(sn, bank(7)[:, 0:HG], pr("nab")[:, hg * HG:(hg + 1) * HG], ALU.add))
                    for h in range(HG):
                        off = (hg * HG + h) * SEQ
                        tick(v.tensor_tensor_reduce(out=prob[h][:, 0:nk], in0=ps[:, (h % 2) * 2 * BLK:(h % 2) * 2 * BLK + nk],
                                                    in1=TA[:, off:off + nk], scale=1.0, scalar=-3.0e38,
                                                    op0=ALU.add, op1=ALU.max, accum_out=mx[:, o4 + h:o4 + h + 1]))
                        dve.wait_ge(att_chain, b * ATT_LINKS + at_c[0])
                        if h + 1 < HG:
                            dve.wait_ge(sim_done, (ub + u) * HG + h + 2)
                        v.tensor_scalar(negm[:, o4 + h:o4 + h + 1], mx[:, o4 + h:o4 + h + 1], sn[:, h:h + 1], -1.0,
                                        ALU.max, ALU.mult).then_inc(added, 1)
                    dve.wait_ge(added, (ub + u + 1) * HG)
                    if u:
                        dve.wait_ge(pn_done, ub + u)
                    v.tensor_tensor(dn, sn, negm[:, o4:o4 + 4], ALU.add).then_inc(dn_done, 1)

                v.tensor_copy(kcur[:, :], kall[:, bass.ds(b * SEQ, SEQ)])
                v.tensor_copy(vcur[:, :], vall[:, bass.ds(b * (NQ * (DH + 1)), NQ * (DH + 1))]).then_inc(kv_cur, 1)
                adds(0)
                for u in range(UNITS):
                    qt, hg = divmod(u, NHG)
                    for h in range(1, HG, 2):
                        for g, (k0, k1) in enumerate(groups(qt)):
                            dve.wait_ge(tr_done, b * TR_B + tr_index(u, h, g) + 1)
                            n = (h * len(groups(qt)) + g) % 2
                            v.tensor_copy(probT[:, k0:k1, h, :], bank(4 + n)[:, 0:(k1 - k0) * P]
                                          .rearrange("p (k q) -> p k q", q=P)).then_inc(evac[1], 1)
                    if u + 1 < UNITS:
                        adds(u + 1)
                    dve.wait_ge(av_done, ub + u + 1)
                    if u >= 2:
                        dve.wait_ge(o_out[u % 2], b * (UNITS * 16) + (u // 2) * 32)
                    elif u == 0:
                        dve.wait_ge(batch_stored, b + 1)
                    src = bank(6).rearrange("p (c a q) -> p c a q", c=2, a=2)
                    for a in range(2):
                        v.tensor_copy(obuf[u % 2][a * 64:a * 64 + 64, :, :], src[0:DH, :, a, :])
                    v.tensor_copy(dbuf[u % 2][DH:DH + 1, :], bank(6)[DH:DH + 1, :]).then_inc(o_copied, 1)
                assert at_c[0] == ATT_LINKS
            dve.wait_ge(den_in, 16)
            v.reciprocal(rcmp, dcmp).then_inc(rden_done, 1)
            for b in range(NB):
                dve.wait_ge(ab_in[b % 2], 16 * 5 * (b // 2 + 1))
                for j in range(2):
                    a = ablk[b % 2][:, 4 * j:4 * j + 4, :]
                    last = v.tensor_tensor(a, a, rden[j], ALU.mult)
                last.then_inc(ab_scaled, 1)
                ln_dve(LN_PROJ + b, lsrc, aT[:, :, b * BLK:(b + 1) * BLK], "go")
            route(2)
            moe_dve(2, aT, xT)


_OUT = ("out_dram", (P, KT, TOK))


def kernel(**inp):
    import numpy as _np
    import concourse.bacc as _bacc
    from concourse import mybir as _mybir
    from concourse.bass_utils import run_bass_kernel_spmd as _run
    c = _np.ascontiguousarray
    g = {k: _np.asarray(a) for k, a in inp.items()}

    def feat(a):
        return a.reshape(KT, P, -1).transpose(1, 0, 2)

    def flat(a):
        return a.reshape(P, -1)

    def expert(gate, up, down):
        parts = [flat(feat(gate))] + ([flat(feat(up))] if up is not None else [])
        parts.append(flat(down.reshape(-1, P, D).transpose(1, 0, 2)))
        return _np.concatenate(parts, axis=1)

    def col(a):
        return a.reshape(KT, P).T

    def rep(a):
        return _np.broadcast_to(a.reshape(1, -1), (P, a.size))

    def dup(a):
        return _np.concatenate([a, a]).reshape(P, 1)

    arr = {}
    arr["xT"] = c(feat(g["x"].reshape(TOK, D).T))
    cst = _np.zeros((P, C_END), _np.float32)
    cst[:, C_ID:C_ID + P] = _np.eye(P)
    cst[:, C_MEAN:C_MEAN + P] = 1.0 / D
    cst[:64, C_B64:C_B64 + 64] = 1.0
    cst[64:, C_B64 + 64:C_B64 + P] = 1.0
    cst[:, C_TRI:C_TRI + P] = _np.triu(_np.ones((P, P)), 1)
    cst[:64, C_SEL] = 1.0
    cst[64:, C_SEL + 1] = 1.0
    cst[:, C_WD:C_WD + E] = E - _np.arange(E)
    cst[:, C_EPS] = 1e-5
    arr["cst"] = cst
    b2 = _np.zeros((P, 1), _np.float32)
    b2[:HEADS, 0] = g["L1_cond_b2"]
    cond = g["cond_64"]
    pieces = dict(w0=col(g["L1_cond_w0"][0]), b0=col(g["L1_cond_b0"]), g0=col(g["L1_cond_g0"]),
                  b1=col(g["L1_cond_b1"]), g1=col(g["L1_cond_g1"]), gn=col(g["L1_cond_g_norm"]),
                  go=col(g["L1_cond_g_out"]), qs=dup(g["L1_cond_q_scale"]), ks=dup(g["L1_cond_k_scale"]),
                  nk=dup(cond[0]), nab=rep(g["L1_cond_null_attn_bias"]), nv=rep(cond[1]), b2=b2)
    arr["par"] = c(_np.concatenate([pieces[n] for n in PAR], axis=1))
    arr["wrt"] = c(_np.concatenate([flat(feat(g["L0_cond_wt"].T)), flat(feat(g["L0_ffn_router_w"].T)),
                                    flat(feat(g["L1_ffn_Wr"]))], axis=1))
    arr["wg"] = c(g["L0_cond_wg"].T)
    arr["condT"] = c(cond.T)
    arr["mask"] = c(g["mask_BxS_bf1"][:, ::-1].reshape(NT, P).T).view(_np.uint8)
    arr["bits"] = c(_np.broadcast_to((1 << _np.arange(BITS - 1, -1, -1)).astype(_np.int32), (P, BITS)))
    arr["posr"] = c(_np.broadcast_to(_np.arange(SEQ).astype(_np.float32), (P, SEQ)))
    arr["w1"] = c(flat(feat(g["L1_cond_w1"])))
    arr["w2"] = c(flat(feat(g["L1_cond_w2"])))
    arr["wexp0"] = c(_np.stack([expert(g["L0_cond_w_gate"][e], g["L0_cond_w_up"][e], g["L0_cond_w_down"][e]) for e in range(E)]))
    arr["wsh0"] = c(expert(g["L0_cond_sw_gate"], g["L0_cond_sw_up"], g["L0_cond_sw_down"]))
    arr["wexp1"] = c(_np.stack([expert(g["L0_ffn_expert_gate"][e], g["L0_ffn_expert_up"][e], g["L0_ffn_expert_down"][e]) for e in range(E)]))
    arr["wsh1"] = c(expert(g["L0_ffn_shared_gate"], g["L0_ffn_shared_up"], g["L0_ffn_shared_down"]))
    arr["wexp2"] = c(_np.stack([expert(g["L1_ffn_W1"][e], None, g["L1_ffn_W2"][e]) for e in range(E)]))
    wkv = g["L1_cond_Wkv"]
    arr["wqk"] = c(feat(_np.concatenate([g["L1_cond_Wq"], wkv[:, :DH], wkv[:, :DH]], axis=1)))
    arr["wv"] = c(feat(wkv[:, DH:]))
    bsel = _np.zeros((18, 9 * P), _np.float32)
    for c_ in range(9):
        bsel[2 * c_, c_ * P:c_ * P + 64] = 1.0
        bsel[2 * c_ + 1, c_ * P + 64:(c_ + 1) * P] = 1.0
    arr["bsel"] = bsel
    arr["wout"] = c(g["L1_cond_Wout"].reshape(NCH, P, D).transpose(1, 0, 2))

    nc = _bacc.Bacc("TRN2", target_bir_lowering=False, num_devices=1)
    A = {n: nc.dram_tensor(f"{n}_dram", a.shape, _mybir.dt.from_np(a.dtype), kind="ExternalInput").ap()
         for n, a in arr.items()}
    A["out"] = nc.dram_tensor(_OUT[0], _OUT[1], _mybir.dt.float32, kind="ExternalOutput").ap()
    build(nc, A)
    r = _run(nc, [{f"{n}_dram": a for n, a in arr.items()}], core_ids=[0])
    o = r.results[0][_OUT[0]]
    return o.transpose(2, 1, 0).reshape(BATCH, SEQ, D)
```

```python
import numpy as np
import concourse.bass as bass
from concourse import mybir
from contextlib import ExitStack

F32 = mybir.dt.float32
BF16 = mybir.dt.bfloat16
I32 = mybir.dt.int32
U8 = mybir.dt.uint8
U32 = mybir.dt.uint32
ALU = mybir.AluOpType
ACT = mybir.ActivationFunctionType
AX = mybir.AxisListType.X

P = 128
BATCH, SEQ, D = 2, 1024, 256
TOK = BATCH * SEQ
KT = D // P
NT = TOK // P
BLK = 512
NB = TOK // BLK
TPB = BLK // P
E = 8
HEADS, DH = 16, 64
NCH = HEADS * DH // P
NQ = SEQ // P
HG = 4
NHG = HEADS // HG
UNITS = NQ * NHG
CAP = 640
BITS = 30
NEG = -1.0e30
LROW = P - 1 + SEQ

PAR = {}
_at = 0
for _n, _w in (("w0", 2), ("b0", 2), ("g0", 2), ("b1", 2), ("g1", 2), ("gn", 2), ("go", 2), ("qs", 1),
               ("ks", 1), ("nk", 1), ("nab", 16), ("nv", 64), ("b2", 1)):
    PAR[_n] = (_at, _at + _w)
    _at += _w
PAR_END = _at

SB = 256
MOE = [dict(mt=1, sh=2, pair=True, top=2), dict(mt=4, sh=4, pair=True, top=1),
       dict(mt=8, sh=0, pair=False, top=2)]
NBLK = [TOK * m["top"] // SB + E - 1 for m in MOE[:2]]
ETILES = (3, 2)
assert sum(ETILES) * P == CAP
SLOTS = [NBLK[0] * SB, NBLK[1] * SB, E * CAP]
NTAB = max(NBLK) + 1

C_ID, C_MEAN, C_B64, C_TRI, C_SEL, C_WD, C_EPS = 0, 128, 256, 384, 512, 514, 522
C_JT, C_KT, C_EB, C_TR = 523, 531, 531 + NTAB, 539 + NTAB
C_END = C_TR + 2 * NT
ATT_LINKS = UNITS * (HG + 1)


def wcols(mt, pair):
    return (2 if pair else 1) * KT * mt * P + mt * D


def steps_of(l):
    blocks = NBLK[l] if l < 2 else E * len(ETILES)
    return NB * MOE[l]["sh"] + blocks * MOE[l]["mt"]


def build(nc, A):
    ctx = ExitStack()
    with ctx:
        def sb(name, shape, dt=F32):
            return ctx.enter_context(nc.sbuf_tensor(name, shape, dt))

        def sem(name):
            return ctx.enter_context(nc.semaphore(name))

        xT = sb("xT", [P, KT, TOK])
        cst = sb("cst", [P, C_END])
        par = sb("par", [P, PAR_END])
        wbuf = [sb(f"wbuf{i}", [P, 4096]) for i in range(2)]
        wsh = sb("wsh", [P, 3072])
        small = sb("small", [P, 2048])
        TA = sb("TA", [P, HEADS * SEQ])
        PB = sb("PB", [P, 8192])
        kall = sb("kall", [P, TOK])
        vall = sb("vall", [P, NT * (DH + 1)])
        kcur = sb("kcur", [P, SEQ])
        vcur = sb("vcur", [P, NQ * (DH + 1)])
        qtile = [sb(f"qtile{i}", [P, NCH, P]) for i in range(2)]
        obuf = [sb(f"obuf{i}", [P, 2, P]) for i in range(2)]
        dbuf = [sb(f"dbuf{i}", [DH + 1, HG * P]) for i in range(2)]
        ones_bf = sb("ones_bf", [P, P], BF16)
        tri_bf = sb("tri_bf", [P, P], BF16)
        mask8 = sb("mask8", [P, NT], U8)
        bits = sb("bits", [P, BITS], I32)
        put_i = sb("put_i", [P, 2 * NT], U32)
        get_i = sb("get_i", [P, 2 * NT], U32)
        btab = sb("btab", [P, NTAB], I32)
        ps = ctx.enter_context(nc.psum_tensor("ps", [P, 8 * BLK], F32))

        def bank(i, n=BLK):
            return ps[:, i * BLK:i * BLK + n]

        ident = cst[:, C_ID:C_ID + P]
        meanm = cst[:, C_MEAN:C_MEAN + P]
        b64 = cst[:, C_B64:C_B64 + P]
        sel2 = cst[:, C_SEL:C_SEL + 2]
        wdesc = cst[:, C_WD:C_WD + E]
        eps = cst[:, C_EPS:C_EPS + 1]

        def pr(name, k=None):
            a, b = PAR[name]
            return par[:, a:b] if k is None else par[:, a + k:a + k + 1]

        def sm(at, n):
            return small[:, at:at + n]
        L = sm(0, 128)
        G, KP, TI = sm(1600, 128), sm(1728, 128), sm(1856, 128)
        R1, R2, R3, R4 = sm(128, 128), sm(256, 128), sm(384, 128), sm(512, 128)
        M1, M2, W1c, W2c, Zc = sm(640, 16), sm(656, 16), sm(672, 16), sm(688, 16), sm(704, 16)
        wts = sm(720, 32)
        slotf = sm(752, 32)
        keptf = sm(784, 32)
        rank_end = sm(816, 8)
        nblk, eblk = sm(824, 8), sm(832, 8)
        ebase = sm(840, 8)
        thr, cand = sm(896, 8), sm(904, 8)
        cnt, take = sm(912, 8), sm(920, 8)
        cmpb = sb("cmpb", [P, P], BF16)
        stdc, rstd = sm(928, 4), sm(932, 4)
        qs8, knull, kn1, kn2 = sm(936, 1), sm(937, 2), sm(939, 1), sm(940, 1)
        n2s, rns = sm(944, 72), sm(1016, 72)
        maskf = sm(1088, 16)
        mx, sn, negm, dn, pn = sm(1104, 8), sm(1112, 4), sm(1120, 8), sm(1128, 4), sm(1136, 8)
        tabf = sm(1290, 32)
        jcmp = sm(1328, 64)
        kcmp = sm(1400, NTAB * E)
        wrt = sm(1152, 3 * KT * E)
        wg = sm(1200, 8)
        cond = sm(1208, 2)
        vnull = sm(1216, DH + 1)

        yT = TA[:, 0:KT * TOK].rearrange("p (k t) -> p k t", k=KT)
        aT = TA[:, KT * TOK:2 * KT * TOK].rearrange("p (k t) -> p k t", k=KT)
        rows = TA[:, 8192:12288].rearrange("p (t d) -> p t d", t=NT)
        xb = [TA[:, 12288 + i * 768:12288 + (i + 1) * 768].rearrange("p (k t) -> p k t", k=KT) for i in range(2)]
        rin = [TA[:, 13824 + i * 768:13824 + (i + 1) * 768].rearrange("p (t d) -> p t d", t=3) for i in range(2)]
        got = [[TA[:, 15360 + (i * 2 + c) * D:15360 + (i * 2 + c + 1) * D] for c in range(2)] for i in range(2)]
        gs = [PB[:, i * BLK:(i + 1) * BLK] for i in range(2)]
        hb = [PB[:, 1024 + i * BLK:1024 + (i + 1) * BLK] for i in range(2)]
        yrow = [PB[:, 2048 + i * 768:2048 + (i + 1) * 768].rearrange("p (t d) -> p t d", t=3) for i in range(2)]
        zrow = PB[:, 6912:6912 + D]
        ablk = [TA[:, 12288:16384].rearrange("p (c t) -> p c t", c=NCH),
                PB[:, 4096:8192].rearrange("p (c t) -> p c t", c=NCH)]
        xc = PB[:, 0:1024].rearrange("p (k t) -> p k t", k=KT)
        sq = PB[:, 1024:2048].rearrange("p (k t) -> p k t", k=KT)
        lsrc = PB[:, 2048:3072].rearrange("p (k t) -> p k t", k=KT)
        lout = PB[:, 3072:4096].rearrange("p (k t) -> p k t", k=KT)
        lrev = lsrc
        posr = PB[:, 4096:5120]
        w1sb = PB[:, 5120:5632]
        w2sb = PB[:, 5632:5664]
        lrow = PB[0:HEADS, 5664:5664 + LROW]
        qraw = TA[:, 0:9 * BLK].rearrange("p (c t) -> p c t", c=9)
        qsq = [TA[:, 9 * BLK + i * BLK:9 * BLK + (i + 1) * BLK] for i in range(2)]
        qout = [TA[:, 11 * BLK + i * BLK:11 * BLK + (i + 1) * BLK] for i in range(2)]
        wqk = PB[:, 4096:4096 + KT * 9 * P].rearrange("p (k m) -> p k m", k=KT)
        wv = PB[:, 6400:6400 + KT * DH].rearrange("p (k m) -> p k m", k=KT)
        bsel = PB[0:18, 6528:6528 + 9 * P]
        rnT = PB[0:18, 7680:7680 + BLK]
        prob = [PB[:, h * SEQ:(h + 1) * SEQ] for h in range(HG)]
        probT = PB[:, 4096:8192].rearrange("p (k h q) -> p k h q", k=NQ, h=HG)
        diag = wsh[:, 0:HG * P]
        wout = wbuf[0][:, 0:NCH * D].rearrange("p (c m) -> p c m", c=NCH)
        rden = [wbuf[1][:, 0:2048].rearrange("p (c t) -> p c t", c=4), wbuf[1][:, 2048:4096].rearrange("p (c t) -> p c t", c=4)]
        dcmp = wsh[:, 1024:1024 + 256]
        rcmp = wsh[:, 1280:1280 + 256]

        l_d = nc.dram_tensor("bias_rows", (HEADS, LROW), F32, kind="Internal").ap()
        q_d = nc.dram_tensor("q_tiles", (P, NCH, TOK), F32, kind="Internal").ap()
        o_d = nc.dram_tensor("attn_num", (P, NCH, TOK), F32, kind="Internal").ap()
        d_d = nc.dram_tensor("attn_den", (HEADS, TOK), F32, kind="Internal").ap()
        xs_d = [nc.dram_tensor(f"slots_in{l}", (SLOTS[l] + (2 * TOK if l == 2 else 0), D), F32, kind="Internal").ap()
                for l in range(3)]
        ys_d = [nc.dram_tensor(f"slots_out{l}", (SLOTS[l], D), F32, kind="Internal").ap() for l in range(3)]
        r_d = nc.dram_tensor("attn_rden", (HEADS, TOK), F32, kind="Internal").ap()

        const_in = sem("const_in")
        relw_in = sem("relw_in")
        wsh_in = sem("wsh_in")
        ln_src, ln_mean, ln_xc, ln_sq = sem("ln_src"), sem("ln_mean"), sem("ln_xc"), sem("ln_sq")
        ln_var, ln_std, ln_rstd, ln_bc, ln_out = (sem("ln_var"), sem("ln_std"), sem("ln_rstd"), sem("ln_bc"),
                                                  sem("ln_out"))
        silu_done, w1_done, w2_done, rows_done, rows_out = (sem("silu_done"), sem("w1_done"), sem("w2_done"),
                                                            sem("rows_done"), sem("rows_out"))
        logits_done, top_diff, top_exp = sem("logits_done"), sem("top_diff"), sem("top_exp")
        ge_ready, ge_count = sem("ge_ready"), sem("ge_count")
        tie_ready, tie_count = sem("tie_ready"), sem("tie_count")
        rank_ready, rank_count = sem("rank_ready"), sem("rank_count")
        score_done, rows_in, zeroed = sem("score_done"), sem("rows_in"), sem("zeroed")
        M = []
        for l in range(3):
            M.append({n: sem(f"m{l}_{n}") for n in (
                "rowt", "rows", "slots", "put", "gu", "act", "h", "down", "yacc", "leaky",
                "w0", "w1", "in0", "in1", "bt", "xb", "yrow", "out0", "out1",
                "get0", "get1", "mixed", "mixt", "acc")})
        dchain, cap_chain, att_chain = sem("dve_chain"), sem("cap_chain"), sem("att_chain")
        q_sqfree, q_tr, q_rnT = sem("q_sqfree"), sem("q_tr"), sem("q_rnT")
        pool_init = sem("pool_init")
        qkv_w_in, wout_in = sem("qkv_w_in"), sem("wout_in")
        q_mm, q_copied, q_sq, q_n2, q_std, q_rn, q_rb, q_norm = (
            sem("q_mm"), sem("q_copied"), sem("q_sq"), sem("q_n2"), sem("q_std"), sem("q_rn"), sem("q_rb"),
            sem("q_norm"))
        q_out = [sem("q_out0"), sem("q_out1")]
        v_mm, v_done, lrev_done = sem("v_mm"), sem("v_done"), sem("lrev_done")
        nk_sq, nk_mm, nk_std, nk_done = sem("nk_sq"), sem("nk_mm"), sem("nk_std"), sem("nk_done")
        toep_in = sem("toep_in")
        kv_cur = sem("kv_cur")
        q_in = [sem("q_in0"), sem("q_in1")]
        null_mm, sim_done, added, dn_done = (sem("null_mm"), sem("sim_done"),
                                                        sem("added"), sem("dn_done"))
        exp_done, pn_done, diag_done, tr_done = (sem("exp_done"), sem("pn_done"), sem("diag_done"),
                                                 sem("tr_done"))
        evac = [sem("evac_act"), sem("evac_dve")]
        av_done, o_copied = sem("av_done"), sem("o_copied")
        o_out, batch_stored = [sem("o_out0"), sem("o_out1")], sem("batch_stored")
        den_in, rden_done, rden_out = sem("den_in"), sem("rden_done"), sem("rden_out")
        ab_in = [sem("ab_in0"), sem("ab_in1")]
        ab_scaled, proj_mm, proj_cp = sem("ab_scaled"), sem("proj_mm"), sem("proj_cp")
        y_out = sem("y_out")

        LN_REL, LN_QKV, LN_PROJ = 0, 4, 8

        class Blocks:
            def __init__(self, l):
                if l < 2:
                    self.blocks = [dict(nt=SB // P, w=i, row=i * SB, fresh=True) for i in range(2)]
                    self.turns, self.rest = divmod(NBLK[l], 2)
                    self.rows_turn = 2 * SB
                else:
                    self.blocks = [dict(nt=nt, w=i, row=i * CAP + j * ETILES[0] * P, fresh=j == 0)
                                   for i in range(2) for j, nt in enumerate(ETILES)]
                    self.turns, self.rest = E // 2, 0
                    self.rows_turn = 2 * CAP
                self.n = len(self.blocks)
                self.total = self.n * self.turns + self.rest
        BL = [Blocks(l) for l in range(3)]

        block = ctx.enter_context(nc.Block())

        def groups(qt):
            n = qt + 1
            return [(a, min(a + 4, n)) for a in range(0, n, 4)]
        EV, _e = [], 0
        for qt in range(NQ):
            EV.append(_e)
            _e += NHG * 2 * len(groups(qt))
        EV_B = _e
        TR_B = 2 * EV_B

        def tr_index(u, h, g):
            qt, hg = divmod(u, NHG)
            n = len(groups(qt))
            return 2 * EV[qt] + (hg * HG + h) * n + g

        def ev_engine(u, h, g):
            return (h * len(groups(u // NHG)) + g) % 2

        def ev_index(u, h, g):
            qt, hg = divmod(u, NHG)
            n = len(groups(qt))
            return EV[qt] + hg * 2 * n + (h * n + g) // 2

        @block.sync
        def _(sp):
            for dst, src in ((cst[:, :], A["cst"]), (par[:, :], A["par"]), (xT[:, :, :], A["xT"]),
                             (wrt, A["wrt"]), (wg[0:64, :], A["wg"]), (cond[0:64, :], A["condT"]),
                             (mask8[:, :], A["mask"]), (bits[:, :], A["bits"])):
                sp.dma_start(dst, src).then_inc(const_in, 16)
            sp.dma_start(rows, A["xrows"]).then_inc(rows_in, 16)
            for dst, src in ((posr, A["posr"]), (w1sb, A["w1"]), (w2sb, A["w2"])):
                sp.dma_start(dst, src).then_inc(relw_in, 16)

            sp.wait_ge(pool_init, 3)
            for l in range(3):
                n = SLOTS[l] // P
                sp.dma_start(xs_d[l][0:SLOTS[l], :].rearrange("(p n) d -> p n d", n=n),
                             zrow.unsqueeze(1).broadcast_to((P, n, D))).then_inc(zeroed, 16)

            def shared_weights(l):
                sp.dma_start(wsh[:, 0:wcols(MOE[l]["sh"], True)], A[f"wsh{l}"]).then_inc(wsh_in, 16)

            def blocks(l):
                m, bl, src, mt, ss = M[l], BL[l], A[f"wexp{l}"], MOE[l]["mt"], NB * MOE[l]["sh"]
                ncol = wcols(mt, MOE[l]["pair"])

                def weights(it, k):
                    if l < 2:
                        ex = sp.value_load(btab[0:1, bass.ds(it * 2 + k, 1)], min_val=0, max_val=E - 1)
                    else:
                        ex = it * 2 + bl.blocks[k]["w"]
                    w = bl.blocks[k]["w"]
                    sp.dma_start(wbuf[w][:, 0:ncol], src[bass.ds(ex, 1)].rearrange("a p n -> (a p) n"))\
                      .then_inc(m[f"w{w}"], 16)

                def load(it, k):
                    b = bl.blocks[k]
                    sp.dma_start(rin[k % 2][:, 0:b["nt"], :],
                                 xs_d[l][bass.ds(it * bl.rows_turn + b["row"], b["nt"] * P), :]
                                 .rearrange("(t p) d -> p t d", p=P)).then_inc(m[f"in{k % 2}"], 16)

                def store(it, k, n):
                    b = bl.blocks[k]
                    sp.wait_ge(m["yrow"], n + 1)
                    sp.dma_start(ys_d[l][bass.ds(it * bl.rows_turn + b["row"], b["nt"] * P), :]
                                 .rearrange("(t p) d -> p t d", p=P), yrow[k % 2][:, 0:b["nt"], :])\
                      .then_inc(m[f"out{k % 2}"], 16)

                for i in range(2):
                    sp.sem_inc(m[f"out{i}"], 16)
                if l == 2:
                    weights(0, 0)
                    weights(0, 2)
                sp.wait_ge(zeroed, 48)
                sp.wait_ge(m["put"], 16 * NT * MOE[l]["top"])
                if l < 2:
                    for k in range(2):
                        weights(0, k)
                        load(0, k)
                else:
                    load(0, 0)
                    load(0, 1)

                def step(it, k, n):
                    sp.wait_ge(m["bt"], n - 1)
                    load(it, k)
                    if bl.blocks[k]["fresh"]:
                        sp.wait_ge(m["down"], (n - (1 if l < 2 else 2)) * mt + ss)
                        weights(it, k)
                    back = k - 2
                    store(it if back >= 0 else it - 1, back % bl.n, n - 2)
                if l < 2:
                    with sp.Fori(1, bl.turns) as it:
                        for k in range(2):
                            step(it, k, it * 2 + k)
                    for k in range(bl.rest):
                        step(bl.turns, k, bl.turns * 2 + k)
                    last = bl.total - 2
                    for n in (last, last + 1):
                        store(n // 2, n % 2, n)
                else:
                    for k in (2, 3):
                        sp.wait_ge(m["bt"], k - 1)
                        load(0, k)
                        store(0, k - 2, k - 2)
                    with sp.Fori(1, bl.turns) as it:
                        for k in range(4):
                            step(it, k, it * 4 + k)
                    for k in (2, 3):
                        store(bl.turns - 1, k, bl.total - 4 + k)

            shared_weights(0)
            blocks(0)
            sp.wait_ge(rows_done, 3)
            sp.dma_start(l_d, lrow).then_inc(rows_out, 16)
            shared_weights(1)
            blocks(1)
            sp.wait_ge(rows_out, 16)
            for dst, src in ((wqk[:, :, :], A["wqk"]), (wv[:, :, :], A["wv"]), (bsel, A["bsel"])):
                sp.dma_start(dst, src).then_inc(qkv_w_in, 16)
            sp.wait_ge(M[1]["down"], steps_of(1))
            sp.dma_start(wout, A["wout"]).then_inc(wout_in, 16)
            for b in range(NB):
                for c in range(NCH):
                    n = b * 9 + c
                    sp.wait_ge(q_norm, n + 1)
                    sp.dma_start(q_d[:, c, b * BLK:(b + 1) * BLK], qout[c % 2]).then_inc(q_out[c % 2], 16)
            for i in range(2):
                sp.wait_ge(q_out[i], 16 * NB * NCH // 2)
            sp.wait_ge(q_norm, NB * 9)
            for h in range(HEADS):
                sp.dma_start(TA[:, h * SEQ:(h + 1) * SEQ],
                             bass.AP(l_d.tensor, h * LROW, [[1, P], [1, SEQ]])).then_inc(toep_in, 16)
            sp.sem_inc(batch_stored, 1)
            with sp.Fori(0, BATCH) as b:
                def load_q(qt):
                    sp.dma_start(qtile[qt % 2][:, :, :], q_d[:, :, bass.ds(b * SEQ + qt * P, P)])\
                      .then_inc(q_in[qt % 2], 16)
                sp.wait_ge(kv_cur, b + 1)
                load_q(0)
                load_q(1)
                for u in range(UNITS):
                    qt, hg = divmod(u, NHG)
                    if hg == 0 and 1 <= qt < NQ - 1:
                        sp.wait_ge(sim_done, (b * UNITS + qt * NHG) * HG)
                        load_q(qt + 1)
                    sp.wait_ge(o_copied, b * UNITS + u + 1)
                    sp.dma_start(o_d[:, hg * 2:hg * 2 + 2, bass.ds(b * SEQ + qt * P, P)], obuf[u % 2][:, :, :])\
                      .then_inc(o_out[u % 2], 16)
                    sp.dma_start(d_d[hg * HG:(hg + 1) * HG, bass.ds(b * SEQ + qt * P, P)],
                                 dbuf[u % 2][DH:DH + 1, :].rearrange("a (h q) -> a h q", h=HG))\
                      .then_inc(o_out[u % 2], 16)
                for i in range(2):
                    sp.wait_ge(o_out[i], (b + 1) * (UNITS * 16))
                sp.sem_inc(batch_stored, 1)
            sp.dma_start(dcmp, d_d.rearrange("h (a t) -> (h a) t", a=8)).then_inc(den_in, 16)
            sp.wait_ge(rden_done, 1)
            sp.dma_start(r_d.rearrange("h (a t) -> (h a) t", a=8), rcmp).then_inc(rden_out, 16)
            sp.wait_ge(rden_out, 16)

            def load_ab(b):
                sp.dma_start(ablk[b % 2][:, :, :], o_d[:, :, b * BLK:(b + 1) * BLK]).then_inc(ab_in[b % 2], 16)
                for par_ in range(2):
                    for j in range(2):
                        sp.dma_start(rden[j][par_ * 64:par_ * 64 + 64, :, :],
                                     bass.AP(r_d.tensor, (par_ + 8 * j) * TOK + b * BLK,
                                             [[0, 64], [2 * TOK, 4], [1, BLK]])).then_inc(ab_in[b % 2], 16)
            load_ab(0)
            for b in range(1, NB):
                sp.wait_ge(proj_mm, b)
                load_ab(b)
            sp.wait_ge(proj_mm, NB)
            blocks(2)
            sp.wait_ge(M[2]["acc"], NB)
            sp.dma_start(A["out"], xT[:, :, :]).then_inc(y_out, 16)
            sp.wait_ge(y_out, 16)

        @block.tensor
        def _(pe):
            mm = nc.tensor.matmul

            def ln_pe(i, src):
                pe.wait_ge(ln_src, i + 1)
                for k in range(KT):
                    last = mm(bank(0), meanm, src[:, k, :], start=(k == 0), stop=(k == KT - 1))
                last.then_inc(ln_mean, 1)
                pe.wait_ge(ln_sq, i + 1)
                for t in range(TPB):
                    for k in range(KT):
                        last = mm(ps[:, BLK + t:BLK + t + 1], sq[:, k, t * P:(t + 1) * P], meanm[:, 0:1],
                                  start=(k == 0), stop=(k == KT - 1))
                last.then_inc(ln_var, 1)
                pe.wait_ge(ln_rstd, i + 1)
                for t in range(TPB):
                    last = mm(ps[:, 2 * BLK + t * P:2 * BLK + (t + 1) * P],
                              rstd[:, t:t + 1].broadcast_to((P, P)), ident, start=True, stop=True)
                last.then_inc(ln_bc, 1)

            def logits_pe(l, src):
                for t in range(NT):
                    o = bank(7)[:, t * E:(t + 1) * E]
                    for k in range(KT):
                        last = mm(o, src[:, k, t * P:(t + 1) * P], wrt[:, (l * KT + k) * E:(l * KT + k + 1) * E],
                                  start=(k == 0), stop=(k == KT - 1 and l > 0))
                    if l == 0:
                        b = t * P // SEQ
                        last = mm(o, cond[0:64, b:b + 1].broadcast_to((64, P)), wg[0:64, :], start=False, stop=True)
                last.then_inc(logits_done, 1)

            def ranks_pe(l, n):
                for i in range(2):
                    pe.wait_ge(rank_ready, n * 2 + i + 1)
                    mm(bank(7)[:, 0:P], ones_bf[:, :] if i == 0 else tri_bf[:, :], cmpb[:, :], start=True, stop=True)\
                        .then_inc(rank_count, 1)

            def rows_pe(l, src):
                for j in range(NT // 2):
                    if j >= 2:
                        pe.wait_ge(M[l]["rows"], 2 * (j - 1))
                    for t in (2 * j, 2 * j + 1):
                        for k in range(KT):
                            o = (4 + j % 2) * BLK + (t % 2) * D + k * P
                            last = nc.tensor.transpose(ps[:, o:o + P], src[:, k, t * P:(t + 1) * P], ident)
                    last.then_inc(M[l]["rowt"], 1)
                pe.wait_ge(M[l]["rows"], NT)

            def hidden(m, w, mt, pair, mi, s, x, n):
                for half in range(2 if pair else 1):
                    for k in range(KT):
                        col = half * KT * mt * P + k * mt * P + mi * P
                        last = mm(bank(2 * half + s % 2, n), w[:, col:col + P], x[:, k, :],
                                  start=(k == 0), stop=(k == KT - 1))
                last.then_inc(m["gu"], 1)

            def shared_pe(l, raw):
                m, sh = M[l], MOE[l]["sh"]
                prev = None

                def down(n, mi, s):
                    pe.wait_ge(m["h"], s + 1)
                    if mi == 0 and n > 0:
                        pe.wait_ge(m["yacc"], n)
                    off = 2 * KT * sh * P + mi * D
                    for k in range(KT):
                        last = mm(bank(4 + k), wsh[:, off + k * P:off + (k + 1) * P], hb[s % 2],
                                  start=(mi == 0), stop=(mi == sh - 1))
                    last.then_inc(m["down"], 1)
                pe.wait_ge(wsh_in, 16 * (l + 1))
                s = 0
                for n in range(NB):
                    for mi in range(sh):
                        hidden(m, wsh, sh, True, mi, s, raw[:, :, n * BLK:(n + 1) * BLK], BLK)
                        if prev is not None:
                            down(*prev)
                        prev = (n, mi, s)
                        s += 1
                down(*prev)
                pe.wait_ge(m["yacc"], NB)

            def blocks_pe(l):
                m, bl, mt, pair = M[l], BL[l], MOE[l]["mt"], MOE[l]["pair"]
                ybank = (4, 5) if l < 2 else (4, 5, 2)

                def turn(it, n0, s0, nblk):
                    def turned(k):
                        nt = bl.blocks[k]["nt"]
                        pe.wait_ge(m[f"in{k % 2}"], (it * (bl.n // 2) + k // 2 + 1) * 16)
                        for t in range(nt):
                            for f in range(KT):
                                last = nc.tensor.transpose(bank(6 + f)[:, t * P:(t + 1) * P],
                                                           rin[k % 2][:, t, f * P:(f + 1) * P], ident)
                        last.then_inc(m["bt"], 1)

                    def down(k, mi, s):
                        b = bl.blocks[k]
                        off = (2 if pair else 1) * KT * mt * P + mi * D
                        pe.wait_ge(m["h"], s0 + s + 1)
                        if mi == 0 and k > 0:
                            pe.wait_ge(m["yrow"], n0 + k)
                        for t in range(b["nt"]):
                            last = mm(bank(ybank[t], D), hb[s % 2][:, t * P:(t + 1) * P],
                                      wbuf[b["w"]][:, off:off + D], start=(mi == 0), stop=(mi == mt - 1))
                        last.then_inc(m["down"], 1)

                    turned(0)
                    s, prev = 0, None
                    for k in range(nblk):
                        b = bl.blocks[k]
                        if b["fresh"]:
                            pe.wait_ge(m[f"w{b['w']}"], (it + 1) * 16)
                        pe.wait_ge(m["xb"], n0 + k + 1)
                        for mi in range(mt):
                            hidden(m, wbuf[b["w"]], mt, pair, mi, s, xb[k % 2][:, :, 0:b["nt"] * P], b["nt"] * P)
                            if mi == 0 and k + 1 < nblk:
                                turned(k + 1)
                            if prev is not None:
                                down(*prev)
                            prev = (k, mi, s)
                            s += 1
                    down(*prev)
                base = NB * MOE[l]["sh"]
                with pe.Fori(0, bl.turns) as it:
                    turn(it, it * bl.n, it * (bl.n * mt) + base, bl.n)
                if bl.rest:
                    turn(bl.turns, bl.turns * bl.n, bl.turns * bl.n * mt + base, bl.rest)

            def mix_pe(l):
                m = M[l]
                for b in range(NB):
                    if b >= 2:
                        pe.wait_ge(m["acc"], b - 1)
                    for t in range(TPB):
                        pe.wait_ge(m["mixed"], b * TPB + t + 1)
                        for k in range(KT):
                            last = nc.tensor.transpose(bank(2 * (b % 2) + k)[:, t * P:(t + 1) * P],
                                                       got[t % 2][0][:, k * P:(k + 1) * P], ident)
                        last.then_inc(m["mixt"], 1)

            pe.wait_ge(const_in, 16 * 8)
            pe.wait_ge(relw_in, 16 * 3)
            for b in range(2):
                ln_pe(LN_REL + 2 * b, lsrc)
                pe.wait_ge(silu_done, 2 * b + 1)
                for mt_ in range(KT):
                    for k in range(KT):
                        last = mm(bank(3 + mt_), w1sb[:, k * D + mt_ * P:k * D + (mt_ + 1) * P], lout[:, k, :],
                                  start=(k == 0), stop=(k == KT - 1))
                last.then_inc(w1_done, 1)
                ln_pe(LN_REL + 2 * b + 1, lsrc)
                pe.wait_ge(silu_done, 2 * b + 2)
                for k in range(KT):
                    last = mm(bank(5)[0:HEADS, :], w2sb[:, k * HEADS:(k + 1) * HEADS], lout[:, k, :],
                              start=(k == 0), stop=(k == KT - 1))
                last.then_inc(w2_done, 1)
            pe.wait_ge(nk_sq, 1)
            mm(bank(6)[:, 0:1], b64, kn1, start=True, stop=True).then_inc(nk_mm, 1)
            pe.wait_ge(nk_std, 1)
            pe.wait_ge(pool_init, 3)
            logits_pe(0, xT)
            ranks_pe(0, 0)
            shared_pe(0, xT)
            blocks_pe(0)
            mix_pe(0)
            pe.wait_ge(M[0]["acc"], NB)
            logits_pe(1, yT)
            rows_pe(1, yT)
            ranks_pe(1, 1)
            shared_pe(1, yT)
            blocks_pe(1)
            mix_pe(1)
            pe.wait_ge(M[1]["acc"], NB)
            pe.wait_ge(qkv_w_in, 48)
            for b in range(NB):
                ln_pe(LN_QKV + b, xT[:, :, b * BLK:(b + 1) * BLK])
                pe.wait_ge(ln_out, LN_QKV + b + 1)

                def n2_mm(c):
                    pe.wait_ge(q_sq, b * 9 + c + 1)
                    for t in range(TPB):
                        o = bank(5)[:, (t * 9 + c) * 2:(t * 9 + c) * 2 + 2]
                        last = mm(o, qsq[c % 2][:, t * P:(t + 1) * P], sel2, start=True, stop=True)
                    last.then_inc(q_n2 if c == 8 else q_sqfree, 1)
                for c in range(9):
                    n = b * 9 + c
                    if n >= 2:
                        pe.wait_ge(q_copied, n - 1)
                        pe.wait_ge(q_sq, n - 1)
                    if c == 8:
                        pe.wait_ge(lrev_done, b + 1)
                    for k in range(KT):
                        last = mm(bank(3 + c % 2), wqk[:, k, c * P:(c + 1) * P], (lrev if c == 8 else lout)[:, k, :],
                                  start=(k == 0), stop=(k == KT - 1))
                    last.then_inc(q_mm, 1)
                    if c >= 1:
                        n2_mm(c - 1)
                n2_mm(8)
                if b >= 1:
                    pe.wait_ge(v_done, b)
                for t in range(TPB):
                    for k in range(KT):
                        last = mm(bank(1)[:, t * DH:(t + 1) * DH], lrev[:, k, t * P:(t + 1) * P], wv[:, k, :],
                                  start=(k == 0), stop=(k == KT - 1))
                last.then_inc(v_mm, 1)
                pe.wait_ge(q_rn, b + 1)
                for t in range(TPB):
                    last = nc.tensor.transpose(bank(5)[0:18, t * P:(t + 1) * P], rns[:, t * 18:(t + 1) * 18], ident)
                last.then_inc(q_tr, 1)
                pe.wait_ge(q_rnT, b + 1)
                for c in range(9):
                    n = b * 9 + c
                    if n >= 2:
                        pe.wait_ge(q_norm, n - 1)
                    mm(bank(6 + n % 2), bsel[:, c * P:(c + 1) * P], rnT, start=True, stop=True).then_inc(q_rb, 1)
                pe.wait_ge(v_done, b + 1)
            pe.wait_ge(nk_done, 1)
            with pe.Fori(0, BATCH) as b:
                ub = b * UNITS

                def sims(u):
                    qt, hg = divmod(u, NHG)
                    nk = (qt + 1) * P
                    if hg == 0:
                        pe.wait_ge(q_in[qt % 2], (b * (NQ // 2) + qt // 2 + 1) * 16)
                    for c in range(2):
                        last = mm(bank(7)[:, 2 * c:2 * c + 2], qtile[qt % 2][:, hg * 2 + c, :], knull,
                                  start=True, stop=True)
                    last.then_inc(null_mm, 1)
                    for h in range(HG):
                        if u * HG + h >= 2:
                            pe.wait_ge(added, (ub + u) * HG + h - 1)
                        base = (h % 2) * 64
                        for f in range(0, nk, BLK):
                            w = min(BLK, nk - f)
                            last = mm(ps[:, (h % 2) * 2 * BLK + f:(h % 2) * 2 * BLK + f + w],
                                      qtile[qt % 2][base:base + 64, hg * 2 + h // 2, :], kcur[base:base + 64, SEQ - nk + f:SEQ - nk + f + w],
                                      start=True, stop=True)
                        last.then_inc(sim_done, 1)

                pe.wait_ge(kv_cur, b + 1)
                sims(0)
                for u in range(UNITS):
                    qt, hg = divmod(u, NHG)
                    n = 0
                    done = []
                    for h in range(HG):
                        pe.wait_ge(exp_done, (ub + u) * HG + h + 1)
                        for g, (k0, k1) in enumerate(groups(qt)):
                            if n >= 2:
                                ph, pg = done[n - 2]
                                pe.wait_ge(evac[ev_engine(u, ph, pg)], b * EV_B + ev_index(u, ph, pg) + 1)
                            for kt in range(k0, k1):
                                o = bank(4 + n % 2)[:, (kt - k0) * P:(kt - k0 + 1) * P]
                                last = nc.tensor.transpose(o, prob[h][:, kt * P:(kt + 1) * P], ident)
                            last.then_inc(tr_done, 1)
                            done.append((h, g))
                            n += 1
                    if u + 1 < UNITS:
                        sims(u + 1)
                    for e in range(2):
                        pe.wait_ge(evac[e], b * EV_B + EV[qt] + (hg + 1) * 2 * len(groups(qt)))
                    if u >= 1:
                        pe.wait_ge(o_copied, ub + u)
                    for kt in range(qt + 1):
                        mm(bank(6)[0:DH + 1, :], vcur[:, (NQ - 1 - qt + kt) * (DH + 1):(NQ - qt + kt) * (DH + 1)],
                           probT[:, kt, :, :].rearrange("p h q -> p (h q)"), start=(kt == 0), stop=False)
                    pe.wait_ge(diag_done, ub + u + 1)
                    mm(bank(6)[0:DH + 1, :], vnull, diag, start=False, stop=True).then_inc(av_done, 1)
            pe.wait_ge(wout_in, 16)
            for b in range(NB):
                pe.wait_ge(ab_scaled, b + 1)
                for k in range(KT):
                    for c in range(NCH):
                        last = mm(bank(3 + k), wout[:, c, k * P:(k + 1) * P], ablk[b % 2][:, c, :],
                                  start=(c == 0), stop=(c == NCH - 1))
                last.then_inc(proj_mm, 1)
                ln_pe(LN_PROJ + b, lsrc)
            pe.wait_ge(ln_out, LN_PROJ + NB)
            logits_pe(2, aT)
            rows_pe(2, aT)
            with pe.Fori(0, BITS) as i:
                pe.wait_ge(ge_ready, i + 1)
                mm(bank(7)[:, 0:P], ones_bf[:, :], cmpb[:, :], start=True, stop=True).then_inc(ge_count, 1)
            for i in range(3):
                pe.wait_ge(tie_ready, i + 1)
                mm(bank(7)[:, 0:P], ones_bf[:, :] if i < 2 else tri_bf[:, :], cmpb[:, :], start=True, stop=True)\
                    .then_inc(tie_count, 1)
            ranks_pe(2, 2)
            blocks_pe(2)
            mix_pe(2)

        @block.scalar
        def _(act):
            fn = nc.scalar.activation

            def ln_act(i):
                act.wait_ge(ln_xc, i + 1)
                fn(sq, xc, ACT.Square).then_inc(ln_sq, 1)
                act.wait_ge(ln_var, i + 1)
                fn(stdc, bank(1)[:, 0:TPB], ACT.Sqrt, bias=eps).then_inc(ln_std, 1)

            def rows_act(l):
                m = M[l]
                if l == 1:
                    act.wait_ge(score_done, 1)
                for t in range(NT):
                    act.wait_ge(m["rowt"], t // 2 + 1)
                    src = ps[:, (4 + t // 2 % 2) * BLK + (t % 2) * D:(4 + t // 2 % 2) * BLK + (t % 2) * D + D]
                    if l == 1:
                        ins = fn(rows[:, t, :], src, ACT.Copy, scale=wts[:, t:t + 1])
                    else:
                        ins = fn(rows[:, t, :], src, ACT.Copy)
                    ins.then_inc(m["rows"], 1)

            def moe_act(l):
                m, bl, mt, sh, pair = M[l], BL[l], MOE[l]["mt"], MOE[l]["sh"], MOE[l]["pair"]
                f = (ACT.Copy, ACT.Silu, ACT.Relu)[l]

                def steps(s0, sizes):
                    for s, n in enumerate(sizes):
                        act.wait_ge(m["gu"], s0 + s + 1)
                        if pair:
                            if s >= 2:
                                act.wait_ge(m["h"], s0 + s - 1)
                            fn(gs[s % 2][:, 0:n], bank(s % 2, n), f).then_inc(m["act"], 1)
                        else:
                            if s >= 2:
                                act.wait_ge(m["down"], s0 + s - 1)
                            fn(hb[s % 2][:, 0:n], bank(s % 2, n), f).then_inc(m["h"], 1)
                sizes = [b["nt"] * P for b in bl.blocks for _ in range(mt)]
                if sh:
                    steps(0, [BLK] * (NB * sh))
                with act.Fori(0, bl.turns) as it:
                    steps(it * len(sizes) + NB * sh, sizes)
                if bl.rest:
                    steps(bl.turns * len(sizes) + NB * sh, sizes[:bl.rest * mt])

            act.wait_ge(const_in, 16 * 8)
            for b in range(2):
                for i in range(2):
                    ln_act(LN_REL + 2 * b + i)
                    act.wait_ge(ln_out, LN_REL + 2 * b + i + 1)
                    fn(lout, lout, ACT.Silu).then_inc(silu_done, 1)
            act.wait_ge(nk_mm, 1)
            fn(kn2, bank(6)[:, 0:1], ACT.Sqrt).then_inc(nk_std, 1)

            def top_act(l):
                act.wait_ge(top_diff, l + 1)
                if l == 0:
                    fn(W2c, Zc, ACT.Exp).then_inc(top_exp, 1)
                elif l == 1:
                    fn(W2c, Zc, ACT.Exp, scale=-1.0).then_inc(top_exp, 1)
                else:
                    fn(R4, R4, ACT.Exp).then_inc(top_exp, 1)
            top_act(0)
            moe_act(0)
            top_act(1)
            rows_act(1)
            moe_act(1)
            for b in range(NB):
                ln_act(LN_QKV + b)
                for c in range(9):
                    n = b * 9 + c
                    act.wait_ge(q_mm, n + 1)
                    if b >= 1:
                        act.wait_ge(q_norm, n - 9 + 1)
                    fn(qraw[:, c, :], bank(3 + c % 2), ACT.Copy).then_inc(q_copied, 1)
                    if c >= 2:
                        act.wait_ge(q_sqfree, b * 8 + c - 1)
                    fn(qsq[c % 2], bank(3 + c % 2), ACT.Square).then_inc(q_sq, 1)
                act.wait_ge(q_n2, b + 1)
                fn(n2s, bank(5)[:, 0:72], ACT.Sqrt).then_inc(q_std, 1)
                act.wait_ge(q_tr, b + 1)
                fn(rnT, bank(5)[0:18, :], ACT.Copy).then_inc(q_rnT, 1)
            with act.Fori(0, BATCH) as b:
                ub = b * UNITS

                def exps(u):
                    qt, hg = divmod(u, NHG)
                    for h in range(HG):
                        act.wait_ge(added, (ub + u) * HG + h + 1)
                        fn(prob[h][:, 0:(qt + 1) * P], prob[h][:, 0:(qt + 1) * P], ACT.Exp,
                           bias=negm[:, (u % 2) * 4 + h:(u % 2) * 4 + h + 1]).then_inc(exp_done, 1)
                    act.wait_ge(dn_done, ub + u + 1)
                    if u >= 2:
                        act.wait_ge(diag_done, ub + u - 1)
                    fn(pn[:, (u % 2) * 4:(u % 2) * 4 + 4], dn, ACT.Exp).then_inc(pn_done, 1)
                exps(0)
                for u in range(UNITS):
                    qt, hg = divmod(u, NHG)
                    for h in range(HG):
                        for g, (k0, k1) in enumerate(groups(qt)):
                            if ev_engine(u, h, g) != 0:
                                continue
                            act.wait_ge(tr_done, b * TR_B + tr_index(u, h, g) + 1)
                            n = (h * len(groups(qt)) + g) % 2
                            fn(probT[:, k0:k1, h, :], bank(4 + n)[:, 0:(k1 - k0) * P]
                               .rearrange("p (k q) -> p k q", q=P), ACT.Copy).then_inc(evac[0], 1)
                    if u + 1 < UNITS:
                        exps(u + 1)
            for b in range(NB):
                act.wait_ge(proj_mm, b + 1)
                for k in range(KT):
                    last = fn(lsrc[:, k, :], bank(3 + k), ACT.Copy)
                last.then_inc(ln_src, 1)
                ln_act(LN_PROJ + b)
            top_act(2)
            rows_act(2)
            moe_act(2)

        @block.gpsimd
        def _(pool):
            nc.gpsimd.memset(zrow, 0.0).then_inc(pool_init, 1)
            nc.gpsimd.memset(ones_bf[:, :], 1.0).then_inc(pool_init, 1)
            pool.wait_ge(const_in, 16 * 8)
            nc.gpsimd.tensor_copy(tri_bf[:, :], cst[:, C_TRI:C_TRI + P]).then_inc(pool_init, 1)

            def put_rows(l):
                m = M[l]
                pool.wait_ge(m["slots"], 1)
                pool.wait_ge(zeroed, 48)
                if l == 0:
                    pool.wait_ge(rows_in, 16)
                for t in range(NT):
                    if l:
                        pool.wait_ge(m["rows"], t + 1)
                    for c in range(MOE[l]["top"]):
                        nc.gpsimd.indirect_dma_start(
                            out=xs_d[l][:, :], out_offset=bass.IndirectOffsetOnAxis(ap=put_i[:, c * NT + t:c * NT + t + 1], axis=0),
                            in_=rows[:, t, :], in_offset=None).then_inc(m["put"], 16)

            def get_rows(l):
                m, n = M[l], BL[l].total
                pool.wait_ge(m["out0"], 16 * ((n + 1) // 2 + 1))
                pool.wait_ge(m["out1"], 16 * (n // 2 + 1))
                for t in range(NT):
                    if t >= 2:
                        pool.wait_ge(m["mixt"], t - 1)
                    for c in range(MOE[l]["top"]):
                        nc.gpsimd.indirect_dma_start(
                            out=got[t % 2][c], out_offset=None, in_=ys_d[l][:, :],
                            in_offset=bass.IndirectOffsetOnAxis(ap=get_i[:, c * NT + t:c * NT + t + 1], axis=0))\
                            .then_inc(m[f"get{t % 2}"], 16)

            for l in range(2):
                put_rows(l)
                get_rows(l)
            for b in range(NB):
                pool.wait_ge(ln_out, LN_QKV + b + 1)
                if b:
                    pool.wait_ge(v_mm, b)
                nc.gpsimd.tensor_copy(lrev, lout[:, :, ::-1]).then_inc(lrev_done, 1)
            with pool.Fori(0, BATCH) as b:
                for u in range(UNITS):
                    pool.wait_ge(pn_done, b * UNITS + u + 1)
                    pool.wait_ge(av_done, b * UNITS + u) if u else None
                    nc.gpsimd.tensor_tensor(
                        diag.rearrange("p (h q) -> p h q", h=HG),
                        ident.unsqueeze(1).broadcast_to((P, HG, P)),
                        pn[:, (u % 2) * 4:(u % 2) * 4 + 4].unsqueeze(2).broadcast_to((P, HG, P)),
                        ALU.mult).then_inc(diag_done, 1)
            put_rows(2)
            get_rows(2)

        @block.vector
        def _(dve):
            v = nc.vector
            chain = [0]

            def link(ins):
                chain[0] += 1
                ins.then_inc(dchain, 1)
                dve.wait_ge(dchain, chain[0])

            def ln_dve(i, src, dst, g):
                dve.wait_ge(ln_mean, i + 1)
                v.tensor_tensor(xc, src, bank(0).unsqueeze(1).broadcast_to((P, KT, BLK)), ALU.subtract)\
                    .then_inc(ln_xc, 1)
                dve.wait_ge(ln_std, i + 1)
                v.reciprocal(rstd, stdc).then_inc(ln_rstd, 1)
                dve.wait_ge(ln_bc, i + 1)
                for k in range(KT):
                    last = v.scalar_tensor_tensor(out=dst[:, k, :], in0=xc[:, k, :], scalar=pr(g, k), in1=bank(2),
                                                  op0=ALU.mult, op1=ALU.mult)
                last.then_inc(ln_out, 1)

            dve.wait_ge(const_in, 16 * 8)
            dve.wait_ge(relw_in, 16 * 3)
            for b in range(2):
                if b:
                    dve.wait_ge(w2_done, b)
                for k in range(KT):
                    last = v.tensor_scalar(lsrc[:, k, :], posr[:, b * BLK:(b + 1) * BLK], pr("w0", k), pr("b0", k),
                                           ALU.mult, ALU.add)
                last.then_inc(ln_src, 1)
                ln_dve(LN_REL + 2 * b, lsrc, lout, "g0")
                dve.wait_ge(w1_done, b + 1)
                for k in range(KT):
                    last = v.tensor_scalar(lsrc[:, k, :], bank(3 + k), pr("b1", k), None, ALU.add)
                last.then_inc(ln_src, 1)
                ln_dve(LN_REL + 2 * b + 1, lsrc, lout, "g1")
                dve.wait_ge(w2_done, b + 1)
                v.tensor_scalar(lrow[:, P - 1 + b * BLK:P - 1 + (b + 1) * BLK], bank(5)[0:HEADS, :], par[0:HEADS, PAR["b2"][0]:PAR["b2"][1]],
                                None, ALU.add).then_inc(rows_done, 1)
            v.memset(lrow[:, 0:P - 1], NEG).then_inc(rows_done, 1)
            v.tensor_tensor(kn1, pr("nk"), pr("nk"), ALU.mult).then_inc(nk_sq, 1)
            link(v.tensor_scalar(qs8, pr("qs"), 8.0, None, ALU.mult))
            link(v.tensor_copy(maskf, mask8[:, :]))
            dve.wait_ge(nk_std, 1)
            link(v.tensor_scalar(kn2, kn2, 1e-12, None, ALU.max))
            link(v.reciprocal(kn2, kn2))
            link(v.tensor_tensor(kn2, kn2, pr("nk"), ALU.mult))
            link(v.tensor_tensor(kn2, kn2, pr("ks"), ALU.mult))
            v.tensor_scalar(knull, sel2, kn2, None, ALU.mult).then_inc(nk_done, 1)
            link(v.tensor_copy(vnull[:, 0:DH], pr("nv")))
            v.memset(vnull[:, DH:DH + 1], 1.0).then_inc(nk_done, 1)

            L3 = L.rearrange("p (t e) -> p t e", e=E)

            def t3(x):
                return x.rearrange("p (t e) -> p t e", e=E)

            def bt(x):
                return x.unsqueeze(2).broadcast_to((P, NT, E))

            def be(x):
                return x.unsqueeze(1).broadcast_to((P, NT, E))

            def pick(src, mval, onehot, tmp):
                link(v.tensor_reduce(mval, t3(src), AX, ALU.max))
                link(v.tensor_tensor(t3(tmp), t3(src), bt(mval), ALU.is_equal))
                link(v.tensor_tensor(t3(tmp), t3(tmp), be(wdesc), ALU.mult))
                link(v.tensor_reduce(W1c, t3(tmp), AX, ALU.max))
                link(v.tensor_tensor(t3(onehot), t3(tmp), bt(W1c), ALU.is_equal))

            def second(first, tmp):
                link(v.scalar_tensor_tensor(out=tmp, in0=first, scalar=NEG, in1=L, op0=ALU.mult, op1=ALU.add))

            def route(l):
                dve.wait_ge(logits_done, l + 1)
                link(v.tensor_scalar(L, bank(7)[:, 0:P], 0.5 if l == 0 else 1.0, None, ALU.mult))
                pick(L, M1, R1, R4)
                if l != 1:
                    second(R1, R3)
                    pick(R3, M2, R2, R4)
                g1, g2 = wts[:, 0:NT], wts[:, NT:2 * NT]
                if l == 0:
                    v.tensor_tensor(Zc, M2, M1, ALU.subtract).then_inc(top_diff, 1)
                    dve.wait_ge(top_exp, 1)
                    link(v.tensor_scalar(W1c, W2c, 1.0, None, ALU.add))
                    link(v.reciprocal(g1, W1c))
                    link(v.tensor_tensor(g2, W2c, g1, ALU.mult))
                    slots(l)
                elif l == 1:
                    v.tensor_copy(Zc, M1).then_inc(top_diff, 1)
                    dve.wait_ge(top_exp, 2)
                    link(v.tensor_scalar(W1c, W2c, 1.0, None, ALU.add))
                    v.reciprocal(g1, W1c).then_inc(score_done, 1)
                    slots(l)
                else:
                    v.tensor_tensor(t3(R4), L3, bt(M1), ALU.subtract).then_inc(top_diff, 1)
                    link(v.tensor_tensor(R3, R1, R2, ALU.add))
                    dve.wait_ge(top_exp, 3)
                    link(v.tensor_reduce(W1c, t3(R4), AX, ALU.add))
                    link(v.reciprocal(W1c, W1c))
                    link(v.tensor_tensor(t3(R4), t3(R4), bt(W1c), ALU.mult))
                    link(v.tensor_tensor(G, R4, R3, ALU.mult))
                    link(v.memset(thr.bitcast(I32), 0))
                    with dve.Fori(0, BITS) as i:
                        def bl(n, ins):
                            ins.then_inc(cap_chain, 1)
                            dve.wait_ge(cap_chain, i * 5 + n)
                        bl(1, v.tensor_tensor(cand.bitcast(I32), thr.bitcast(I32),
                                              bits[:, bass.ds(i, 1)].broadcast_to((P, E)), ALU.bitwise_or))
                        v.tensor_tensor(t3(cmpb[:, :]), t3(G), be(cand), ALU.is_ge).then_inc(ge_ready, 1)
                        dve.wait_ge(ge_count, i + 1)
                        bl(2, v.tensor_reduce(cnt, bank(7)[:, 0:P].rearrange("p (t e) -> p e t", e=E), AX, ALU.add))
                        bl(3, v.tensor_scalar(take, cnt, CAP - 0.5, None, ALU.is_ge))
                        bl(4, v.tensor_tensor(cand, cand, take, ALU.mult))
                        bl(5, v.tensor_tensor(thr, thr, cand, ALU.max))
                    link(v.tensor_tensor(t3(KP), t3(G), be(thr), ALU.is_gt))
                    v.tensor_copy(cmpb[:, :], KP).then_inc(tie_ready, 1)
                    dve.wait_ge(tie_count, 1)
                    link(v.tensor_reduce(cnt, bank(7)[:, 0:P].rearrange("p (t e) -> p e t", e=E), AX, ALU.add))
                    link(v.tensor_scalar(cnt, cnt, -1.0, float(CAP), ALU.mult, ALU.add))
                    link(v.tensor_tensor(t3(TI), t3(G), be(thr), ALU.is_equal))
                    link(v.tensor_tensor(TI, TI, R3, ALU.mult))
                    v.tensor_copy(cmpb[:, :], TI).then_inc(tie_ready, 1)
                    dve.wait_ge(tie_count, 2)
                    link(v.tensor_copy(R4, bank(7)[:, 0:P]))
                    v.tensor_copy(cmpb[:, :], TI).then_inc(tie_ready, 1)
                    dve.wait_ge(tie_count, 3)
                    link(v.tensor_copy(L, bank(7)[:, 0:P]))
                    before()
                    link(v.tensor_tensor(t3(L), t3(L), be(cnt), ALU.is_lt))
                    link(v.tensor_tensor(TI, TI, L, ALU.mult))
                    link(v.tensor_tensor(KP, KP, TI, ALU.add))
                    link(v.tensor_tensor(KP, KP, R3, ALU.mult))
                    for c, r in ((0, R1), (1, R2)):
                        w, kf = wts[:, c * NT:(c + 1) * NT], keptf[:, c * NT:(c + 1) * NT]
                        link(v.tensor_tensor(R4, r, KP, ALU.mult))
                        link(v.tensor_reduce(kf, t3(R4), AX, ALU.add))
                        link(v.tensor_tensor(R4, R4, G, ALU.mult))
                        link(v.tensor_reduce(w, t3(R4), AX, ALU.add))
                    slots(l)

            def before():
                for t in range(1, NT):
                    link(v.tensor_tensor(R4[:, t * E:(t + 1) * E], R4[:, t * E:(t + 1) * E],
                                         R4[:, (t - 1) * E:t * E], ALU.add))
                link(v.tensor_tensor(L[:, E:], L[:, E:], R4[:, 0:(NT - 1) * E], ALU.add))

            def slots(l):
                if l == 1:
                    v.tensor_copy(cmpb[:, :], R1).then_inc(rank_ready, 1)
                elif l == 0:
                    v.tensor_tensor(cmpb[:, :], R1, R2, ALU.add).then_inc(rank_ready, 1)
                else:
                    v.tensor_copy(cmpb[:, :], KP).then_inc(rank_ready, 1)
                dve.wait_ge(rank_count, 2 * l + 1)
                v.tensor_copy(R4, bank(7)[:, 0:P]).then_inc(rank_ready, 1)
                dve.wait_ge(rank_count, 2 * l + 2)
                link(v.tensor_copy(L, bank(7)[:, 0:P]))
                before()
                if l < 2:
                    link(v.tensor_tensor(jcmp.rearrange("p (e j) -> p e j", j=8),
                                         R4[:, (NT - 1) * E:].unsqueeze(2).broadcast_to((P, E, 8)),
                                         cst[:, C_JT:C_JT + 8].unsqueeze(1).broadcast_to((P, E, 8)), ALU.is_gt))
                    link(v.tensor_reduce(nblk, jcmp.rearrange("p (e j) -> p e j", j=8), AX, ALU.add))
                    link(v.tensor_copy(eblk, nblk))
                    for e in range(1, E):
                        link(v.tensor_tensor(eblk[:, e:e + 1], eblk[:, e:e + 1], eblk[:, e - 1:e], ALU.add))
                    link(v.tensor_tensor(ebase, eblk, nblk, ALU.subtract))
                    link(v.tensor_scalar(ebase, ebase, float(SB), None, ALU.mult))
                    k3 = kcmp.rearrange("p (k e) -> p k e", e=E)
                    link(v.tensor_tensor(k3, eblk.unsqueeze(1).broadcast_to((P, NTAB, E)),
                                         cst[:, C_KT:C_KT + NTAB].unsqueeze(2).broadcast_to((P, NTAB, E)), ALU.is_le))
                    link(v.tensor_reduce(tabf[:, 0:NTAB], k3, AX, ALU.add))
                    link(v.tensor_scalar(tabf[:, 0:NTAB], tabf[:, 0:NTAB], float(E - 1), None, ALU.min))
                    if l:
                        dve.wait_ge(M[0]["out0"], 16 * ((BL[0].total + 1) // 2 + 1))
                    link(v.tensor_copy(btab[:, :], tabf[:, 0:NTAB]))
                    link(v.tensor_tensor(t3(L), t3(L), be(ebase), ALU.add))
                else:
                    link(v.tensor_scalar(L, L, CAP - 1.0, None, ALU.min))
                    link(v.tensor_tensor(t3(L), t3(L), be(cst[:, C_EB:C_EB + E]), ALU.add))
                for c, r in ((0, R1), (1, R2))[:MOE[l]["top"]]:
                    link(v.tensor_tensor(r, r, L, ALU.mult))
                    link(v.tensor_reduce(slotf[:, c * NT:(c + 1) * NT], t3(r), AX, ALU.add))
                n = MOE[l]["top"] * NT
                link(v.tensor_copy(get_i[:, 0:n], slotf[:, 0:n]))
                if l == 2:
                    tr = cst[:, C_TR:C_TR + 2 * NT]
                    link(v.tensor_tensor(slotf, slotf, tr, ALU.subtract))
                    link(v.tensor_tensor(slotf, slotf, keptf, ALU.mult))
                    link(v.tensor_tensor(slotf, slotf, tr, ALU.add))
                v.tensor_copy(put_i[:, 0:n], slotf[:, 0:n]).then_inc(M[l]["slots"], 1)

            def shared_dve(l, acc):
                m, sh = M[l], MOE[l]["sh"]

                def add(n):
                    dve.wait_ge(m["down"], (n + 1) * sh)
                    a = acc[:, :, n * BLK:(n + 1) * BLK]
                    y = ps[:, 4 * BLK:6 * BLK].rearrange("p (k t) -> p k t", k=KT)
                    if l == 0:
                        v.tensor_copy(a, y).then_inc(m["yacc"], 1)
                    else:
                        v.tensor_tensor(a, a, y, ALU.add).then_inc(m["yacc"], 1)
                s = 0
                for n in range(NB):
                    for mi in range(sh):
                        multiply(l, s, 0, BLK)
                        if mi == 0 and n:
                            add(n - 1)
                        s += 1
                add(NB - 1)

            def multiply(l, s, s0, n):
                m = M[l]
                dve.wait_ge(m["act"], s0 + s + 1)
                if s >= 2:
                    dve.wait_ge(m["down"], s0 + s - 1)
                g = gs[s % 2][:, 0:n]
                if l == 0:
                    v.scalar_tensor_tensor(out=g, in0=g, scalar=0.01, in1=g, op0=ALU.mult, op1=ALU.max)\
                        .then_inc(m["leaky"], 1)
                    dve.wait_ge(m["leaky"], s0 + s + 1)
                v.tensor_tensor(hb[s % 2][:, 0:n], g, bank(2 + s % 2, n), ALU.mult).then_inc(m["h"], 1)

            def blocks_dve(l):
                m, bl, mt, pair = M[l], BL[l], MOE[l]["mt"], MOE[l]["pair"]

                def turn(it, n0, s0, nblk):
                    def take_in(k):
                        n = bl.blocks[k]["nt"] * P
                        dve.wait_ge(m["bt"], n0 + k + 1)
                        if k >= 2:
                            dve.wait_ge(m["gu"], s0 + (k - 1) * mt)
                        v.tensor_copy(xb[k % 2][:, :, 0:n], ps[:, 6 * BLK:8 * BLK]
                                      .rearrange("p (k t) -> p k t", k=KT)[:, :, 0:n]).then_inc(m["xb"], 1)

                    def give_out(k):
                        dve.wait_ge(m["down"], s0 + (k + 1) * mt)
                        o = k % 2
                        dve.wait_ge(m[f"out{o}"], (it * (bl.n // 2) + k // 2 + 1) * 16)
                        if bl.blocks[k]["nt"] == 3:
                            v.tensor_copy(yrow[o][:, 2, :], bank(2, D))
                        v.tensor_copy(yrow[o][:, 0:2, :], ps[:, 4 * BLK:6 * BLK]
                                      .rearrange("p (t d) -> p t d", t=2)[:, :, 0:D]).then_inc(m["yrow"], 1)

                    take_in(0)
                    s = 0
                    for k in range(nblk):
                        for mi in range(mt):
                            if pair:
                                multiply(l, s, s0, bl.blocks[k]["nt"] * P)
                            if mi == 0:
                                if k:
                                    give_out(k - 1)
                                if k + 1 < nblk:
                                    take_in(k + 1)
                            s += 1
                    give_out(nblk - 1)
                base = NB * MOE[l]["sh"]
                with dve.Fori(0, bl.turns) as it:
                    turn(it, it * bl.n, it * (bl.n * mt) + base, bl.n)
                if bl.rest:
                    turn(bl.turns, bl.turns * bl.n, bl.turns * bl.n * mt + base, bl.rest)

            def mix_dve(l, acc):
                m, top = M[l], MOE[l]["top"]

                def add(b):
                    dve.wait_ge(m["mixt"], (b + 1) * TPB)
                    a = acc[:, :, b * BLK:(b + 1) * BLK]
                    v.tensor_tensor(a, a, ps[:, 2 * (b % 2) * BLK:(2 * (b % 2) + 2) * BLK]
                                    .rearrange("p (k t) -> p k t", k=KT), ALU.add).then_inc(m["acc"], 1)
                for t in range(NT):
                    g = got[t % 2]
                    dve.wait_ge(m[f"get{t % 2}"], 16 * top * (t // 2 + 1))
                    if top == 1:
                        dve.sem_inc(m["mixed"], 1)
                    else:
                        link(v.tensor_scalar(g[0], g[0], wts[:, t:t + 1], None, ALU.mult))
                        v.scalar_tensor_tensor(out=g[0], in0=g[1], scalar=wts[:, NT + t:NT + t + 1], in1=g[0],
                                               op0=ALU.mult, op1=ALU.add).then_inc(m["mixed"], 1)
                    if t % TPB == 1 and t > TPB:
                        add(t // TPB - 1)
                add(NB - 1)
                dve.wait_ge(m["acc"], NB)

            route(0)
            shared_dve(0, yT)
            blocks_dve(0)
            mix_dve(0, yT)
            route(1)
            shared_dve(1, xT)
            blocks_dve(1)
            mix_dve(1, xT)
            for b in range(NB):
                if b:
                    dve.wait_ge(v_mm, b)
                dve.sem_inc(ln_src, 1)
                ln_dve(LN_QKV + b, xT[:, :, b * BLK:(b + 1) * BLK], lout, "gn")
                dve.wait_ge(q_std, b + 1)
                link(v.tensor_scalar(n2s, n2s, 1e-12, None, ALU.max))
                v.reciprocal(rns, n2s).then_inc(q_rn, 1)
                dve.wait_ge(v_mm, b + 1)
                for t in range(TPB):
                    tt = (b ^ 1) * TPB + t
                    o = vall[:, tt * (DH + 1):(tt + 1) * (DH + 1)]
                    v.tensor_scalar(o[:, 0:DH], bank(1)[:, t * DH:(t + 1) * DH], maskf[:, tt:tt + 1], None, ALU.mult)
                    last = v.tensor_copy(o[:, DH:DH + 1], maskf[:, tt:tt + 1])
                last.then_inc(v_done, 1)
                for c in range(9):
                    n = b * 9 + c
                    dve.wait_ge(q_rb, n + 1)
                    if c < NCH:
                        dst = qout[c % 2]
                        w = b * (NCH // 2) + c // 2
                        if w:
                            dve.wait_ge(q_out[c % 2], 16 * w)
                    else:
                        dst = kall[:, (b ^ 1) * BLK:((b ^ 1) + 1) * BLK]
                    v.scalar_tensor_tensor(out=dst, in0=qraw[:, c, :], scalar=(qs8 if c < NCH else pr("ks")),
                                           in1=bank(6 + n % 2), op0=ALU.mult, op1=ALU.mult).then_inc(q_norm, 1)
            dve.wait_ge(v_done, NB)
            dve.wait_ge(q_norm, NB * 9)
            with dve.Fori(0, BATCH) as b:
                ub = b * UNITS
                at_c = [0]

                def tick(ins):
                    at_c[0] += 1
                    ins.then_inc(att_chain, 1)

                def adds(u):
                    qt, hg = divmod(u, NHG)
                    nk = (qt + 1) * P
                    o4 = (u % 2) * 4
                    dve.wait_ge(null_mm, ub + u + 1)
                    dve.wait_ge(sim_done, (ub + u) * HG + 1)
                    tick(v.tensor_tensor(sn, bank(7)[:, 0:HG], pr("nab")[:, hg * HG:(hg + 1) * HG], ALU.add))
                    for h in range(HG):
                        off = (hg * HG + h) * SEQ
                        tick(v.tensor_tensor_reduce(out=prob[h][:, 0:nk], in0=ps[:, (h % 2) * 2 * BLK:(h % 2) * 2 * BLK + nk],
                                                    in1=TA[:, off:off + nk], scale=1.0, scalar=-3.0e38,
                                                    op0=ALU.add, op1=ALU.max, accum_out=mx[:, o4 + h:o4 + h + 1]))
                        dve.wait_ge(att_chain, b * ATT_LINKS + at_c[0])
                        if h + 1 < HG:
                            dve.wait_ge(sim_done, (ub + u) * HG + h + 2)
                        v.tensor_scalar(negm[:, o4 + h:o4 + h + 1], mx[:, o4 + h:o4 + h + 1], sn[:, h:h + 1], -1.0,
                                        ALU.max, ALU.mult).then_inc(added, 1)
                    dve.wait_ge(added, (ub + u + 1) * HG)
                    if u:
                        dve.wait_ge(pn_done, ub + u)
                    v.tensor_tensor(dn, sn, negm[:, o4:o4 + 4], ALU.add).then_inc(dn_done, 1)

                v.tensor_copy(kcur[:, :], kall[:, bass.ds(b * SEQ, SEQ)])
                v.tensor_copy(vcur[:, :], vall[:, bass.ds(b * (NQ * (DH + 1)), NQ * (DH + 1))]).then_inc(kv_cur, 1)
                adds(0)
                for u in range(UNITS):
                    qt, hg = divmod(u, NHG)
                    for h in range(HG):
                        for g, (k0, k1) in enumerate(groups(qt)):
                            if ev_engine(u, h, g) != 1:
                                continue
                            dve.wait_ge(tr_done, b * TR_B + tr_index(u, h, g) + 1)
                            n = (h * len(groups(qt)) + g) % 2
                            v.tensor_copy(probT[:, k0:k1, h, :], bank(4 + n)[:, 0:(k1 - k0) * P]
                                          .rearrange("p (k q) -> p k q", q=P)).then_inc(evac[1], 1)
                    if u + 1 < UNITS:
                        adds(u + 1)
                    dve.wait_ge(av_done, ub + u + 1)
                    if u >= 2:
                        dve.wait_ge(o_out[u % 2], b * (UNITS * 16) + (u // 2) * 32)
                    elif u == 0:
                        dve.wait_ge(batch_stored, b + 1)
                    src = bank(6).rearrange("p (c a q) -> p c a q", c=2, a=2)
                    for a in range(2):
                        v.tensor_copy(obuf[u % 2][a * 64:a * 64 + 64, :, :], src[0:DH, :, a, :])
                    v.tensor_copy(dbuf[u % 2][DH:DH + 1, :], bank(6)[DH:DH + 1, :]).then_inc(o_copied, 1)
                assert at_c[0] == ATT_LINKS
            dve.wait_ge(den_in, 16)
            v.reciprocal(rcmp, dcmp).then_inc(rden_done, 1)
            for b in range(NB):
                dve.wait_ge(ab_in[b % 2], 16 * 5 * (b // 2 + 1))
                for j in range(2):
                    a = ablk[b % 2][:, 4 * j:4 * j + 4, :]
                    last = v.tensor_tensor(a, a, rden[j], ALU.mult)
                last.then_inc(ab_scaled, 1)
                ln_dve(LN_PROJ + b, lsrc, aT[:, :, b * BLK:(b + 1) * BLK], "go")
            route(2)
            blocks_dve(2)
            mix_dve(2, xT)


_OUT = ("out_dram", (P, KT, TOK))


def kernel(**inp):
    import numpy as _np
    import concourse.bacc as _bacc
    from concourse import mybir as _mybir
    from concourse.bass_utils import run_bass_kernel_spmd as _run
    c = _np.ascontiguousarray
    g = {k: _np.asarray(a) for k, a in inp.items()}

    def feat(a):
        return a.reshape(KT, P, -1).transpose(1, 0, 2)

    def flat(a):
        return a.reshape(P, -1)

    def expert(gate, up, down):
        parts = [flat(feat(gate))] + ([flat(feat(up))] if up is not None else [])
        parts.append(flat(down.reshape(-1, P, D).transpose(1, 0, 2)))
        return _np.concatenate(parts, axis=1)

    def col(a):
        return a.reshape(KT, P).T

    def rep(a):
        return _np.broadcast_to(a.reshape(1, -1), (P, a.size))

    def dup(a):
        return _np.concatenate([a, a]).reshape(P, 1)

    arr = {}
    arr["xT"] = c(feat(g["x"].reshape(TOK, D).T))
    cst = _np.zeros((P, C_END), _np.float32)
    cst[:, C_ID:C_ID + P] = _np.eye(P)
    cst[:, C_MEAN:C_MEAN + P] = 1.0 / D
    cst[:64, C_B64:C_B64 + 64] = 1.0
    cst[64:, C_B64 + 64:C_B64 + P] = 1.0
    cst[:, C_TRI:C_TRI + P] = _np.triu(_np.ones((P, P)), 1)
    cst[:64, C_SEL] = 1.0
    cst[64:, C_SEL + 1] = 1.0
    cst[:, C_WD:C_WD + E] = E - _np.arange(E)
    cst[:, C_EPS] = 1e-5
    cst[:, C_JT:C_JT + 8] = SB * _np.arange(8)
    cst[:, C_KT:C_KT + NTAB] = _np.arange(NTAB)
    cst[:, C_EB:C_EB + E] = CAP * _np.arange(E)
    cst[:, C_TR:C_TR + 2 * NT] = (E * CAP + P * _np.arange(2 * NT))[None, :] + _np.arange(P)[:, None]
    arr["cst"] = cst
    b2 = _np.zeros((P, 1), _np.float32)
    b2[:HEADS, 0] = g["L1_cond_b2"]
    cond = g["cond_64"]
    pieces = dict(w0=col(g["L1_cond_w0"][0]), b0=col(g["L1_cond_b0"]), g0=col(g["L1_cond_g0"]),
                  b1=col(g["L1_cond_b1"]), g1=col(g["L1_cond_g1"]), gn=col(g["L1_cond_g_norm"]),
                  go=col(g["L1_cond_g_out"]), qs=dup(g["L1_cond_q_scale"]), ks=dup(g["L1_cond_k_scale"]),
                  nk=dup(cond[0]), nab=rep(g["L1_cond_null_attn_bias"]), nv=rep(cond[1]), b2=b2)
    arr["par"] = c(_np.concatenate([pieces[n] for n in PAR], axis=1))
    arr["wrt"] = c(_np.concatenate([flat(feat(g["L0_cond_wt"].T)), flat(feat(g["L0_ffn_router_w"].T)),
                                    flat(feat(g["L1_ffn_Wr"]))], axis=1))
    arr["xrows"] = c(g["x"].reshape(NT, P, D).transpose(1, 0, 2))
    arr["wg"] = c(g["L0_cond_wg"].T)
    arr["condT"] = c(cond.T)
    arr["mask"] = c(g["mask_BxS_bf1"][:, ::-1].reshape(NT, P).T).view(_np.uint8)
    arr["bits"] = c(_np.broadcast_to((1 << _np.arange(BITS - 1, -1, -1)).astype(_np.int32), (P, BITS)))
    arr["posr"] = c(_np.broadcast_to(_np.arange(SEQ).astype(_np.float32), (P, SEQ)))
    arr["w1"] = c(flat(feat(g["L1_cond_w1"])))
    arr["w2"] = c(flat(feat(g["L1_cond_w2"])))
    arr["wexp0"] = c(_np.stack([expert(g["L0_cond_w_gate"][e], g["L0_cond_w_up"][e], g["L0_cond_w_down"][e]) for e in range(E)]))
    arr["wsh0"] = c(expert(g["L0_cond_sw_gate"], g["L0_cond_sw_up"], g["L0_cond_sw_down"]))
    arr["wexp1"] = c(_np.stack([expert(g["L0_ffn_expert_gate"][e], g["L0_ffn_expert_up"][e], g["L0_ffn_expert_down"][e]) for e in range(E)]))
    arr["wsh1"] = c(expert(g["L0_ffn_shared_gate"], g["L0_ffn_shared_up"], g["L0_ffn_shared_down"]))
    arr["wexp2"] = c(_np.stack([expert(g["L1_ffn_W1"][e], None, g["L1_ffn_W2"][e]) for e in range(E)]))
    wkv = g["L1_cond_Wkv"]
    arr["wqk"] = c(feat(_np.concatenate([g["L1_cond_Wq"], wkv[:, :DH], wkv[:, :DH]], axis=1)))
    arr["wv"] = c(feat(wkv[:, DH:]))
    bsel = _np.zeros((18, 9 * P), _np.float32)
    for c_ in range(9):
        bsel[2 * c_, c_ * P:c_ * P + 64] = 1.0
        bsel[2 * c_ + 1, c_ * P + 64:(c_ + 1) * P] = 1.0
    arr["bsel"] = bsel
    arr["wout"] = c(g["L1_cond_Wout"].reshape(NCH, P, D).transpose(1, 0, 2))

    nc = _bacc.Bacc("TRN2", target_bir_lowering=False, num_devices=1)
    A = {n: nc.dram_tensor(f"{n}_dram", a.shape, _mybir.dt.from_np(a.dtype), kind="ExternalInput").ap()
         for n, a in arr.items()}
    A["out"] = nc.dram_tensor(_OUT[0], _OUT[1], _mybir.dt.float32, kind="ExternalOutput").ap()
    build(nc, A)
    r = _run(nc, [{f"{n}_dram": a for n, a in arr.items()}], core_ids=[0])
    o = r.results[0][_OUT[0]]
    return o.transpose(2, 1, 0).reshape(BATCH, SEQ, D)
```

```python
import numpy as np
import concourse.bass as bass
from concourse import mybir
from contextlib import ExitStack

F32 = mybir.dt.float32
F32R = mybir.dt.float32r
BF16 = mybir.dt.bfloat16
I32 = mybir.dt.int32
U8 = mybir.dt.uint8
U32 = mybir.dt.uint32
ALU = mybir.AluOpType
ACT = mybir.ActivationFunctionType
AX = mybir.AxisListType.X

P = 128
BATCH, SEQ, D = 2, 1024, 256
TOK = BATCH * SEQ
KT = D // P
NT = TOK // P
BLK = 512
NB = TOK // BLK
TPB = BLK // P
E = 8
HEADS, DH = 16, 64
NCH = HEADS * DH // P
NQ = SEQ // P
HG = 4
NHG = HEADS // HG
UNITS = NQ * NHG
CAP = 640
BITS = 30
STEP = 4
NEG = -1.0e30
LROW = P - 1 + SEQ

PAR = {}
_at = 0
for _n, _w in (("w0", 2), ("b0", 2), ("g0", 2), ("b1", 2), ("g1", 2), ("gn", 2), ("go", 2), ("qs", 1),
               ("ks", 1), ("nk", 1), ("nab", 16), ("nv", 1), ("b2", 1)):
    PAR[_n] = (_at, _at + _w)
    _at += _w
PAR_END = _at

SB = 256
RING = 4
MOE = [dict(mt=1, sh=2, pair=True, top=2), dict(mt=4, sh=4, pair=True, top=1),
       dict(mt=8, sh=0, pair=False, top=2)]
NBLK = [TOK * m["top"] // SB + E - 1 for m in MOE[:2]]
ETILES = (3, 2)
assert sum(ETILES) * P == CAP
SLOTS = [NBLK[0] * SB, NBLK[1] * SB, E * CAP]
NTAB = max(NBLK) + 1

C_ID, C_MEAN, C_B64, C_TRI, C_SEL, C_WD, C_EPS = 0, 128, 256, 384, 512, 514, 522
C_JT, C_KT, C_EB, C_TR = 523, 531, 531 + NTAB, 539 + NTAB
C_END = C_TR + 2 * NT
ATT_LINKS = UNITS * (HG + 1) + 1


def wcols(mt, pair):
    return (2 if pair else 1) * KT * mt * P + mt * D


def shared_before(l):
    return (NB, NB - 1, 0)[l]


def build(nc, A):
    ctx = ExitStack()
    with ctx:
        def sb(name, shape, dt=F32):
            return ctx.enter_context(nc.sbuf_tensor(name, shape, dt))

        def sem(name):
            return ctx.enter_context(nc.semaphore(name))

        xT = sb("xT", [P, KT, TOK])
        cst = sb("cst", [P, C_END])
        par = sb("par", [P, PAR_END])
        wbuf = [sb(f"wbuf{i}", [P, 4096]) for i in range(2)]
        wsh = sb("wsh", [P, 3072])
        small = sb("small", [P, 2048])
        TA = sb("TA", [P, HEADS * SEQ])
        PB = sb("PB", [P, 8192])
        vall = sb("vall", [P, NT * (DH + 1)])
        kcur = [sb(f"kcur{i}", [P, SEQ], F32R) for i in range(2)]
        vcur = sb("vcur", [P, NQ * (DH + 1)])
        qtile = [sb(f"qtile{i}", [P, HEADS, P], F32R) for i in range(2)]
        obuf = [sb(f"obuf{i}", [P, 2, P]) for i in range(2)]
        ones_bf = sb("ones_bf", [P, P], BF16)
        tri_bf = sb("tri_bf", [P, P], BF16)
        mask8 = sb("mask8", [P, NT], U8)
        bits = sb("bits", [P, BITS // 2 * STEP], I32)
        put_i = sb("put_i", [P, 2 * NT], U32)
        get_i = sb("get_i", [P, 2 * NT], U32)
        btab = sb("btab", [P, NTAB], I32)
        ps = ctx.enter_context(nc.psum_tensor("ps", [P, 8 * BLK], F32))

        def bank(i, n=BLK):
            return ps[:, i * BLK:i * BLK + n]

        ident = cst[:, C_ID:C_ID + P]
        meanm = cst[:, C_MEAN:C_MEAN + P]
        b64 = cst[:, C_B64:C_B64 + P]
        sel2 = cst[:, C_SEL:C_SEL + 2]
        wdesc = cst[:, C_WD:C_WD + E]
        eps = cst[:, C_EPS:C_EPS + 1]

        def pr(name, k=None):
            a, b = PAR[name]
            return par[:, a:b] if k is None else par[:, a + k:a + k + 1]

        def sm(at, n):
            return small[:, at:at + n]
        L = sm(0, 128)
        G, KP, TI = sm(1600, 128), sm(1728, 128), sm(1856, 128)
        R1, R2, R3, R4 = sm(128, 128), sm(256, 128), sm(384, 128), sm(512, 128)
        M1, M2, W1c, W2c, Zc = sm(640, 16), sm(656, 16), sm(672, 16), sm(688, 16), sm(704, 16)
        wts = sm(720, 32)
        slotf = sm(752, 32)
        keptf = sm(784, 32)
        rank_end = sm(816, 8)
        nblk, eblk = sm(824, 8), sm(832, 8)
        ebase = sm(840, 8)
        thr, cnt = sm(896, 8), sm(904, 8)
        cand = sm(1248, STEP * E)
        ccnt = sm(1400, (STEP - 1) * E)
        cmpb = sb("cmpb", [P, P], BF16)
        cmpc = sb("cmpc", [P, (STEP - 1) * P], BF16)
        stdc, rstd = [sm(928, 4), sm(1136, 4)], [sm(932, 4), sm(1140, 4)]
        qs8, knull, kn1, kn2 = sm(936, 1), sm(937, 2), sm(939, 1), sm(940, 1)
        n2s, rns = sm(944, 72), sm(1016, 72)
        maskf = sm(1088, 16)
        mx, sn2, negm, dn = sm(1104, 8), sm(1112, 8), sm(1120, 8), sm(1128, 4)
        tabf = sm(1290, 32)
        jcmp = sm(1328, 64)
        kcmp = sm(1400, NTAB * E)
        scan = sm(1400, NT * E)
        wrt = sm(1152, 3 * KT * E)
        wg = sm(1200, 8)
        cond = sm(1208, 2)
        vsel = sm(1216, 2 * HEADS)
        pnull = sb("pnull", [P, BATCH * NQ * HEADS])

        yT = TA[:, 0:KT * TOK].rearrange("p (k t) -> p k t", k=KT)
        aT = TA[:, KT * TOK:2 * KT * TOK].rearrange("p (k t) -> p k t", k=KT)
        rows = TA[:, 8192:12288].rearrange("p (t d) -> p t d", t=NT)
        xb = [TA[:, 12288 + i * 768:12288 + (i + 1) * 768].rearrange("p (k t) -> p k t", k=KT) for i in range(2)]
        rin = [TA[:, 13824 + i * 768:13824 + (i + 1) * 768].rearrange("p (t d) -> p t d", t=3) for i in range(2)]
        got = [[rows[:, i * 2 + c, :] for c in range(2)] for i in range(RING)]
        gs = [PB[:, i * BLK:(i + 1) * BLK] for i in range(2)]
        hb = [PB[:, 1024 + i * BLK:1024 + (i + 1) * BLK] for i in range(2)]
        yrow = [PB[:, 2048 + i * 768:2048 + (i + 1) * 768].rearrange("p (t d) -> p t d", t=3) for i in range(2)]
        zrow = PB[:, 6912:6912 + D]
        ablk = [TA[:, 12288:16384].rearrange("p (c t) -> p c t", c=NCH),
                PB[:, 4096:8192].rearrange("p (c t) -> p c t", c=NCH)]
        def lanes(at):
            return [x[:, a:a + 1024].rearrange("p (k t) -> p k t", k=KT) for x, a in ((PB, at), (TA, 4096 + at))]
        xc, sq, lsrcs, louts = lanes(0), lanes(1024), lanes(2048), lanes(3072)
        lsrc, lout = lsrcs[0], louts[0]
        lrev = lsrc
        lnb = [lout, wsh[:, 0:1024].rearrange("p (k t) -> p k t", k=KT)]
        posr = PB[:, 4096:5120]
        w1sb = PB[:, 5120:5632]
        w2sb = PB[:, 5632:5664]
        lrow = PB[0:HEADS, 5664:5664 + LROW]
        qraw = [wbuf[0][:, c * BLK:(c + 1) * BLK] for c in range(8)] + [wbuf[1][:, c * BLK:(c + 1) * BLK] for c in (0, 5, 6, 7)]
        qsq = [wbuf[1][:, (1 + i) * BLK:(2 + i) * BLK] for i in range(2)]
        qout = [wbuf[1][:, (3 + i) * BLK:(4 + i) * BLK] for i in range(2)]
        wqk = PB[:, 4096:4096 + KT * 9 * P].rearrange("p (k m) -> p k m", k=KT)
        wv = PB[:, 6400:6400 + KT * DH].rearrange("p (k m) -> p k m", k=KT)
        bsel = PB[0:32 + 18, 6528:6528 + 9 * P]
        bsel_r = qtile[0].rearrange("p h q -> p (h q)")[0:32 + 18, 0:9 * P]
        rnT = qtile[1].rearrange("p h q -> p (h q)")[0:32 + 18, 0:BLK]
        prob = [PB[:, h * SEQ:(h + 1) * SEQ] for h in range(HG)]
        probT = PB[:, 4096:8192].rearrange("p (k h q) -> p k h q", k=NQ, h=HG)
        qtwice = [wbuf[1][:, i * 2048:(i + 1) * 2048].rearrange("p (h q) -> p h q", h=HEADS) for i in range(2)]
        dbuf = [wsh[0:DH + 1, i * BLK:(i + 1) * BLK] for i in range(2)]
        kall = wsh[:, 1024:3072]
        wout = wbuf[0][:, 0:NCH * D].rearrange("p (c m) -> p c m", c=NCH)
        rden = [wbuf[1][:, 0:2048].rearrange("p (c t) -> p c t", c=4), wbuf[1][:, 2048:4096].rearrange("p (c t) -> p c t", c=4)]
        dcmp, rcmp, pcmp = wsh[:, 0:256], wsh[:, 256:512], wsh[:, 512:768]
        pnT = wsh[:, 1280:1536]
        wnull = wsh[0:HEADS, 1536:1536 + D]
        prT = TA[0:HEADS, 0:TOK]

        l_d = nc.dram_tensor("bias_rows", (HEADS, LROW), F32, kind="Internal").ap()
        q_d = nc.dram_tensor("q_tiles", (DH, HEADS, TOK), F32, kind="Internal").ap()
        o_d = nc.dram_tensor("attn_num", (P, NCH, TOK), F32, kind="Internal").ap()
        d_d = nc.dram_tensor("attn_den", (HEADS, TOK), F32, kind="Internal").ap()
        xs_d = [nc.dram_tensor(f"slots_in{l}", (SLOTS[l] + (2 * TOK if l == 2 else 0), D), F32, kind="Internal").ap()
                for l in range(3)]
        ys_d = [nc.dram_tensor(f"slots_out{l}", (SLOTS[l], D), F32, kind="Internal").ap() for l in range(3)]
        p_d = nc.dram_tensor("null_prob", (HEADS, TOK), F32, kind="Internal").ap()
        pr_d = nc.dram_tensor("null_share", (HEADS, TOK), F32, kind="Internal").ap()
        r_d = nc.dram_tensor("attn_rden", (HEADS, TOK), F32, kind="Internal").ap()

        const_in = sem("const_in")
        relw_in = sem("relw_in")
        wsh_in = sem("wsh_in")
        ln_src, ln_mean, ln_xc, ln_sq = sem("ln_src"), sem("ln_mean"), sem("ln_xc"), sem("ln_sq")
        ln_var, ln_std, ln_rstd, ln_bc, ln_out = (sem("ln_var"), sem("ln_std"), sem("ln_rstd"), sem("ln_bc"),
                                                  sem("ln_out"))
        silu_done, w1_done, w2_done, rows_done, rows_out = (sem("silu_done"), sem("w1_done"), sem("w2_done"),
                                                            sem("rows_done"), sem("rows_out"))
        logits_done, top_diff, top_exp = sem("logits_done"), sem("top_diff"), sem("top_exp")
        ge_ready, ge_count = sem("ge_ready"), sem("ge_count")
        tie_ready, tie_count = sem("tie_ready"), sem("tie_count")
        rank_ready, rank_count = sem("rank_ready"), sem("rank_count")
        score_done, rows_in, zeroed = sem("score_done"), sem("rows_in"), sem("zeroed")
        M = []
        for l in range(3):
            names = ["slots", "put", "gu", "h", "down", "w0", "w1", "in0", "in1", "bt", "xb", "yrow", "out", "yfree",
                     "mixed", "mixt", "acc"]
            names += ["rowt", "rows"] if l else ["leaky"]
            names += ["act", "yacc"] if l < 2 else []
            names += ["w2", "w3"] if l == 0 else []
            M.append({n: sem(f"m{l}_{n}") for n in names})
        got_in = [sem(f"got_in{i}") for i in range(RING)]
        GOT = [16 * (NT // RING) * sum(m["top"] for m in MOE[:l]) for l in range(3)]
        dchain, cap_chain, att_chain = sem("dve_chain"), sem("cap_chain"), sem("att_chain")
        q_sqfree, q_tr, q_rnT = sem("q_sqfree"), sem("q_tr"), sem("q_rnT")
        pool_init = sem("pool_init")
        qkv_w_in, wout_in = sem("qkv_w_in"), sem("wout_in")
        q_mm, q_copied, q_sq, q_n2, q_std, q_rn, q_rb, q_norm = (
            sem("q_mm"), sem("q_copied"), sem("q_sq"), sem("q_n2"), sem("q_std"), sem("q_rn"), sem("q_rb"),
            sem("q_norm"))
        q_out = [sem("q_out0"), sem("q_out1")]
        v_mm, v_done, lrev_done = sem("v_mm"), sem("v_done"), sem("lrev_done")
        nk_sq, nk_mm, nk_std, nk_done = sem("nk_sq"), sem("nk_mm"), sem("nk_std"), sem("nk_done")
        toep_in = sem("toep_in")
        kv_cur = sem("kv_cur")
        q_in = [sem("q_in0"), sem("q_in1")]
        q_round, q_split = sem("q_round"), sem("q_split")
        null_mm, sim_done, added, dn_done = (sem("null_mm"), sem("sim_done"),
                                                        sem("added"), sem("dn_done"))
        exp_done, pn_done, tr_done = sem("exp_done"), sem("pn_done"), sem("tr_done")
        evac = [sem("evac_act"), sem("evac_dve")]
        av_done, o_copied = sem("av_done"), sem("o_copied")
        o_out, batch_stored = [sem("o_out0"), sem("o_out1")], sem("batch_stored")
        pn_tr, pn_cp, den_out, wn_mm, wn_cp = sem("pn_tr"), sem("pn_cp"), sem("den_out"), sem("wn_mm"), sem("wn_cp")
        den_in, rden_done = sem("den_in"), sem("rden_done")
        ab_in, scale_in = [sem("ab_in0"), sem("ab_in1")], sem("scale_in")
        ab_scaled, proj_mm = sem("ab_scaled"), sem("proj_mm")
        y_out = sem("y_out")

        LN_REL, LN_QKV, LN_PROJ = 0, 4, 8

        def lane(i):
            return i % 2 if i < LN_QKV else 0

        class Blocks:
            def __init__(self, l):
                if l < 2:
                    self.nw = (4, 2)[l]
                    self.blocks = [dict(nt=SB // P, w=i, row=i * SB, fresh=True) for i in range(self.nw)]
                    self.turns, self.rest = divmod(NBLK[l], self.nw)
                    self.rows_turn = self.nw * SB
                else:
                    self.blocks = [dict(nt=nt, w=i, row=i * CAP + j * ETILES[0] * P, fresh=j == 0)
                                   for i in range(2) for j, nt in enumerate(ETILES)]
                    self.turns, self.rest = E // 2, 0
                    self.rows_turn = 2 * CAP
                self.n = len(self.blocks)
                self.total = self.n * self.turns + self.rest
        BL = [Blocks(l) for l in range(3)]

        def wslot(l, w):
            return wbuf[w // 2][:, w % 2 * 2048:(w % 2 + 1) * 2048] if l == 0 else wbuf[w]

        block = ctx.enter_context(nc.Block())

        def groups(qt):
            n = qt + 1
            return [(a, min(a + 4, n)) for a in range(0, n, 4)]
        EV, _e = [], 0
        for qt in range(NQ):
            EV.append(_e)
            _e += NHG * 2 * len(groups(qt))
        EV_B = _e
        TR_B = 2 * EV_B

        def tr_index(u, h, g):
            qt, hg = divmod(u, NHG)
            n = len(groups(qt))
            return 2 * EV[qt] + (hg * HG + h) * n + g

        TB = (4, 5, 2, 3, 0, 1)

        def tr_bank(u, h, g):
            return TB[(h * len(groups(u // NHG)) + g) % len(TB)]

        def ev_engine(u, h, g):
            return (h * len(groups(u // NHG)) + g) % 2

        def ev_index(u, h, g):
            qt, hg = divmod(u, NHG)
            n = len(groups(qt))
            return EV[qt] + hg * 2 * n + (h * n + g) // 2

        def mix_bank(l, b):
            return 2 * (b % 2) if l == 2 else 6
        LAST1 = shared_before(1) * MOE[1]["sh"] + BL[1].total * MOE[1]["mt"]
        assert MOE[1]["sh"] == NB

        @block.sync
        def _(sp):
            def zero_slots(l):
                n = SLOTS[l] // P
                sp.dma_start(xs_d[l][0:SLOTS[l], :].rearrange("(p n) d -> p n d", n=n),
                             zrow.unsqueeze(1).broadcast_to((P, n, D))).then_inc(zeroed, 16)

            for dst, src in ((cst[:, :], A["cst"]), (par[:, :], A["par"]), (xT[:, :, :], A["xT"]),
                             (wrt, A["wrt"]), (wg[0:64, :], A["wg"]), (cond[0:64, :], A["condT"]),
                             (mask8[:, :], A["mask"]), (bits[:, :], A["bits"])):
                sp.dma_start(dst, src).then_inc(const_in, 16)
            sp.dma_start(rows, A["xrows"]).then_inc(rows_in, 16)
            sp.wait_ge(pool_init, 3)
            zero_slots(0)
            for dst, src in ((posr, A["posr"]), (w1sb, A["w1"]), (w2sb, A["w2"])):
                sp.dma_start(dst, src).then_inc(relw_in, 16)

            def shared_weights(l):
                sp.dma_start(wsh[:, 0:wcols(MOE[l]["sh"], True)], A[f"wsh{l}"]).then_inc(wsh_in, 16)

            def blocks(l):
                m, bl, src, mt, ss = M[l], BL[l], A[f"wexp{l}"], MOE[l]["mt"], shared_before(l) * MOE[l]["sh"]
                ncol = wcols(mt, MOE[l]["pair"])

                def weights(it, k):
                    w = k % bl.n if l < 2 else bl.blocks[k]["w"]
                    if l < 2:
                        ex = sp.value_load(btab[0:1, bass.ds(it * bl.n + k, 1)], min_val=0, max_val=E - 1)
                    else:
                        ex = it * 2 + w
                    sp.dma_start(wslot(l, w)[:, 0:ncol], src[bass.ds(ex, 1)].rearrange("a p n -> (a p) n"))\
                      .then_inc(m[f"w{w}"], 16)

                def load(it, k):
                    b = bl.blocks[k]
                    sp.dma_start(rin[k % 2][:, 0:b["nt"], :],
                                 xs_d[l][bass.ds(it * bl.rows_turn + b["row"], b["nt"] * P), :]
                                 .rearrange("(t p) d -> p t d", p=P)).then_inc(m[f"in{k % 2}"], 16)

                if l == 2:
                    weights(0, 0)
                    weights(0, 2)
                sp.wait_ge(zeroed, 48 if l else 16)
                sp.wait_ge(m["put"], 16 * NT * MOE[l]["top"])
                load(0, 0)
                load(0, 1)
                ahead = 1 if l == 0 else 0
                if l < 2:
                    for k in range(2 + ahead):
                        weights(0, k)

                def step(it, k, n, more=True, used=True):
                    sp.wait_ge(m["bt"], n - 1)
                    load(it, k)
                    if l < 2 and more:
                        if used:
                            sp.wait_ge(m["down"], (n + ahead - bl.nw + 1) * mt + ss)
                        weights(it, k + ahead)
                    elif l == 2 and bl.blocks[k]["fresh"]:
                        sp.wait_ge(m["down"], (n - 2) * mt)
                        weights(it, k)
                if l < 2:
                    for k in range(2, bl.n):
                        step(0, k, k, used=k + ahead >= bl.nw)
                    with sp.Fori(1, bl.turns) as it:
                        for k in range(bl.n):
                            step(it, k, it * bl.n + k)
                    for k in range(bl.rest):
                        step(bl.turns, k, bl.turns * bl.n + k, k + ahead < bl.rest)
                else:
                    for k in (2, 3):
                        sp.wait_ge(m["bt"], k - 1)
                        load(0, k)
                    with sp.Fori(1, bl.turns) as it:
                        for k in range(4):
                            step(it, k, it * 4 + k)

            shared_weights(0)
            blocks(0)
            shared_weights(1)
            sp.wait_ge(rows_done, 3)
            sp.dma_start(l_d, lrow).then_inc(rows_out, 16)
            zero_slots(1)
            zero_slots(2)
            blocks(1)
            sp.wait_ge(rows_out, 16)
            for dst, src in ((wqk[:, :, :], A["wqk"]), (wv[:, :, :], A["wv"]), (bsel, A["bsel"])):
                sp.dma_start(dst, src).then_inc(qkv_w_in, 16)
            sp.wait_ge(M[1]["acc"], NB)
            for h in range(HEADS):
                sp.dma_start(TA[:, h * SEQ:(h + 1) * SEQ],
                             bass.AP(l_d.tensor, h * LROW, [[1, P], [1, SEQ]])).then_inc(toep_in, 16)
            for b in range(NB):
                for c in range(NCH):
                    n = b * 9 + c
                    sp.wait_ge(q_norm, n + 1)
                    for a in range(2):
                        sp.dma_start(q_d[:, 2 * c + a, b * BLK:(b + 1) * BLK], qout[c % 2][a * DH:(a + 1) * DH, :])\
                          .then_inc(q_out[c % 2], 16)
            for i in range(2):
                sp.wait_ge(q_out[i], 16 * NB * NCH)
            sp.wait_ge(q_norm, NB * 9)
            sp.dma_start(wout, A["wout"]).then_inc(wout_in, 16)
            sp.sem_inc(batch_stored, 1)
            with sp.Fori(0, BATCH) as b:
                def load_q(qt):
                    for a in range(2):
                        sp.dma_start(qtwice[qt % 2][a * DH:(a + 1) * DH, :, :], q_d[:, :, bass.ds(b * SEQ + qt * P, P)])\
                          .then_inc(q_in[qt % 2], 16)
                sp.wait_ge(kv_cur, b + 1)
                load_q(0)
                load_q(1)
                for u in range(UNITS):
                    qt, hg = divmod(u, NHG)
                    if hg == 0 and 1 <= qt < NQ - 1:
                        sp.wait_ge(sim_done, (b * UNITS + qt * NHG) * HG)
                        load_q(qt + 1)
                    sp.wait_ge(o_copied, b * UNITS + u + 1)
                    sp.dma_start(o_d[:, hg * 2:hg * 2 + 2, bass.ds(b * SEQ + qt * P, P)], obuf[u % 2][:, :, :])\
                      .then_inc(o_out[u % 2], 16)
                    sp.dma_start(d_d[hg * HG:(hg + 1) * HG, bass.ds(b * SEQ + qt * P, P)],
                                 dbuf[u % 2][DH:DH + 1, :].rearrange("a (h q) -> a h q", h=HG))\
                      .then_inc(o_out[u % 2], 16)
                for i in range(2):
                    sp.wait_ge(o_out[i], (b + 1) * (UNITS * 16))
                sp.sem_inc(batch_stored, 1)
            def load_ab(b):
                sp.dma_start(ablk[b % 2][:, :, :], o_d[:, :, b * BLK:(b + 1) * BLK]).then_inc(ab_in[b % 2], 16)

            def load_scale(b):
                for par_ in range(2):
                    for j in range(2):
                        sp.dma_start(rden[j][par_ * 64:par_ * 64 + 64, :, :],
                                     bass.AP(r_d.tensor, (par_ + 8 * j) * TOK + b * BLK,
                                             [[0, 64], [2 * TOK, 4], [1, BLK]])).then_inc(scale_in, 16)

            sp.dma_start(dcmp, d_d.rearrange("h (a t) -> (h a) t", a=8)).then_inc(den_in, 16)
            load_ab(0)
            sp.wait_ge(pn_cp, 1)
            for b in range(BATCH):
                for qt in range(NQ):
                    sp.dma_start(p_d[:, b * SEQ + qt * P:b * SEQ + (qt + 1) * P],
                                 pnT[qt * HEADS:(qt + 1) * HEADS, b * P:(b + 1) * P]).then_inc(den_out, 16)
            sp.wait_ge(den_out, 16 * BATCH * NQ)
            sp.dma_start(pcmp, p_d.rearrange("h (a t) -> (h a) t", a=8)).then_inc(den_in, 16)
            sp.wait_ge(rden_done, 1)
            sp.dma_start(r_d.rearrange("h (a t) -> (h a) t", a=8), rcmp).then_inc(den_out, 16)
            sp.dma_start(pr_d.rearrange("h (a t) -> (h a) t", a=8), pcmp).then_inc(den_out, 16)
            sp.wait_ge(den_out, 16 * (BATCH * NQ + 2))
            sp.dma_start(prT, pr_d).then_inc(den_in, 16)

            for b in range(NB):
                if b >= 2:
                    sp.wait_ge(proj_mm, b - 1)
                    load_ab(b)
                if b:
                    sp.wait_ge(ab_scaled, b)
                load_scale(b)
                if b == 0:
                    load_ab(1)
            sp.wait_ge(proj_mm, NB)
            blocks(2)
            for b in range(NB):
                sp.wait_ge(M[2]["acc"], b + 1)
                sp.dma_start(A["out"][:, :, b * BLK:(b + 1) * BLK], xT[:, :, b * BLK:(b + 1) * BLK]).then_inc(y_out, 16)
            sp.wait_ge(y_out, 16 * NB)

        @block.tensor
        def _(pe):
            mm = nc.tensor.matmul

            def mean_pe(i, src):
                pe.wait_ge(ln_src, i + 1)
                for k in range(KT):
                    last = mm(bank(3 * lane(i)), meanm, src[:, k, :], start=(k == 0), stop=(k == KT - 1))
                last.then_inc(ln_mean, 1)

            def var_pe(i):
                pe.wait_ge(ln_sq, i + 1)
                for t in range(TPB):
                    for k in range(KT):
                        last = mm(bank(3 * lane(i) + 1)[:, t:t + 1], sq[lane(i)][:, k, t * P:(t + 1) * P], meanm[:, 0:1],
                                  start=(k == 0), stop=(k == KT - 1))
                last.then_inc(ln_var, 1)

            def spread_pe(i):
                pe.wait_ge(ln_rstd, i + 1)
                for t in range(TPB):
                    last = mm(bank(3 * lane(i) + 2)[:, t * P:(t + 1) * P],
                              rstd[lane(i)][:, t:t + 1].broadcast_to((P, P)), ident, start=True, stop=True)
                last.then_inc(ln_bc, 1)

            def relpos_pe(r):
                n = r // 4
                for b in range(2):
                    i = LN_REL + 2 * n + b
                    if r % 4 == 0:
                        mean_pe(i, lsrcs[b])
                    elif r % 4 == 1:
                        var_pe(i)
                    elif r % 4 == 2:
                        spread_pe(i)
                    elif n == 0:
                        pe.wait_ge(silu_done, b + 1)
                        for mt_ in range(KT):
                            for k in range(KT):
                                last = mm(bank(3 * b + 2 * mt_), w1sb[:, k * D + mt_ * P:k * D + (mt_ + 1) * P],
                                          louts[b][:, k, :], start=(k == 0), stop=(k == KT - 1))
                        last.then_inc(w1_done, 1)
                    else:
                        pe.wait_ge(silu_done, 2 + b + 1)
                        for k in range(KT):
                            last = mm(bank(3 * b + 1)[0:HEADS, :], w2sb[:, k * HEADS:(k + 1) * HEADS], louts[b][:, k, :],
                                      start=(k == 0), stop=(k == KT - 1))
                        last.then_inc(w2_done, 1)

            def ln_pe(i, src):
                mean_pe(i, src)
                var_pe(i)
                spread_pe(i)

            def logits_pe(l, src):
                for t in range(NT):
                    o = bank(7)[:, t * E:(t + 1) * E]
                    for k in range(KT):
                        last = mm(o, src[:, k, t * P:(t + 1) * P], wrt[:, (l * KT + k) * E:(l * KT + k + 1) * E],
                                  start=(k == 0), stop=(k == KT - 1 and l > 0))
                    if l == 0:
                        b = t * P // SEQ
                        last = mm(o, cond[0:64, b:b + 1].broadcast_to((64, P)), wg[0:64, :], start=False, stop=True)
                last.then_inc(logits_done, 1)

            def ranks_pe(l, n):
                for i in range(2):
                    pe.wait_ge(rank_ready, n * 2 + i + 1)
                    mm(bank(7)[:, 0:P], ones_bf[:, :] if i == 0 else tri_bf[:, :], cmpb[:, :], start=True, stop=True)\
                        .then_inc(rank_count, 1)

            def rows_pe(l, src):
                for j in range(NT // 2):
                    if j >= 2:
                        pe.wait_ge(M[l]["rows"], 2 * (j - 1))
                    for t in (2 * j, 2 * j + 1):
                        for k in range(KT):
                            o = (4 + j % 2) * BLK + (t % 2) * D + k * P
                            last = nc.tensor.transpose(ps[:, o:o + P], src[:, k, t * P:(t + 1) * P], ident)
                    last.then_inc(M[l]["rowt"], 1)
                pe.wait_ge(M[l]["rows"], NT)

            def hidden(m, w, mt, pair, mi, s, x, n):
                for half in range(2 if pair else 1):
                    for k in range(KT):
                        col = half * KT * mt * P + k * mt * P + mi * P
                        last = mm(bank(2 * half + s % 2, n), w[:, col:col + P], x[:, k, :],
                                  start=(k == 0), stop=(k == KT - 1))
                last.then_inc(m["gu"], 1)

            def shared_pe(l, raw):
                m, sh = M[l], MOE[l]["sh"]
                prev = None

                def down(n, mi, s):
                    pe.wait_ge(m["h"], s + 1)
                    if mi == 0 and n > 0:
                        pe.wait_ge(m["yacc"], n)
                    off = 2 * KT * sh * P + mi * D
                    for k in range(KT):
                        last = mm(bank(4 + k), wsh[:, off + k * P:off + (k + 1) * P], hb[s % 2],
                                  start=(mi == 0), stop=(mi == sh - 1))
                    last.then_inc(m["down"], 1)
                pe.wait_ge(wsh_in, 16 * (l + 1))
                s = 0
                for n in range(shared_before(l)):
                    for mi in range(sh):
                        hidden(m, wsh, sh, True, mi, s, raw[:, :, n * BLK:(n + 1) * BLK], BLK)
                        if prev is not None:
                            down(*prev)
                        prev = (n, mi, s)
                        s += 1
                down(*prev)
                pe.wait_ge(m["yacc"], shared_before(l))

            def last_hidden(mi):
                if mi == 0:
                    pe.wait_ge(M[1]["yrow"], BL[1].total)
                hidden(M[1], wsh, MOE[1]["sh"], True, mi, mi, yT[:, :, (NB - 1) * BLK:], BLK)

            def last_down(mi):
                sh = MOE[1]["sh"]
                off = 2 * KT * sh * P + mi * D
                pe.wait_ge(M[1]["h"], LAST1 + mi + 1)
                for k in range(KT):
                    last = mm(bank(4 + k), wsh[:, off + k * P:off + (k + 1) * P], hb[mi % 2],
                              start=(mi == 0), stop=(mi == sh - 1))
                last.then_inc(M[1]["down"], 1)

            def blocks_pe(l):
                m, bl, mt, pair = M[l], BL[l], MOE[l]["mt"], MOE[l]["pair"]
                ybank = (4, 5) if l < 2 else (4, 5, 2)

                def turn(it, n0, s0, nblk):
                    def turned(k):
                        nt = bl.blocks[k]["nt"]
                        if k:
                            pe.wait_ge(m["xb"], n0 + k)
                        pe.wait_ge(m[f"in{k % 2}"], (it * (bl.n // 2) + k // 2 + 1) * 16)
                        for t in range(nt):
                            for f in range(KT):
                                last = nc.tensor.transpose(bank(6 + f)[:, t * P:(t + 1) * P],
                                                           rin[k % 2][:, t, f * P:(f + 1) * P], ident)
                        last.then_inc(m["bt"], 1)

                    def down(k, mi, s):
                        b = bl.blocks[k]
                        off = (2 if pair else 1) * KT * mt * P + mi * D
                        pe.wait_ge(m["h"], s0 + s + 1)
                        if mi == 0 and k > 0:
                            pe.wait_ge(m["yrow"], n0 + k)
                        for t in range(b["nt"]):
                            last = mm(bank(ybank[t], D), hb[s % 2][:, t * P:(t + 1) * P],
                                      wslot(l, b["w"])[:, off:off + D], start=(mi == 0), stop=(mi == mt - 1))
                        last.then_inc(m["down"], 1)

                    turned(0)
                    s, prev = 0, None
                    for k in range(nblk):
                        b = bl.blocks[k]
                        if b["fresh"]:
                            pe.wait_ge(m[f"w{b['w']}"], (it + 1) * 16)
                        if k + 1 == nblk:
                            pe.wait_ge(m["xb"], n0 + k + 1)
                        if k + 1 < nblk:
                            turned(k + 1)
                        for mi in range(mt):
                            hidden(m, wslot(l, b["w"]), mt, pair, mi, s, xb[k % 2][:, :, 0:b["nt"] * P], b["nt"] * P)
                            if prev is not None:
                                down(*prev)
                            prev = (k, mi, s)
                            s += 1
                    down(*prev)
                base = shared_before(l) * MOE[l]["sh"]
                with pe.Fori(0, bl.turns) as it:
                    turn(it, it * bl.n, it * (bl.n * mt) + base, bl.n)
                if bl.rest:
                    turn(bl.turns, bl.turns * bl.n, bl.turns * bl.n * mt + base, bl.rest)

            def mix_pe(l):
                m = M[l]
                for b in range(NB):
                    if l == 1:
                        last_hidden(b)
                    if b >= (2 if l == 2 else 1):
                        pe.wait_ge(m["acc"], b - 1 if l == 2 else b)
                    for t in range(TPB):
                        pe.wait_ge(m["mixed"], b * TPB + t + 1)
                        for k in range(KT):
                            last = nc.tensor.transpose(bank(mix_bank(l, b) + k)[:, t * P:(t + 1) * P],
                                                       got[t % RING][0][:, k * P:(k + 1) * P], ident)
                        last.then_inc(m["mixt"], 1)
                        if l == 0 and t % 2:
                            relpos_pe((b * TPB + t) // 2)
                    if l == 1:
                        last_down(b)

            pe.wait_ge(const_in, 16 * 8)
            pe.wait_ge(pool_init, 3)
            logits_pe(0, xT)
            ranks_pe(0, 0)
            shared_pe(0, xT)
            blocks_pe(0)
            pe.wait_ge(relw_in, 16 * 3)
            mix_pe(0)
            pe.wait_ge(nk_sq, 1)
            mm(bank(5)[:, 0:1], b64, kn1, start=True, stop=True).then_inc(nk_mm, 1)
            pe.wait_ge(nk_std, 1)
            pe.wait_ge(rows_done, 3)
            pe.wait_ge(M[0]["acc"], NB)
            logits_pe(1, yT)
            rows_pe(1, yT)
            ranks_pe(1, 1)
            shared_pe(1, yT)
            blocks_pe(1)
            mix_pe(1)
            pe.wait_ge(M[1]["acc"], NB)
            pe.wait_ge(qkv_w_in, 48)
            ln_pe(LN_QKV, xT[:, :, 0:BLK])

            def n2_mm(b, c):
                pe.wait_ge(q_sq, b * 9 + c + 1)
                for t in range(TPB):
                    o = bank(5)[:, (t * 9 + c) * 2:(t * 9 + c) * 2 + 2]
                    last = mm(o, qsq[c % 2][:, t * P:(t + 1) * P], sel2, start=True, stop=True)
                last.then_inc(q_n2 if c == 8 else q_sqfree, 1)

            def spread_norm(b, c):
                n = b * 9 + c
                if c == 0:
                    pe.wait_ge(q_rnT, b + 1)
                if n >= 2:
                    pe.wait_ge(q_norm, n - 1)
                mm(bank(6 + n % 2), bsel_r[:, c * P:(c + 1) * P], rnT, start=True, stop=True).then_inc(q_rb, 1)

            def turn_norm(b):
                pe.wait_ge(q_rn, b + 1)
                for t in range(TPB):
                    last = nc.tensor.transpose(bank(0)[0:18, t * P:(t + 1) * P], rns[:, t * 18:(t + 1) * 18], ident)
                last.then_inc(q_tr, 1)
            for b in range(NB):
                pe.wait_ge(ln_out, LN_QKV + b + 1)
                nxt = LN_QKV + b + 1
                for c in range(9):
                    n = b * 9 + c
                    if n >= 2:
                        pe.wait_ge(q_copied, n - 1)
                        pe.wait_ge(q_sq, n - 1)
                    if c == 8:
                        pe.wait_ge(lrev_done, b + 1)
                    for k in range(KT):
                        last = mm(bank(3 + n % 2), wqk[:, k, c * P:(c + 1) * P], (lrev if c == 8 else lnb[b % 2])[:, k, :],
                                  start=(k == 0), stop=(k == KT - 1))
                    last.then_inc(q_mm, 1)
                    if c == 0 and b:
                        turn_norm(b - 1)
                    if c >= 1:
                        if b:
                            spread_norm(b - 1, c - 1)
                        n2_mm(b, c - 1)
                    if b + 1 < NB:
                        if c == 2:
                            mean_pe(nxt, xT[:, :, (b + 1) * BLK:(b + 2) * BLK])
                        elif c == 4:
                            if b:
                                pe.wait_ge(v_done, b)
                            var_pe(nxt)
                        elif c == 6:
                            spread_pe(nxt)
                n2_mm(b, 8)
                if b:
                    spread_norm(b - 1, 8)
                    pe.wait_ge(v_done, b)
                for t in range(TPB):
                    for k in range(KT):
                        last = mm(bank(1)[:, t * DH:(t + 1) * DH], lrev[:, k, t * P:(t + 1) * P], wv[:, k, :],
                                  start=(k == 0), stop=(k == KT - 1))
                last.then_inc(v_mm, 1)
            turn_norm(NB - 1)
            for c in range(9):
                spread_norm(NB - 1, c)
            pe.wait_ge(v_done, NB)
            pe.wait_ge(nk_done, 2)
            with pe.Fori(0, BATCH) as b:
                ub = b * UNITS

                def left(u, banks):
                    last = {}
                    for h in range(HG):
                        for g in range(len(groups(u // NHG))):
                            if tr_bank(u, h, g) in banks:
                                last[ev_engine(u, h, g)] = ev_index(u, h, g) + 1
                    for e in sorted(last):
                        pe.wait_ge(evac[e], b * EV_B + last[e])

                def null_sims(u):
                    qt, hg = divmod(u, NHG)
                    pe.wait_ge(q_split, ub + u + 1)
                    for h in range(HG):
                        last = mm(bank(7)[:, h:h + 1], qtwice[qt % 2][0:DH, hg * HG + h, :], knull[0:DH, 0:1],
                                  start=True, stop=True)
                    last.then_inc(null_mm, 1)

                def sims(u, heads):
                    qt, hg = divmod(u, NHG)
                    nk = (qt + 1) * P
                    for h in heads:
                        if u * HG + h >= 2:
                            pe.wait_ge(added, (ub + u) * HG + h - 1)
                        if h < 2 and u:
                            left(u - 1, (2 * h, 2 * h + 1))
                        for f in range(0, nk, BLK):
                            w = min(BLK, nk - f)
                            for i in range(2):
                                last = mm(ps[:, (h % 2) * 2 * BLK + f:(h % 2) * 2 * BLK + f + w],
                                          qtile[qt % 2][:, hg * HG + h, :], kcur[i][:, SEQ - nk + f:SEQ - nk + f + w],
                                          start=(i == 0), stop=(i == 1))
                        last.then_inc(sim_done, 1)

                pe.wait_ge(kv_cur, b + 1)
                null_sims(0)
                sims(0, range(HG))
                for u in range(UNITS):
                    qt, hg = divmod(u, NHG)
                    n = 0
                    done = []
                    for h in range(HG):
                        pe.wait_ge(exp_done, (ub + u) * HG + h + 1)
                        for g, (k0, k1) in enumerate(groups(qt)):
                            if n >= len(TB):
                                ph, pg = done[n - len(TB)]
                                pe.wait_ge(evac[ev_engine(u, ph, pg)], b * EV_B + ev_index(u, ph, pg) + 1)
                            if n == 2:
                                pe.wait_ge(added, (ub + u + 1) * HG)
                            for kt in range(k0, k1):
                                o = bank(tr_bank(u, h, g))[:, (kt - k0) * P:(kt - k0 + 1) * P]
                                last = nc.tensor.transpose(o, prob[h][:, kt * P:(kt + 1) * P], ident)
                            last.then_inc(tr_done, 1)
                            done.append((h, g))
                            n += 1
                    if u + 1 < UNITS:
                        null_sims(u + 1)
                        sims(u + 1, (0, 1))
                    for e in range(2):
                        pe.wait_ge(evac[e], b * EV_B + EV[qt] + (hg + 1) * 2 * len(groups(qt)))
                    if u >= 1:
                        pe.wait_ge(o_copied, ub + u)
                    later = {(qt + 1) // 3: (2,), (2 * qt + 2) // 3: (3,)} if qt else {0: (2, 3)}
                    for kt in range(qt + 1):
                        if kt in later and u + 1 < UNITS:
                            sims(u + 1, later[kt])
                        last = mm(bank(6)[0:DH + 1, :], vcur[:, (NQ - 1 - qt + kt) * (DH + 1):(NQ - qt + kt) * (DH + 1)],
                           probT[:, kt, :, :].rearrange("p h q -> p (h q)"), start=(kt == 0), stop=(kt == qt))
                    last.then_inc(av_done, 1)
            pe.wait_ge(pn_done, BATCH * UNITS)
            for b in range(BATCH):
                last = nc.tensor.transpose(bank(0)[:, b * P:(b + 1) * P], pnull[:, b * P:(b + 1) * P], ident)
            last.then_inc(pn_tr, 1)
            pe.wait_ge(wout_in, 16)
            for c in range(NCH):
                last = mm(bank(1)[0:HEADS, 0:D], vsel[:, HEADS - 2 - 2 * c:2 * HEADS - 2 - 2 * c], wout[:, c, :],
                          start=(c == 0), stop=(c == NCH - 1))
            last.then_inc(wn_mm, 1)
            pe.wait_ge(pn_cp, 1)
            pe.wait_ge(wn_cp, 1)
            pe.wait_ge(den_in, 48)
            for b in range(NB):
                pe.wait_ge(ab_scaled, b + 1)
                prev = LN_PROJ + b - 1
                for k in range(KT):
                    o = bank(3 + 2 * (b % 2) + k)
                    mm(o, wnull[:, k * P:(k + 1) * P], prT[:, b * BLK:(b + 1) * BLK], start=True, stop=False)
                    for c in range(NCH):
                        last = mm(o, wout[:, c, k * P:(k + 1) * P], ablk[b % 2][:, c, :],
                                  start=False, stop=(c == NCH - 1))
                        if b and k == 0 and c == 1:
                            mean_pe(prev, lsrc)
                        elif b and k == 0 and c == 5:
                            var_pe(prev)
                        elif b and k == 1 and c == 1:
                            spread_pe(prev)
                last.then_inc(proj_mm, 1)
            ln_pe(LN_PROJ + NB - 1, lsrc)
            pe.wait_ge(ln_out, LN_PROJ + NB)
            logits_pe(2, aT)
            rows_pe(2, aT)
            with pe.Fori(0, BITS // 2) as i:
                pe.wait_ge(ge_ready, i + 1)
                mm(bank(7)[:, 0:(STEP - 1) * P], ones_bf[:, :], cmpc[:, :], start=True, stop=True).then_inc(ge_count, 1)
            for i in range(3):
                pe.wait_ge(tie_ready, i + 1)
                mm(bank(7)[:, 0:P], ones_bf[:, :] if i < 2 else tri_bf[:, :], cmpb[:, :], start=True, stop=True)\
                    .then_inc(tie_count, 1)
            ranks_pe(2, 2)
            blocks_pe(2)
            mix_pe(2)

        @block.scalar
        def _(act):
            fn = nc.scalar.activation

            def square_act(i):
                act.wait_ge(ln_xc, i + 1)
                fn(sq[lane(i)], xc[lane(i)], ACT.Square).then_inc(ln_sq, 1)

            def std_act(i):
                act.wait_ge(ln_var, i + 1)
                fn(stdc[lane(i)], bank(3 * lane(i) + 1)[:, 0:TPB], ACT.Sqrt, bias=eps).then_inc(ln_std, 1)

            def ln_act(i):
                square_act(i)
                std_act(i)

            def rows_act(l):
                m = M[l]
                if l == 1:
                    act.wait_ge(score_done, 1)
                for t in range(NT):
                    act.wait_ge(m["rowt"], t // 2 + 1)
                    src = ps[:, (4 + t // 2 % 2) * BLK + (t % 2) * D:(4 + t // 2 % 2) * BLK + (t % 2) * D + D]
                    if l == 1:
                        ins = fn(rows[:, t, :], src, ACT.Copy, scale=wts[:, t:t + 1])
                    else:
                        ins = fn(rows[:, t, :], src, ACT.Copy)
                    ins.then_inc(m["rows"], 1)

            def moe_act(l):
                m, bl, mt, sh, pair = M[l], BL[l], MOE[l]["mt"], MOE[l]["sh"], MOE[l]["pair"]
                f = (ACT.Copy, ACT.Silu, ACT.Relu)[l]

                def steps(s0, sizes):
                    for s, n in enumerate(sizes):
                        act.wait_ge(m["gu"], s0 + s + 1)
                        if pair:
                            if s >= 2:
                                act.wait_ge(m["h"], s0 + s - 1)
                            fn(gs[s % 2][:, 0:n], bank(s % 2, n), f).then_inc(m["act"], 1)
                        else:
                            if s >= 2:
                                act.wait_ge(m["down"], s0 + s - 1)
                            fn(hb[s % 2][:, 0:n], bank(s % 2, n), f).then_inc(m["h"], 1)
                sizes = [b["nt"] * P for b in bl.blocks for _ in range(mt)]
                first = shared_before(l) * sh
                if sh:
                    steps(0, [BLK] * first)
                with act.Fori(0, bl.turns) as it:
                    steps(it * len(sizes) + first, sizes)
                if bl.rest:
                    steps(bl.turns * len(sizes) + first, sizes[:bl.rest * mt])
                if l == 1:
                    steps(LAST1, [BLK] * sh)

            act.wait_ge(const_in, 16 * 8)
            def top_act(l):
                act.wait_ge(top_diff, l + 1)
                if l == 0:
                    fn(W2c, Zc, ACT.Exp).then_inc(top_exp, 1)
                elif l == 1:
                    fn(W2c, Zc, ACT.Exp, scale=-1.0).then_inc(top_exp, 1)
                else:
                    fn(R4, R4, ACT.Exp).then_inc(top_exp, 1)
            top_act(0)
            moe_act(0)
            for n in range(2):
                for part in (square_act, std_act):
                    for b in range(2):
                        part(LN_REL + 2 * n + b)
                for b in range(2):
                    act.wait_ge(ln_out, LN_REL + 2 * n + b + 1)
                    fn(louts[b], louts[b], ACT.Silu).then_inc(silu_done, 1)
            act.wait_ge(nk_mm, 1)
            fn(kn2, bank(5)[:, 0:1], ACT.Sqrt).then_inc(nk_std, 1)
            top_act(1)
            rows_act(1)
            moe_act(1)
            ln_act(LN_QKV)
            for b in range(NB):
                for c in range(9):
                    n = b * 9 + c
                    if n >= len(qraw):
                        act.wait_ge(q_norm, n - len(qraw) + 1)
                    act.wait_ge(q_mm, n + 1)
                    if c >= 2:
                        act.wait_ge(q_sqfree, b * 8 + c - 1)
                    elif b:
                        act.wait_ge(q_n2, b)
                    fn(qsq[c % 2], bank(3 + n % 2), ACT.Square).then_inc(q_sq, 1)
                    fn(qraw[n % len(qraw)], bank(3 + n % 2), ACT.Copy).then_inc(q_copied, 1)
                    if b + 1 < NB:
                        if c == 3:
                            square_act(LN_QKV + b + 1)
                        elif c == 5:
                            std_act(LN_QKV + b + 1)
                act.wait_ge(q_n2, b + 1)
                fn(n2s, bank(5)[:, 0:72], ACT.Sqrt).then_inc(q_std, 1)
            with act.Fori(0, BATCH) as b:
                ub = b * UNITS

                def exps(u):
                    qt, hg = divmod(u, NHG)
                    for h in range(HG):
                        act.wait_ge(added, (ub + u) * HG + h + 1)
                        fn(prob[h][:, 0:(qt + 1) * P], prob[h][:, 0:(qt + 1) * P], ACT.Exp,
                           bias=negm[:, (u % 2) * 4 + h:(u % 2) * 4 + h + 1]).then_inc(exp_done, 1)
                    act.wait_ge(dn_done, ub + u + 1)
                    fn(pnull[:, bass.ds(b * (NQ * HEADS) + (qt * HEADS + hg * HG), HG)], dn, ACT.Exp).then_inc(pn_done, 1)
                exps(0)
                for u in range(UNITS):
                    qt, hg = divmod(u, NHG)
                    for h in range(HG):
                        for g, (k0, k1) in enumerate(groups(qt)):
                            if ev_engine(u, h, g) != 0:
                                continue
                            act.wait_ge(tr_done, b * TR_B + tr_index(u, h, g) + 1)
                            fn(probT[:, k0:k1, h, :], bank(tr_bank(u, h, g))[:, 0:(k1 - k0) * P]
                               .rearrange("p (k q) -> p k q", q=P), ACT.Copy).then_inc(evac[0], 1)
                    if u + 1 < UNITS:
                        exps(u + 1)
            act.wait_ge(pn_tr, 1)
            fn(pnT, bank(0)[:, 0:BATCH * P], ACT.Copy).then_inc(pn_cp, 1)
            act.wait_ge(wn_mm, 1)
            fn(wnull, bank(1)[0:HEADS, 0:D], ACT.Copy).then_inc(wn_cp, 1)
            for b in range(NB):
                act.wait_ge(proj_mm, b + 1)
                for k in range(KT):
                    last = fn(lsrc[:, k, :], bank(3 + 2 * (b % 2) + k), ACT.Copy)
                last.then_inc(ln_src, 1)
                ln_act(LN_PROJ + b)
            top_act(2)
            rows_act(2)
            moe_act(2)

        @block.gpsimd
        def _(pool):
            nc.gpsimd.memset(zrow, 0.0).then_inc(pool_init, 1)
            nc.gpsimd.memset(ones_bf[:, :], 1.0).then_inc(pool_init, 1)
            pool.wait_ge(const_in, 16 * 8)
            nc.gpsimd.tensor_copy(tri_bf[:, :], cst[:, C_TRI:C_TRI + P]).then_inc(pool_init, 1)

            def put_rows(l):
                m = M[l]
                pool.wait_ge(m["slots"], 1)
                pool.wait_ge(zeroed, 48 if l else 16)
                if l == 0:
                    pool.wait_ge(rows_in, 16)
                for t in range(NT):
                    if l:
                        pool.wait_ge(m["rows"], t + 1)
                    for c in range(MOE[l]["top"]):
                        nc.gpsimd.indirect_dma_start(
                            out=xs_d[l][:, :], out_offset=bass.IndirectOffsetOnAxis(ap=put_i[:, c * NT + t:c * NT + t + 1], axis=0),
                            in_=rows[:, t, :], in_offset=None).then_inc(m["put"], 16)

            def store_blocks(l):
                m, bl = M[l], BL[l]
                pool.sem_inc(m["yfree"], 2)

                def store(it, k):
                    b = bl.blocks[k]
                    pool.wait_ge(m["yrow"], it * bl.n + k + 1)
                    nc.gpsimd.dma_start(ys_d[l][bass.ds(it * bl.rows_turn + b["row"], b["nt"] * P), :]
                                        .rearrange("(t p) d -> p t d", p=P), yrow[k % 2][:, 0:b["nt"], :])\
                        .then_inc(m["out"], 16)
                    pool.wait_ge(m["out"], (it * bl.n + k + 1) * 16)
                    pool.sem_inc(m["yfree"], 1)
                with pool.Fori(0, bl.turns) as it:
                    for k in range(bl.n):
                        store(it, k)
                for k in range(bl.rest):
                    store(bl.turns, k)

            def get_rows(l):
                m = M[l]
                for t in range(NT):
                    if t >= RING:
                        pool.wait_ge(m["mixt"], t - RING + 1)
                    for c in range(MOE[l]["top"]):
                        nc.gpsimd.indirect_dma_start(
                            out=got[t % RING][c], out_offset=None, in_=ys_d[l][:, :],
                            in_offset=bass.IndirectOffsetOnAxis(ap=get_i[:, c * NT + t:c * NT + t + 1], axis=0))\
                            .then_inc(got_in[t % RING], 16)

            for l in range(2):
                put_rows(l)
                store_blocks(l)
                get_rows(l)
            for b in range(NB):
                pool.wait_ge(ln_out, LN_QKV + b + 1)
                if b:
                    pool.wait_ge(v_mm, b)
                nc.gpsimd.tensor_copy(lrev, lnb[b % 2][:, :, ::-1]).then_inc(lrev_done, 1)
            pool.wait_ge(nk_done, 2)
            zeros = vsel[:, 0:1].unsqueeze(2).broadcast_to((P, HG, P))
            with pool.Fori(0, BATCH) as b:
                pool.wait_ge(kv_cur, b + 1)
                for u in range(UNITS):
                    qt, hg = divmod(u, NHG)
                    heads = slice(hg * HG, (hg + 1) * HG)
                    if hg == 0:
                        pool.wait_ge(q_in[qt % 2], (b * (NQ // 2) + qt // 2 + 1) * 32)
                        if qt >= 2:
                            pool.wait_ge(sim_done, (b * UNITS + (qt - 1) * NHG) * HG)
                    raw = qtwice[qt % 2][:, heads, :]
                    if u:
                        pool.wait_ge(q_split, b * UNITS + u)
                    nc.gpsimd.tensor_tensor(qtile[qt % 2][:, heads, :], raw, zeros, ALU.add).then_inc(q_round, 1)
                    pool.wait_ge(q_round, b * UNITS + u + 1)
                    lo = qtile[qt % 2][DH:P, heads, :]
                    nc.gpsimd.tensor_tensor(lo, qtwice[qt % 2][DH:P, heads, :], lo.bitcast(F32), ALU.subtract)\
                        .then_inc(q_split, 1)
            put_rows(2)
            store_blocks(2)
            get_rows(2)

        @block.vector
        def _(dve):
            v = nc.vector
            chain = [0]

            def link(ins):
                chain[0] += 1
                ins.then_inc(dchain, 1)
                dve.wait_ge(dchain, chain[0])

            def center_dve(i, src):
                if i >= LN_QKV:
                    dve.wait_ge(ln_out, i)
                dve.wait_ge(ln_mean, i + 1)
                v.tensor_tensor(xc[lane(i)], src, bank(3 * lane(i)).unsqueeze(1).broadcast_to((P, KT, BLK)), ALU.subtract)\
                    .then_inc(ln_xc, 1)

            def rstd_dve(i):
                dve.wait_ge(ln_std, i + 1)
                v.reciprocal(rstd[lane(i)], stdc[lane(i)]).then_inc(ln_rstd, 1)

            def scale_dve(i, dst, g):
                dve.wait_ge(ln_bc, i + 1)
                for k in range(KT):
                    last = v.scalar_tensor_tensor(out=dst[:, k, :], in0=xc[lane(i)][:, k, :], scalar=pr(g, k),
                                                  in1=bank(3 * lane(i) + 2), op0=ALU.mult, op1=ALU.mult)
                last.then_inc(ln_out, 1)

            def ln_dve(i, src, dst, g):
                center_dve(i, src)
                rstd_dve(i)
                scale_dve(i, dst, g)

            dve.wait_ge(const_in, 16 * 8)
            def relpos_dve(r):
                n = r // 4
                for b in range(2):
                    i = LN_REL + 2 * n + b
                    if r < 0:
                        for k in range(KT):
                            last = v.tensor_scalar(lsrcs[b][:, k, :], posr[:, b * BLK:(b + 1) * BLK], pr("w0", k), pr("b0", k),
                                                   ALU.mult, ALU.add)
                        last.then_inc(ln_src, 1)
                    elif r % 4 == 0:
                        center_dve(i, lsrcs[b])
                    elif r % 4 == 1:
                        rstd_dve(i)
                    elif r % 4 == 2:
                        scale_dve(i, louts[b], "g1" if n else "g0")
                    elif n == 0:
                        dve.wait_ge(w1_done, b + 1)
                        for k in range(KT):
                            last = v.tensor_scalar(lsrcs[b][:, k, :], bank(3 * b + 2 * k), pr("b1", k), None, ALU.add)
                        last.then_inc(ln_src, 1)
                    else:
                        dve.wait_ge(w2_done, b + 1)
                        v.tensor_scalar(lrow[:, P - 1 + b * BLK:P - 1 + (b + 1) * BLK], bank(3 * b + 1)[0:HEADS, :],
                                        par[0:HEADS, PAR["b2"][0]:PAR["b2"][1]], None, ALU.add).then_inc(rows_done, 1)

            L3 = L.rearrange("p (t e) -> p t e", e=E)

            def t3(x):
                return x.rearrange("p (t e) -> p t e", e=E)

            def bt(x):
                return x.unsqueeze(2).broadcast_to((P, NT, E))

            def be(x):
                return x.unsqueeze(1).broadcast_to((P, NT, E))

            def pick(src, mval, onehot, tmp):
                link(v.tensor_reduce(mval, t3(src), AX, ALU.max))
                link(v.tensor_tensor(t3(tmp), t3(src), bt(mval), ALU.is_equal))
                link(v.tensor_tensor(t3(tmp), t3(tmp), be(wdesc), ALU.mult))
                link(v.tensor_reduce(W1c, t3(tmp), AX, ALU.max))
                link(v.tensor_tensor(t3(onehot), t3(tmp), bt(W1c), ALU.is_equal))

            def second(first, tmp):
                link(v.scalar_tensor_tensor(out=tmp, in0=first, scalar=NEG, in1=L, op0=ALU.mult, op1=ALU.add))

            def route(l):
                dve.wait_ge(logits_done, l + 1)
                link(v.tensor_scalar(L, bank(7)[:, 0:P], 0.5 if l == 0 else 1.0, None, ALU.mult))
                pick(L, M1, R1, R4)
                if l != 1:
                    second(R1, R3)
                    pick(R3, M2, R2, R4)
                g1, g2 = wts[:, 0:NT], wts[:, NT:2 * NT]
                if l == 0:
                    v.tensor_tensor(Zc, M2, M1, ALU.subtract).then_inc(top_diff, 1)
                    dve.wait_ge(top_exp, 1)
                    link(v.tensor_scalar(W1c, W2c, 1.0, None, ALU.add))
                    link(v.reciprocal(g1, W1c))
                    link(v.tensor_tensor(g2, W2c, g1, ALU.mult))
                    slots(l)
                elif l == 1:
                    v.tensor_copy(Zc, M1).then_inc(top_diff, 1)
                    dve.wait_ge(top_exp, 2)
                    link(v.tensor_scalar(W1c, W2c, 1.0, None, ALU.add))
                    v.reciprocal(g1, W1c).then_inc(score_done, 1)
                    slots(l)
                else:
                    v.tensor_tensor(t3(R4), L3, bt(M1), ALU.subtract).then_inc(top_diff, 1)
                    link(v.tensor_tensor(R3, R1, R2, ALU.add))
                    dve.wait_ge(top_exp, 3)
                    link(v.tensor_reduce(W1c, t3(R4), AX, ALU.add))
                    link(v.reciprocal(W1c, W1c))
                    link(v.tensor_tensor(t3(R4), t3(R4), bt(W1c), ALU.mult))
                    link(v.tensor_tensor(G, R4, R3, ALU.mult))
                    link(v.memset(thr.bitcast(I32), 0))
                    cand3 = cand.rearrange("p (j e) -> p j e", e=E)
                    with dve.Fori(0, BITS // 2) as i:
                        def bl(n, ins):
                            ins.then_inc(cap_chain, 1)
                            dve.wait_ge(cap_chain, i * 4 + n)
                        bl(1, v.tensor_tensor(cand3.bitcast(I32), thr.bitcast(I32).unsqueeze(1).broadcast_to((P, STEP, E)),
                                              bits[:, bass.ds(i * STEP, STEP)].unsqueeze(2).broadcast_to((P, STEP, E)),
                                              ALU.bitwise_or))
                        v.tensor_tensor(cmpc[:, :].rearrange("p (j t e) -> p j t e", t=NT, e=E),
                                        t3(G).unsqueeze(1).broadcast_to((P, STEP - 1, NT, E)),
                                        cand3[:, 1:, :].unsqueeze(2).broadcast_to((P, STEP - 1, NT, E)), ALU.is_ge)\
                            .then_inc(ge_ready, 1)
                        dve.wait_ge(ge_count, i + 1)
                        bl(2, v.tensor_reduce(ccnt.rearrange("p (j e) -> p j e", e=E), bank(7)[:, 0:(STEP - 1) * P]
                                              .rearrange("p (j t e) -> p j e t", t=NT, e=E), AX, ALU.add))
                        bl(3, v.scalar_tensor_tensor(out=cand[:, E:], in0=ccnt, scalar=CAP - 0.5, in1=cand[:, E:],
                                                     op0=ALU.is_ge, op1=ALU.mult))
                        bl(4, v.tensor_reduce(thr, cand.rearrange("p (j e) -> p e j", e=E), AX, ALU.max))
                    link(v.tensor_tensor(t3(KP), t3(G), be(thr), ALU.is_gt))
                    v.tensor_copy(cmpb[:, :], KP).then_inc(tie_ready, 1)
                    dve.wait_ge(tie_count, 1)
                    link(v.tensor_reduce(cnt, bank(7)[:, 0:P].rearrange("p (t e) -> p e t", e=E), AX, ALU.add))
                    link(v.tensor_scalar(cnt, cnt, -1.0, float(CAP), ALU.mult, ALU.add))
                    link(v.tensor_tensor(t3(TI), t3(G), be(thr), ALU.is_equal))
                    link(v.tensor_tensor(TI, TI, R3, ALU.mult))
                    v.tensor_copy(cmpb[:, :], TI).then_inc(tie_ready, 1)
                    dve.wait_ge(tie_count, 2)
                    link(v.tensor_copy(R4, bank(7)[:, 0:P]))
                    v.tensor_copy(cmpb[:, :], TI).then_inc(tie_ready, 1)
                    dve.wait_ge(tie_count, 3)
                    link(v.tensor_copy(L, bank(7)[:, 0:P]))
                    before()
                    link(v.tensor_tensor(t3(L), t3(L), be(cnt), ALU.is_lt))
                    link(v.tensor_tensor(TI, TI, L, ALU.mult))
                    link(v.tensor_tensor(KP, KP, TI, ALU.add))
                    link(v.tensor_tensor(KP, KP, R3, ALU.mult))
                    for c, r in ((0, R1), (1, R2)):
                        w, kf = wts[:, c * NT:(c + 1) * NT], keptf[:, c * NT:(c + 1) * NT]
                        link(v.tensor_tensor(R4, r, KP, ALU.mult))
                        link(v.tensor_reduce(kf, t3(R4), AX, ALU.add))
                        link(v.tensor_tensor(R4, R4, G, ALU.mult))
                        link(v.tensor_reduce(w, t3(R4), AX, ALU.add))
                    slots(l)

            def before():
                a, z, d = R4, scan, E
                while d < NT * E:
                    v.tensor_copy(z[:, 0:d], a[:, 0:d])
                    link(v.tensor_tensor(z[:, d:], a[:, d:], a[:, 0:NT * E - d], ALU.add))
                    a, z, d = z, a, 2 * d
                assert a is R4
                link(v.tensor_tensor(L[:, E:], L[:, E:], R4[:, 0:(NT - 1) * E], ALU.add))

            def slots(l):
                if l == 1:
                    v.tensor_copy(cmpb[:, :], R1).then_inc(rank_ready, 1)
                elif l == 0:
                    v.tensor_tensor(cmpb[:, :], R1, R2, ALU.add).then_inc(rank_ready, 1)
                else:
                    v.tensor_copy(cmpb[:, :], KP).then_inc(rank_ready, 1)
                dve.wait_ge(rank_count, 2 * l + 1)
                v.tensor_copy(R4, bank(7)[:, 0:P]).then_inc(rank_ready, 1)
                dve.wait_ge(rank_count, 2 * l + 2)
                link(v.tensor_copy(L, bank(7)[:, 0:P]))
                before()
                if l < 2:
                    link(v.tensor_tensor(jcmp.rearrange("p (e j) -> p e j", j=8),
                                         R4[:, (NT - 1) * E:].unsqueeze(2).broadcast_to((P, E, 8)),
                                         cst[:, C_JT:C_JT + 8].unsqueeze(1).broadcast_to((P, E, 8)), ALU.is_gt))
                    link(v.tensor_reduce(nblk, jcmp.rearrange("p (e j) -> p e j", j=8), AX, ALU.add))
                    link(v.tensor_copy(eblk, nblk))
                    for e in range(1, E):
                        link(v.tensor_tensor(eblk[:, e:e + 1], eblk[:, e:e + 1], eblk[:, e - 1:e], ALU.add))
                    link(v.tensor_tensor(ebase, eblk, nblk, ALU.subtract))
                    link(v.tensor_scalar(ebase, ebase, float(SB), None, ALU.mult))
                    k3 = kcmp.rearrange("p (k e) -> p k e", e=E)
                    link(v.tensor_tensor(k3, eblk.unsqueeze(1).broadcast_to((P, NTAB, E)),
                                         cst[:, C_KT:C_KT + NTAB].unsqueeze(2).broadcast_to((P, NTAB, E)), ALU.is_le))
                    link(v.tensor_reduce(tabf[:, 0:NTAB], k3, AX, ALU.add))
                    link(v.tensor_scalar(tabf[:, 0:NTAB], tabf[:, 0:NTAB], float(E - 1), None, ALU.min))
                    if l:
                        dve.wait_ge(M[0]["yfree"], BL[0].total + 2)
                    link(v.tensor_copy(btab[:, :], tabf[:, 0:NTAB]))
                    link(v.tensor_tensor(t3(L), t3(L), be(ebase), ALU.add))
                else:
                    link(v.tensor_scalar(L, L, CAP - 1.0, None, ALU.min))
                    link(v.tensor_tensor(t3(L), t3(L), be(cst[:, C_EB:C_EB + E]), ALU.add))
                for c, r in ((0, R1), (1, R2))[:MOE[l]["top"]]:
                    link(v.tensor_tensor(r, r, L, ALU.mult))
                    link(v.tensor_reduce(slotf[:, c * NT:(c + 1) * NT], t3(r), AX, ALU.add))
                n = MOE[l]["top"] * NT
                link(v.tensor_copy(get_i[:, 0:n], slotf[:, 0:n]))
                if l == 2:
                    tr = cst[:, C_TR:C_TR + 2 * NT]
                    link(v.tensor_tensor(slotf, slotf, tr, ALU.subtract))
                    link(v.tensor_tensor(slotf, slotf, keptf, ALU.mult))
                    link(v.tensor_tensor(slotf, slotf, tr, ALU.add))
                v.tensor_copy(put_i[:, 0:n], slotf[:, 0:n]).then_inc(M[l]["slots"], 1)

            def shared_dve(l, acc):
                m, sh = M[l], MOE[l]["sh"]

                def add(n):
                    dve.wait_ge(m["down"], (n + 1) * sh)
                    a = acc[:, :, n * BLK:(n + 1) * BLK]
                    y = ps[:, 4 * BLK:6 * BLK].rearrange("p (k t) -> p k t", k=KT)
                    if l == 0:
                        v.tensor_copy(a, y).then_inc(m["yacc"], 1)
                    else:
                        v.tensor_tensor(a, a, y, ALU.add).then_inc(m["yacc"], 1)
                s = 0
                for n in range(shared_before(l)):
                    for mi in range(sh):
                        multiply(l, s, 0, BLK)
                        if mi == 0 and n:
                            add(n - 1)
                        s += 1
                add(shared_before(l) - 1)

            def multiply(l, s, s0, n):
                m = M[l]
                dve.wait_ge(m["act"], s0 + s + 1)
                if s >= 2:
                    dve.wait_ge(m["down"], s0 + s - 1)
                g = gs[s % 2][:, 0:n]
                if l == 0:
                    v.scalar_tensor_tensor(out=g, in0=g, scalar=0.01, in1=g, op0=ALU.mult, op1=ALU.max)\
                        .then_inc(m["leaky"], 1)
                    dve.wait_ge(m["leaky"], s0 + s + 1)
                v.tensor_tensor(hb[s % 2][:, 0:n], g, bank(2 + s % 2, n), ALU.mult).then_inc(m["h"], 1)

            def blocks_dve(l):
                m, bl, mt, pair = M[l], BL[l], MOE[l]["mt"], MOE[l]["pair"]

                def turn(it, n0, s0, nblk):
                    def take_in(k):
                        n = bl.blocks[k]["nt"] * P
                        dve.wait_ge(m["bt"], n0 + k + 1)
                        if k >= 2:
                            dve.wait_ge(m["gu"], s0 + (k - 1) * mt)
                        v.tensor_copy(xb[k % 2][:, :, 0:n], ps[:, 6 * BLK:8 * BLK]
                                      .rearrange("p (k t) -> p k t", k=KT)[:, :, 0:n]).then_inc(m["xb"], 1)

                    def give_out(k):
                        dve.wait_ge(m["down"], s0 + (k + 1) * mt)
                        o = k % 2
                        dve.wait_ge(m["yfree"], n0 + k + 1)
                        if bl.blocks[k]["nt"] == 3:
                            v.tensor_copy(yrow[o][:, 2, :], bank(2, D))
                        v.tensor_copy(yrow[o][:, 0:2, :], ps[:, 4 * BLK:6 * BLK]
                                      .rearrange("p (t d) -> p t d", t=2)[:, :, 0:D]).then_inc(m["yrow"], 1)

                    take_in(0)
                    s = 0
                    for k in range(nblk):
                        for mi in range(mt):
                            if mi == 0 and k + 1 < nblk:
                                take_in(k + 1)
                            if pair:
                                multiply(l, s, s0, bl.blocks[k]["nt"] * P)
                            if mi == 0 and k:
                                give_out(k - 1)
                            s += 1
                    give_out(nblk - 1)
                base = shared_before(l) * MOE[l]["sh"]
                with dve.Fori(0, bl.turns) as it:
                    turn(it, it * bl.n, it * (bl.n * mt) + base, bl.n)
                if bl.rest:
                    turn(bl.turns, bl.turns * bl.n, bl.turns * bl.n * mt + base, bl.rest)

            def mix_dve(l, acc):
                m, top = M[l], MOE[l]["top"]

                def add(b):
                    dve.wait_ge(m["mixt"], (b + 1) * TPB)
                    a = acc[:, :, b * BLK:(b + 1) * BLK]
                    v.tensor_tensor(a, a, ps[:, mix_bank(l, b) * BLK:(mix_bank(l, b) + 2) * BLK]
                                    .rearrange("p (k t) -> p k t", k=KT), ALU.add).then_inc(m["acc"], 1)
                for t in range(NT):
                    if l == 1 and t % TPB == 0:
                        multiply(l, t // TPB, LAST1, BLK)
                    g = got[t % RING]
                    dve.wait_ge(got_in[t % RING], GOT[l] + 16 * top * (t // RING + 1))
                    if top == 1:
                        dve.sem_inc(m["mixed"], 1)
                    else:
                        link(v.tensor_scalar(g[0], g[0], wts[:, t:t + 1], None, ALU.mult))
                        v.scalar_tensor_tensor(out=g[0], in0=g[1], scalar=wts[:, NT + t:NT + t + 1], in1=g[0],
                                               op0=ALU.mult, op1=ALU.add).then_inc(m["mixed"], 1)
                    if t % TPB == (1 if l == 2 else 0) and t >= TPB:
                        add(t // TPB - 1)
                    if l == 0 and t and t % 2 == 0:
                        relpos_dve(t // 2 - 1)
                if l == 1:
                    dve.wait_ge(m["down"], LAST1 + MOE[1]["sh"])
                    a = acc[:, :, (NB - 1) * BLK:]
                    v.tensor_tensor(a, a, ps[:, 4 * BLK:6 * BLK].rearrange("p (k t) -> p k t", k=KT), ALU.add)\
                        .then_inc(m["yacc"], 1)
                    dve.wait_ge(m["yacc"], NB)
                add(NB - 1)
                if l == 0:
                    relpos_dve(NT // 2 - 1)
                dve.wait_ge(m["acc"], NB)

            route(0)
            shared_dve(0, yT)
            blocks_dve(0)
            dve.wait_ge(relw_in, 16 * 3)
            dve.wait_ge(M[0]["yfree"], BL[0].total + 2)
            relpos_dve(-1)
            v.memset(lrow[:, 0:P - 1], NEG).then_inc(rows_done, 1)
            mix_dve(0, yT)
            v.tensor_tensor(kn1, pr("nk"), pr("nk"), ALU.mult).then_inc(nk_sq, 1)
            link(v.tensor_scalar(qs8, pr("qs"), 8.0, None, ALU.mult))
            link(v.tensor_copy(maskf, mask8[:, :]))
            dve.wait_ge(nk_std, 1)
            link(v.tensor_scalar(kn2, kn2, 1e-12, None, ALU.max))
            link(v.reciprocal(kn2, kn2))
            link(v.tensor_tensor(kn2, kn2, pr("nk"), ALU.mult))
            link(v.tensor_tensor(kn2, kn2, pr("ks"), ALU.mult))
            v.tensor_scalar(knull, sel2, kn2, None, ALU.mult).then_inc(nk_done, 1)
            link(v.memset(vsel, 0.0))
            v.tensor_scalar(vsel[:, HEADS - 2:HEADS], sel2, pr("nv"), None, ALU.mult).then_inc(nk_done, 1)

            route(1)
            shared_dve(1, xT)
            blocks_dve(1)
            mix_dve(1, xT)
            for _ in range(NB):
                dve.sem_inc(ln_src, 1)
            ln_dve(LN_QKV, xT[:, :, 0:BLK], lnb[0], "gn")

            dve.wait_ge(qkv_w_in, 48)
            v.tensor_copy(bsel_r, bsel)
            link(v.tensor_scalar(rnT, bsel[:, 0:BLK], 0.0, None, ALU.mult))

            def norm_rows(b):
                dve.wait_ge(q_tr, b + 1)
                if b:
                    dve.wait_ge(q_rb, b * 9)
                link(v.tensor_copy(rnT[0:18, :], bank(0)[0:18, :]))
                v.tensor_tensor(rnT[32:50, :], bank(0)[0:18, :], rnT[0:18, :].bitcast(F32), ALU.subtract).then_inc(q_rnT, 1)

            def normalise(b, c):
                n = b * 9 + c
                if c == 0:
                    norm_rows(b)
                dve.wait_ge(q_rb, n + 1)
                if c < NCH:
                    dst = qout[c % 2]
                    w = b * (NCH // 2) + c // 2
                    if w:
                        dve.wait_ge(q_out[c % 2], 32 * w)
                else:
                    dst = kall[:, (b ^ 1) * BLK:((b ^ 1) + 1) * BLK]
                v.scalar_tensor_tensor(out=dst, in0=qraw[n % len(qraw)], scalar=(qs8 if c < NCH else pr("ks")),
                                       in1=bank(6 + n % 2), op0=ALU.mult, op1=ALU.mult).then_inc(q_norm, 1)
            for b in range(NB):
                nxt = LN_QKV + b + 1
                for c in range(9):
                    if b:
                        normalise(b - 1, c)
                    if b + 1 < NB:
                        if c == 1:
                            center_dve(nxt, xT[:, :, (b + 1) * BLK:(b + 2) * BLK])
                        elif c == 4:
                            rstd_dve(nxt)
                        elif c == 6:
                            if b:
                                dve.wait_ge(v_mm, b)
                            scale_dve(nxt, lnb[(b + 1) % 2], "gn")
                dve.wait_ge(q_std, b + 1)
                link(v.tensor_scalar(n2s, n2s, 1e-12, None, ALU.max))
                v.reciprocal(rns, n2s).then_inc(q_rn, 1)
                dve.wait_ge(v_mm, b + 1)
                for t in range(TPB):
                    tt = (b ^ 1) * TPB + t
                    o = vall[:, tt * (DH + 1):(tt + 1) * (DH + 1)]
                    v.tensor_scalar(o[:, 0:DH], bank(1)[:, t * DH:(t + 1) * DH], maskf[:, tt:tt + 1], None, ALU.mult)
                    last = v.tensor_copy(o[:, DH:DH + 1], maskf[:, tt:tt + 1])
                last.then_inc(v_done, 1)
            for c in range(9):
                normalise(NB - 1, c)
            dve.wait_ge(v_done, NB)
            dve.wait_ge(q_norm, NB * 9)
            with dve.Fori(0, BATCH) as b:
                ub = b * UNITS
                at_c = [0]

                def tick(ins):
                    at_c[0] += 1
                    ins.then_inc(att_chain, 1)

                def adds(u):
                    qt, hg = divmod(u, NHG)
                    nk = (qt + 1) * P
                    o4 = (u % 2) * 4
                    sn = sn2[:, o4:o4 + 4]
                    dve.wait_ge(null_mm, ub + u + 1)
                    dve.wait_ge(sim_done, (ub + u) * HG + 1)
                    tick(v.tensor_tensor(sn, bank(7)[:, 0:HG], pr("nab")[:, hg * HG:(hg + 1) * HG], ALU.add))
                    for h in range(HG):
                        off = (hg * HG + h) * SEQ
                        tick(v.tensor_tensor_reduce(out=prob[h][:, 0:nk], in0=ps[:, (h % 2) * 2 * BLK:(h % 2) * 2 * BLK + nk],
                                                    in1=TA[:, off:off + nk], scale=1.0, scalar=-3.0e38,
                                                    op0=ALU.add, op1=ALU.max, accum_out=mx[:, o4 + h:o4 + h + 1]))
                        dve.wait_ge(att_chain, b * ATT_LINKS + at_c[0])
                        if h + 1 < HG:
                            dve.wait_ge(sim_done, (ub + u) * HG + h + 2)
                        v.tensor_scalar(negm[:, o4 + h:o4 + h + 1], mx[:, o4 + h:o4 + h + 1], sn[:, h:h + 1], -1.0,
                                        ALU.max, ALU.mult).then_inc(added, 1)
                    dve.wait_ge(added, (ub + u + 1) * HG)
                    if u:
                        dve.wait_ge(pn_done, ub + u)
                    v.tensor_tensor(dn, sn, negm[:, o4:o4 + 4], ALU.add).then_inc(dn_done, 1)

                keys = kall[:, bass.ds(b * SEQ, SEQ)]
                tick(v.tensor_copy(kcur[0][:, :], keys))
                dve.wait_ge(att_chain, b * ATT_LINKS + 1)
                v.tensor_tensor(kcur[1][:, :], keys, kcur[0][:, :].bitcast(F32), ALU.subtract)
                v.tensor_copy(vcur[:, :], vall[:, bass.ds(b * (NQ * (DH + 1)), NQ * (DH + 1))]).then_inc(kv_cur, 1)
                adds(0)
                for u in range(UNITS):
                    qt, hg = divmod(u, NHG)
                    for h in range(HG):
                        for g, (k0, k1) in enumerate(groups(qt)):
                            if ev_engine(u, h, g) != 1:
                                continue
                            dve.wait_ge(tr_done, b * TR_B + tr_index(u, h, g) + 1)
                            v.tensor_copy(probT[:, k0:k1, h, :], bank(tr_bank(u, h, g))[:, 0:(k1 - k0) * P]
                                          .rearrange("p (k q) -> p k q", q=P)).then_inc(evac[1], 1)
                    if u + 1 < UNITS:
                        adds(u + 1)
                    dve.wait_ge(av_done, ub + u + 1)
                    if u >= 2:
                        dve.wait_ge(o_out[u % 2], b * (UNITS * 16) + (u // 2) * 32)
                    elif u == 0:
                        dve.wait_ge(batch_stored, b + 1)
                    src = bank(6).rearrange("p (c a q) -> p c a q", c=2, a=2)
                    for a in range(2):
                        v.tensor_copy(obuf[u % 2][a * 64:a * 64 + 64, :, :], src[0:DH, :, a, :])
                    v.tensor_copy(dbuf[u % 2][DH:DH + 1, :], bank(6)[DH:DH + 1, :]).then_inc(o_copied, 1)
                assert at_c[0] == ATT_LINKS
            dve.wait_ge(den_in, 32)
            link(v.tensor_tensor(dcmp, dcmp, pcmp, ALU.add))
            link(v.reciprocal(rcmp, dcmp))
            v.tensor_tensor(pcmp, pcmp, rcmp, ALU.mult).then_inc(rden_done, 1)
            def weigh(b):
                dve.wait_ge(ab_in[b % 2], 16 * (b // 2 + 1))
                dve.wait_ge(scale_in, 64 * (b + 1))
                for j in range(2):
                    a = ablk[b % 2][:, 4 * j:4 * j + 4, :]
                    last = v.tensor_tensor(a, a, rden[j], ALU.mult)
                last.then_inc(ab_scaled, 1)
            weigh(0)
            weigh(1)
            for b in range(NB):
                center_dve(LN_PROJ + b, lsrc)
                rstd_dve(LN_PROJ + b)
                scale_dve(LN_PROJ + b, aT[:, :, b * BLK:(b + 1) * BLK], "go")
                if b + 2 < NB:
                    weigh(b + 2)
            route(2)
            blocks_dve(2)
            mix_dve(2, xT)


_OUT = ("out_dram", (P, KT, TOK))


def kernel(**inp):
    import numpy as _np
    import concourse.bacc as _bacc
    from concourse import mybir as _mybir
    from concourse.bass_utils import run_bass_kernel_spmd as _run
    c = _np.ascontiguousarray
    g = {k: _np.asarray(a) for k, a in inp.items()}

    def feat(a):
        return a.reshape(KT, P, -1).transpose(1, 0, 2)

    def flat(a):
        return a.reshape(P, -1)

    def expert(gate, up, down):
        parts = [flat(feat(gate))] + ([flat(feat(up))] if up is not None else [])
        parts.append(flat(down.reshape(-1, P, D).transpose(1, 0, 2)))
        return _np.concatenate(parts, axis=1)

    def col(a):
        return a.reshape(KT, P).T

    def rep(a):
        return _np.broadcast_to(a.reshape(1, -1), (P, a.size))

    def dup(a):
        return _np.concatenate([a, a]).reshape(P, 1)

    arr = {}
    arr["xT"] = c(feat(g["x"].reshape(TOK, D).T))
    cst = _np.zeros((P, C_END), _np.float32)
    cst[:, C_ID:C_ID + P] = _np.eye(P)
    cst[:, C_MEAN:C_MEAN + P] = 1.0 / D
    cst[:64, C_B64:C_B64 + 64] = 1.0
    cst[64:, C_B64 + 64:C_B64 + P] = 1.0
    cst[:, C_TRI:C_TRI + P] = _np.triu(_np.ones((P, P)), 1)
    cst[:64, C_SEL] = 1.0
    cst[64:, C_SEL + 1] = 1.0
    cst[:, C_WD:C_WD + E] = E - _np.arange(E)
    cst[:, C_EPS] = 1e-5
    cst[:, C_JT:C_JT + 8] = SB * _np.arange(8)
    cst[:, C_KT:C_KT + NTAB] = _np.arange(NTAB)
    cst[:, C_EB:C_EB + E] = CAP * _np.arange(E)
    cst[:, C_TR:C_TR + 2 * NT] = (E * CAP + P * _np.arange(2 * NT))[None, :] + _np.arange(P)[:, None]
    arr["cst"] = cst
    b2 = _np.zeros((P, 1), _np.float32)
    b2[:HEADS, 0] = g["L1_cond_b2"]
    cond = g["cond_64"]
    pieces = dict(w0=col(g["L1_cond_w0"][0]), b0=col(g["L1_cond_b0"]), g0=col(g["L1_cond_g0"]),
                  b1=col(g["L1_cond_b1"]), g1=col(g["L1_cond_g1"]), gn=col(g["L1_cond_g_norm"]),
                  go=col(g["L1_cond_g_out"]), qs=dup(g["L1_cond_q_scale"]), ks=dup(g["L1_cond_k_scale"]),
                  nk=dup(cond[0]), nab=rep(g["L1_cond_null_attn_bias"]), nv=dup(cond[1]), b2=b2)
    arr["par"] = c(_np.concatenate([pieces[n] for n in PAR], axis=1))
    arr["wrt"] = c(_np.concatenate([flat(feat(g["L0_cond_wt"].T)), flat(feat(g["L0_ffn_router_w"].T)),
                                    flat(feat(g["L1_ffn_Wr"]))], axis=1))
    arr["xrows"] = c(g["x"].reshape(NT, P, D).transpose(1, 0, 2))
    arr["wg"] = c(g["L0_cond_wg"].T)
    arr["condT"] = c(cond.T)
    arr["mask"] = c(g["mask_BxS_bf1"][:, ::-1].reshape(NT, P).T).view(_np.uint8)
    two = _np.arange(STEP)[None, :] << _np.arange(BITS - 2, -1, -2)[:, None]
    arr["bits"] = c(_np.broadcast_to(two.reshape(-1).astype(_np.int32), (P, two.size)))
    arr["posr"] = c(_np.broadcast_to(_np.arange(SEQ).astype(_np.float32), (P, SEQ)))
    arr["w1"] = c(flat(feat(g["L1_cond_w1"])))
    arr["w2"] = c(flat(feat(g["L1_cond_w2"])))
    arr["wexp0"] = c(_np.stack([expert(g["L0_cond_w_gate"][e], g["L0_cond_w_up"][e], g["L0_cond_w_down"][e]) for e in range(E)]))
    arr["wsh0"] = c(expert(g["L0_cond_sw_gate"], g["L0_cond_sw_up"], g["L0_cond_sw_down"]))
    arr["wexp1"] = c(_np.stack([expert(g["L0_ffn_expert_gate"][e], g["L0_ffn_expert_up"][e], g["L0_ffn_expert_down"][e]) for e in range(E)]))
    arr["wsh1"] = c(expert(g["L0_ffn_shared_gate"], g["L0_ffn_shared_up"], g["L0_ffn_shared_down"]))
    arr["wexp2"] = c(_np.stack([expert(g["L1_ffn_W1"][e], None, g["L1_ffn_W2"][e]) for e in range(E)]))
    wkv = g["L1_cond_Wkv"]
    arr["wqk"] = c(feat(_np.concatenate([g["L1_cond_Wq"], wkv[:, :DH], wkv[:, :DH]], axis=1)))
    arr["wv"] = c(feat(wkv[:, DH:]))
    bsel = _np.zeros((32 + 18, 9 * P), _np.float32)
    for c_ in range(9):
        for r_ in (0, 32):
            bsel[r_ + 2 * c_, c_ * P:c_ * P + 64] = 1.0
            bsel[r_ + 2 * c_ + 1, c_ * P + 64:(c_ + 1) * P] = 1.0
    arr["bsel"] = bsel
    arr["wout"] = c(g["L1_cond_Wout"].reshape(NCH, P, D).transpose(1, 0, 2))

    nc = _bacc.Bacc("TRN2", target_bir_lowering=False, num_devices=1)
    A = {n: nc.dram_tensor(f"{n}_dram", a.shape, _mybir.dt.from_np(a.dtype), kind="ExternalInput").ap()
         for n, a in arr.items()}
    A["out"] = nc.dram_tensor(_OUT[0], _OUT[1], _mybir.dt.float32, kind="ExternalOutput").ap()
    build(nc, A)
    r = _run(nc, [{f"{n}_dram": a for n, a in arr.items()}], core_ids=[0])
    o = r.results[0][_OUT[0]]
    return o.transpose(2, 1, 0).reshape(BATCH, SEQ, D)
```
